# Optimizing a Trainium2 kernel written in Bass

```python
import numpy as np
import jax
import jax.numpy as jnp

def _softmax(x, axis=-1):
    return jax.nn.softmax(x, axis=axis)

def _gelu(x):
    return jax.nn.gelu(x, approximate=True)

def _silu(x):
    return jax.nn.silu(x)

def _sigmoid(x):
    return jax.nn.sigmoid(x)

def _layernorm(x, axis=-1, eps=1e-05):
    m = jnp.mean(x, axis=axis, keepdims=True)
    v = jnp.var(x, axis=axis, keepdims=True)
    return (x - m) / jnp.sqrt(v + eps)

def _scatter_add(tgt, idx, src, axis=0):
    return tgt.at[idx].add(src)

def _segment_sum(src, seg, n):
    return jax.ops.segment_sum(src, seg, n)
kernel_name = 'mk_conv_preact_d4_conv_nchw48_r2_64373b'

def setup_inputs(seed: int=0):
    np.random.seed(seed)
    _w = jnp.asarray

    def _rec_inputs():
        import jax
        import jax.numpy as jnp
        _gk = jax.random.key(seed)
        x = -0.0004039 + 1 * jax.random.normal(jax.random.fold_in(_gk, 1), (4, 48, 128, 128), jnp.float32)
        return x
    x = _rec_inputs()

    def _L0_conv_setup():
        import jax, jax.numpy as jnp
        import numpy as np
        from jax import lax
        NUM_HEADS = 1
        DN = ('NCHW', 'OIHW', 'NCHW')
        EPS = 1e-12

        def _l2_normalize(t):
            n = jnp.sqrt(jnp.sum(t * t, axis=-1, keepdims=True))
            return t / jnp.maximum(n, EPS)
        key = jax.random.key(seed)
        k0, k1, k2, k3 = jax.random.split(key, 4)
        b, c, h, w = (4, 48, 128, 128)
        x = jax.random.normal(k0, (b, c, h, w), dtype=jnp.float32)
        qkv_w = jax.random.normal(k1, (3 * c, c, 1, 1), dtype=jnp.float32) * 0.05
        dw_w = jax.random.normal(k2, (3 * c, 1, 3, 3), dtype=jnp.float32) * 0.05
        proj_w = jax.random.normal(k3, (c, c, 1, 1), dtype=jnp.float32) * 0.05
        temperature = jnp.ones((NUM_HEADS, 1, 1), dtype=jnp.float32)
        return {'x': x, 'qkv_w': qkv_w, 'dw_w': dw_w, 'proj_w': proj_w, 'temperature': temperature}
    _L0_conv_all = _L0_conv_setup()
    _L0_conv_in = {k: v for k, v in _L0_conv_all.items() if k in ('qkv_w', 'dw_w', 'proj_w', 'temperature')}
    del _L0_conv_all

    def _L1_conv_setup():
        import jax, jax.numpy as jnp
        import numpy as np
        B, C, H, W = (32, 48, 32, 64)
        K = 5

        def _conv1d(x, w, b):
            y = jax.lax.conv_general_dilated(x, w, window_strides=(1,), padding=[(2, 2)], dimension_numbers=('NCH', 'OIH', 'NCH'))
            return y + b[None, :, None]
        key = jax.random.key(seed)
        ks = jax.random.split(key, 7)
        s = 0.02
        return {'x': jax.random.normal(ks[0], (B, C, H, W), dtype=jnp.float32), 'down_w': jax.random.normal(ks[1], (C, C, K), dtype=jnp.float32) * s, 'down_b': jax.random.normal(ks[2], (C,), dtype=jnp.float32) * s, 'right_w': jax.random.normal(ks[3], (C, C, K), dtype=jnp.float32) * s, 'right_b': jax.random.normal(ks[4], (C,), dtype=jnp.float32) * s, 'left_w': jax.random.normal(ks[5], (C, C, K), dtype=jnp.float32) * s, 'left_b': jax.random.normal(ks[6], (C,), dtype=jnp.float32) * s}
    _L1_conv_all = _L1_conv_setup()
    _L1_conv_in = {k: v for k, v in _L1_conv_all.items() if k in ('down_w', 'down_b', 'right_w', 'right_b', 'left_w', 'left_b')}
    del _L1_conv_all

    def _L2_conv_setup():
        import jax, jax.numpy as jnp
        import numpy as np
        B, C, H, W = (32, 48, 32, 64)
        K = 5

        def _conv1d(x, w, b):
            y = jax.lax.conv_general_dilated(x, w, window_strides=(1,), padding=[(2, 2)], dimension_numbers=('NCH', 'OIH', 'NCH'))
            return y + b[None, :, None]
        key = jax.random.key(seed)
        ks = jax.random.split(key, 7)
        s = 0.02
        return {'x': jax.random.normal(ks[0], (B, C, H, W), dtype=jnp.float32), 'down_w': jax.random.normal(ks[1], (C, C, K), dtype=jnp.float32) * s, 'down_b': jax.random.normal(ks[2], (C,), dtype=jnp.float32) * s, 'right_w': jax.random.normal(ks[3], (C, C, K), dtype=jnp.float32) * s, 'right_b': jax.random.normal(ks[4], (C,), dtype=jnp.float32) * s, 'left_w': jax.random.normal(ks[5], (C, C, K), dtype=jnp.float32) * s, 'left_b': jax.random.normal(ks[6], (C,), dtype=jnp.float32) * s}
    _L2_conv_all = _L2_conv_setup()
    _L2_conv_in = {k: v for k, v in _L2_conv_all.items() if k in ('down_w', 'down_b', 'right_w', 'right_b', 'left_w', 'left_b')}
    del _L2_conv_all

    def _L3_conv_setup():
        import jax, jax.numpy as jnp
        import numpy as np
        LN_EPS = 1e-05
        DN = ('NCHW', 'OIHW', 'NCHW')

        def _layernorm(x, gamma, beta):
            m = x.mean(-1, keepdims=True)
            v = ((x - m) ** 2).mean(-1, keepdims=True)
            return (x - m) / jnp.sqrt(v + LN_EPS) * gamma + beta
        key = jax.random.key(seed)
        ks = jax.random.split(key, 6)
        dim, hid, B, H, W = (48, 16, 16, 128, 128)
        C = hid // 2
        x = jax.random.normal(ks[0], (B, dim, H, W), jnp.float32)
        W1 = jax.random.normal(ks[1], (dim, hid), jnp.float32) * 0.05
        b1 = jnp.zeros((hid,), jnp.float32)
        gamma = jnp.ones((C,), jnp.float32)
        beta = jnp.zeros((C,), jnp.float32)
        dw_w = jax.random.normal(ks[2], (C, 1, 3, 3), jnp.float32) * 0.1
        dw_b = jnp.zeros((C,), jnp.float32)
        pw_w = jax.random.normal(ks[3], (C, C, 1, 1), jnp.float32) * 0.1
        pw_b = jnp.zeros((C,), jnp.float32)
        W2 = jax.random.normal(ks[4], (C, dim), jnp.float32) * 0.1
        b2 = jnp.zeros((dim,), jnp.float32)
        return {'x': x, 'W1': W1, 'b1': b1, 'gamma': gamma, 'beta': beta, 'dw_w': dw_w, 'dw_b': dw_b, 'pw_w': pw_w, 'pw_b': pw_b, 'W2': W2, 'b2': b2}
    _L3_conv_all = _L3_conv_setup()
    _L3_conv_in = {k: v for k, v in _L3_conv_all.items() if k in ('W1', 'b1', 'gamma', 'beta', 'dw_w', 'dw_b', 'pw_w', 'pw_b', 'W2', 'b2')}
    del _L3_conv_all
    return {'x': x, 'L0_conv_qkv_w': _L0_conv_in['qkv_w'], 'L0_conv_dw_w': _L0_conv_in['dw_w'], 'L0_conv_proj_w': _L0_conv_in['proj_w'], 'L0_conv_temperature': _L0_conv_in['temperature'], 'L1_conv_down_w': _L1_conv_in['down_w'], 'L1_conv_down_b': _L1_conv_in['down_b'], 'L1_conv_right_w': _L1_conv_in['right_w'], 'L1_conv_right_b': _L1_conv_in['right_b'], 'L1_conv_left_w': _L1_conv_in['left_w'], 'L1_conv_left_b': _L1_conv_in['left_b'], 'L2_conv_down_w': _L2_conv_in['down_w'], 'L2_conv_down_b': _L2_conv_in['down_b'], 'L2_conv_right_w': _L2_conv_in['right_w'], 'L2_conv_right_b': _L2_conv_in['right_b'], 'L2_conv_left_w': _L2_conv_in['left_w'], 'L2_conv_left_b': _L2_conv_in['left_b'], 'L3_conv_W1': _L3_conv_in['W1'], 'L3_conv_b1': _L3_conv_in['b1'], 'L3_conv_gamma': _L3_conv_in['gamma'], 'L3_conv_beta': _L3_conv_in['beta'], 'L3_conv_dw_w': _L3_conv_in['dw_w'], 'L3_conv_dw_b': _L3_conv_in['dw_b'], 'L3_conv_pw_w': _L3_conv_in['pw_w'], 'L3_conv_pw_b': _L3_conv_in['pw_b'], 'L3_conv_W2': _L3_conv_in['W2'], 'L3_conv_b2': _L3_conv_in['b2']}

def reference(x, L0_conv_qkv_w, L0_conv_dw_w, L0_conv_proj_w, L0_conv_temperature, L1_conv_down_w, L1_conv_down_b, L1_conv_right_w, L1_conv_right_b, L1_conv_left_w, L1_conv_left_b, L2_conv_down_w, L2_conv_down_b, L2_conv_right_w, L2_conv_right_b, L2_conv_left_w, L2_conv_left_b, L3_conv_W1, L3_conv_b1, L3_conv_gamma, L3_conv_beta, L3_conv_dw_w, L3_conv_dw_b, L3_conv_pw_w, L3_conv_pw_b, L3_conv_W2, L3_conv_b2):
    import jax
    import jax.numpy as jnp

    def _L0_conv_ref(x, qkv_w, dw_w, proj_w, temperature):
        import jax, jax.numpy as jnp
        import numpy as np
        from jax import lax
        NUM_HEADS = 1
        DN = ('NCHW', 'OIHW', 'NCHW')
        EPS = 1e-12

        def _l2_normalize(t):
            n = jnp.sqrt(jnp.sum(t * t, axis=-1, keepdims=True))
            return t / jnp.maximum(n, EPS)
        b, c, h, w = x.shape
        heads = NUM_HEADS
        qkv = lax.conv_general_dilated(x, qkv_w, (1, 1), 'VALID', dimension_numbers=DN)
        qkv = lax.conv_general_dilated(qkv, dw_w, (1, 1), ((1, 1), (1, 1)), feature_group_count=3 * c, dimension_numbers=DN)
        q, k, v = jnp.split(qkv, 3, axis=1)
        q = q.reshape(b, heads, c // heads, h * w)
        k = k.reshape(b, heads, c // heads, h * w)
        v = v.reshape(b, heads, c // heads, h * w)
        q = _l2_normalize(q)
        k = _l2_normalize(k)
        attn = jax.nn.softmax(jnp.einsum('bhcn,bhdn->bhcd', q, k) * temperature, axis=-1)
        out = jnp.einsum('bhcd,bhdn->bhcn', attn, v).reshape(b, c, h, w)
        return lax.conv_general_dilated(out, proj_w, (1, 1), 'VALID', dimension_numbers=DN)

    def _L1_conv_ref(x, down_w, down_b, right_w, right_b, left_w, left_b):
        import jax, jax.numpy as jnp
        import numpy as np
        B, C, H, W = (32, 48, 32, 64)
        K = 5

        def _conv1d(x, w, b):
            y = jax.lax.conv_general_dilated(x, w, window_strides=(1,), padding=[(2, 2)], dimension_numbers=('NCH', 'OIH', 'NCH'))
            return y + b[None, :, None]
        Bb, Cc, Hh, Ww = x.shape

        def step(w, b):

            def f(carry, inp):
                nxt = inp + _conv1d(carry, w, b)
                return (nxt, nxt)
            return f
        xs = jnp.moveaxis(x, 2, 0)
        d0 = xs[0]
        _, d_rest = jax.lax.scan(step(down_w, down_b), d0, xs[1:])
        D = jnp.concatenate([d0[None], d_rest], 0)
        seq = jnp.concatenate([D[Hh - 3::-1], D[Hh - 1:Hh]], 0)
        u0 = D[Hh - 1]
        _, u_rest = jax.lax.scan(step(down_w, down_b), u0, seq)
        U = jnp.concatenate([u0[None], u_rest], 0)[::-1]
        ws = jnp.moveaxis(jnp.moveaxis(U, 0, 2), 3, 0)
        r0 = ws[0]
        _, r_rest = jax.lax.scan(step(right_w, right_b), r0, ws[1:])
        R = jnp.concatenate([r0[None], r_rest], 0)
        l0 = R[Ww - 1]
        _, l_rest = jax.lax.scan(step(left_w, left_b), l0, R[Ww - 2::-1])
        L = jnp.concatenate([l0[None], l_rest], 0)[::-1]
        return jnp.moveaxis(L, 0, 3)

    def _L2_conv_ref(x, down_w, down_b, right_w, right_b, left_w, left_b):
        import jax, jax.numpy as jnp
        import numpy as np
        B, C, H, W = (32, 48, 32, 64)
        K = 5

        def _conv1d(x, w, b):
            y = jax.lax.conv_general_dilated(x, w, window_strides=(1,), padding=[(2, 2)], dimension_numbers=('NCH', 'OIH', 'NCH'))
            return y + b[None, :, None]
        Bb, Cc, Hh, Ww = x.shape

        def step(w, b):

            def f(carry, inp):
                nxt = inp + _conv1d(carry, w, b)
                return (nxt, nxt)
            return f
        xs = jnp.moveaxis(x, 2, 0)
        d0 = xs[0]
        _, d_rest = jax.lax.scan(step(down_w, down_b), d0, xs[1:])
        D = jnp.concatenate([d0[None], d_rest], 0)
        seq = jnp.concatenate([D[Hh - 3::-1], D[Hh - 1:Hh]], 0)
        u0 = D[Hh - 1]
        _, u_rest = jax.lax.scan(step(down_w, down_b), u0, seq)
        U = jnp.concatenate([u0[None], u_rest], 0)[::-1]
        ws = jnp.moveaxis(jnp.moveaxis(U, 0, 2), 3, 0)
        r0 = ws[0]
        _, r_rest = jax.lax.scan(step(right_w, right_b), r0, ws[1:])
        R = jnp.concatenate([r0[None], r_rest], 0)
        l0 = R[Ww - 1]
        _, l_rest = jax.lax.scan(step(left_w, left_b), l0, R[Ww - 2::-1])
        L = jnp.concatenate([l0[None], l_rest], 0)[::-1]
        return jnp.moveaxis(L, 0, 3)

    def _L3_conv_ref(x, W1, b1, gamma, beta, dw_w, dw_b, pw_w, pw_b, W2, b2):
        import jax, jax.numpy as jnp
        import numpy as np
        LN_EPS = 1e-05
        DN = ('NCHW', 'OIHW', 'NCHW')

        def _layernorm(x, gamma, beta):
            m = x.mean(-1, keepdims=True)
            v = ((x - m) ** 2).mean(-1, keepdims=True)
            return (x - m) / jnp.sqrt(v + LN_EPS) * gamma + beta
        B, dim, H, W = x.shape
        t = x.reshape(B, H * W, dim)
        t = jax.nn.gelu(t @ W1 + b1, approximate=False)
        t = jax.nn.gelu(t, approximate=False)
        C = t.shape[-1] // 2
        x1, x2 = (t[..., :C], t[..., C:])
        n = _layernorm(x2, gamma, beta)
        nc = n.transpose(0, 2, 1).reshape(B, C, H, W)
        sp = jax.lax.conv_general_dilated(nc, dw_w, (1, 1), 'SAME', feature_group_count=C, dimension_numbers=DN) + dw_b[None, :, None, None]
        ch = jax.lax.conv_general_dilated(nc, pw_w, (1, 1), 'SAME', dimension_numbers=DN) + pw_b[None, :, None, None]
        sp = sp.reshape(B, C, H * W).transpose(0, 2, 1)
        ch = ch.reshape(B, C, H * W).transpose(0, 2, 1)
        g = x1 * (sp * ch)
        out = g @ W2 + b2
        return out.reshape(B, H, W, dim).transpose(0, 3, 1, 2)

    def _gn(v, G=16, eps=1e-05):
        B_, C_, H_, W_ = v.shape
        g = v.reshape(B_, G, C_ // G, H_, W_)
        m = jnp.mean(g, axis=(2, 3, 4), keepdims=True)
        s = jnp.var(g, axis=(2, 3, 4), keepdims=True)
        return ((g - m) / jnp.sqrt(s + eps)).reshape(v.shape)

    def _ln_c(v, eps=1e-06):
        m = jnp.mean(v, axis=1, keepdims=True)
        s = jnp.var(v, axis=1, keepdims=True)
        return (v - m) / jnp.sqrt(s + eps)

    def _ln_t(v, eps=1e-05):
        m = jnp.mean(v, axis=-1, keepdims=True)
        s = jnp.var(v, axis=-1, keepdims=True)
        return (v - m) / jnp.sqrt(s + eps)

    def _to_tokens(v):
        B_, C_, H_, W_ = v.shape
        return v.reshape(B_, C_, H_ * W_).transpose(0, 2, 1)

    def _from_tokens(t, like):
        B_, C_, H_, W_ = like.shape
        return t.transpose(0, 2, 1).reshape(B_, C_, H_, W_)
    x = x + _L0_conv_ref(_gn(x), L0_conv_qkv_w, L0_conv_dw_w, L0_conv_proj_w, L0_conv_temperature)
    x = x + _L1_conv_ref(_gn(x), L1_conv_down_w, L1_conv_down_b, L1_conv_right_w, L1_conv_right_b, L1_conv_left_w, L1_conv_left_b)
    x = x + _L2_conv_ref(_gn(x), L2_conv_down_w, L2_conv_down_b, L2_conv_right_w, L2_conv_right_b, L2_conv_left_w, L2_conv_left_b)
    x = x + _L3_conv_ref(_gn(x), L3_conv_W1, L3_conv_b1, L3_conv_gamma, L3_conv_beta, L3_conv_dw_w, L3_conv_dw_b, L3_conv_pw_w, L3_conv_pw_b, L3_conv_W2, L3_conv_b2)
    return x

_drawn_inputs = setup_inputs


def setup_inputs(seed=0):
    import zlib

    import numpy as np

    out = dict(_drawn_inputs(seed))
    spreads = {'L3_conv_b1': (0.0, 0.8),
     'L3_conv_gamma': (1.0, 0.6),
     'L3_conv_beta': (0.0, 0.8),
     'L3_conv_dw_b': (0.0, 0.8),
     'L3_conv_pw_b': (0.0, 0.8),
     'L3_conv_b2': (0.0, 2.0)}
    factors = {'L0_conv_qkv_w': 8.0,
     'L0_conv_dw_w': 8.0,
     'L0_conv_proj_w': 8.0,
     'L1_conv_right_b': 4.6,
     'L1_conv_left_b': 4.068,
     'L2_conv_down_b': 3.958,
     'L2_conv_right_b': 7.23,
     'L2_conv_left_b': 5.999,
     'L3_conv_W1': 8.0,
     'L3_conv_dw_w': 8.0,
     'L3_conv_pw_w': 8.0,
     'L3_conv_W2': 8.0}
    for name, (base, spread) in spreads.items():
        noise = np.random.default_rng([zlib.crc32(name.encode()), seed]).standard_normal(out[name].shape)
        drawn = base * np.exp(spread * noise) if base else spread * noise
        out[name] = jnp.asarray(drawn.astype(out[name].dtype))
    for name, factor in factors.items():
        out[name] = (out[name] * factor).astype(out[name].dtype)
    return out
```

```python
from contextlib import ExitStack

import concourse.bass as bass
from concourse import mybir

ALU = mybir.AluOpType
ACT = mybir.ActivationFunctionType
AX = mybir.AxisListType.X
F32 = mybir.dt.float32
ds = bass.ds

NB, C, H, W = 4, 48, 128, 128
HALF = 64
P = HALF + C
LO, HI = slice(0, C), slice(HALF, P)
K2, J2 = H // 2, W // 2
SUB = K2 * J2
IMG = 2 * SUB
COLS = NB * IMG
BN = 512
NSTAT = IMG // BN
GN_EPS = 1e-5
NORM_FLOOR_SQ = 1e-24

IN_ROWS = 16
IN_COLS = IN_ROWS * W
LOADS = H // IN_ROWS

BLK = 8
NBLK = K2 // BLK
ZSUB = (BLK + 2) * J2
PAIRS = 4 * NBLK
QK = 2 * C

STEPS = H - 1
PASSES = 4
CHUNK = 2048
NCH = COLS // CHUNK

TOK = 48
HID = 16
G = HID // 2
TCOLS = H * W * C // 128
TPAIRS = TCOLS // (2 * TOK)
GROUPS = TPAIRS // 4
GW = W + 2
WQ = 16
NQ = W // WQ
LN_EPS = 1e-5

TWO = 2


X_STATS = 1 + NB * LOADS // 2
N_CONST = 17 + 2 * G
N_SCAN_DMA = 2 + 6 * 10
N_BAND = G * 3 * 5
ATT_LINKS = 8
MLP_LINKS = 12


class Chain:

    def __init__(self, eng, sem):
        self.eng, self.sem, self.links, self.turn = eng, sem, 0, None

    def enter(self, turn, rate):
        self.turn, self.rate, self.first = turn, rate, self.links

    def leave(self, turns):
        assert self.links == self.first + self.rate, (self.links - self.first, self.rate)
        self.links, self.turn = self.first + turns * self.rate, None

    def link(self, ins):
        ins.then_inc(self.sem, 1)
        self.links += 1
        self.eng.wait_ge(self.sem, self.links if self.turn is None else self.turn * self.rate + self.links)


def build(nc, x, qkv_t, v_w, dw_t, dw_v, proj_t, temp, scan_w, scan_b,
          w1, b1, gamma, beta, gdw, gdw_b, gpw_t, gpw_b, w2, b2,
          ident_c, group_half_c, group_flat_c, saved, flat, out):
    with ExitStack() as ctx:
        def sb(name, shape):
            return ctx.enter_context(nc.sbuf_tensor(name, shape, F32))

        def sem(name):
            return ctx.enter_context(nc.semaphore(name))

        image = sb("image", [128, COLS])
        identp = sb("identp", [128, 130])
        group_half = sb("group_half", [P, P])
        group_flat = sb("group_flat", [128, 128])
        stats = sb("stats", [128, NB * NSTAT * 6])
        mean_var = sb("mean_var", [128, NB, 2])
        gn_mean = sb("gn_mean", [128, NB])
        gn_off = sb("gn_off", [128, NB])
        gn_sq = sb("gn_sq", [128, NB])
        gn_var = sb("gn_var", [128, NB])
        gn_std = sb("gn_std", [128, NB])
        gn_scale = sb("gn_scale", [128, NB])
        gn_shift = sb("gn_shift", [128, NB])
        scan_bias = sb("scan_bias", [P, 6])
        scan_wt = sb("scan_wt", [P, 6, 3, P])
        band = sb("band", [128, 3 * G, 128])
        gates = sb("gates", [128, 8 * G + 9 * G])
        work = sb("work", [128, 13300])
        ident = identp[:, 1:129]
        image5 = image[0:P, :].rearrange("p (b s k j) -> p b s k j", b=NB, s=2, k=K2)

        def cut(at, dims, parts=128):
            n = 1
            for m in dims:
                n *= m
            v = work[0:parts, at:at + n]
            if len(dims) == 2:
                v = v.rearrange("p (a b) -> p a b", a=dims[0])
            elif len(dims) == 3:
                v = v.rearrange("p (a b c) -> p a b c", a=dims[0], b=dims[1])
            return v

        rows_in = [cut(i * IN_COLS, [IN_COLS], P) for i in range(2)]
        blk_z = [cut(i * 2 * ZSUB, [2 * ZSUB], P) for i in range(2)]
        blk_n = [cut((2 + i) * 2 * ZSUB, [2 * ZSUB], P) for i in range(2)]
        at = 8 * ZSUB
        qkv_sb = cut(at, [3 * C], P)
        at += 3 * C
        qk_w = [cut(at + i * 6 * QK, [3, 2, QK], P) for i in range(2)]
        at += 12 * QK
        v_taps = cut(at, [9, P], C)
        at += 9 * P
        out_w = [cut(at + i * 3 * P, [3, P], P) for i in range(2)]
        at += 6 * P
        dw_sb = cut(at, [9, 3 * C], P)
        at += 27 * C
        gram = cut(at, [QK], QK)
        gram_d = cut(at + QK, [QK], QK)
        at += 2 * QK
        v_sb, proj_sb, logits, probs, probs_n, mix_t = (cut(at + i * C, [C], C) for i in range(6))
        ones = cut(at + 6 * C, [C], QK)
        at += 7 * C
        dwv_sb, temp_sb, col = cut(at, [9], C), cut(at + 9, [1], C), cut(at + 10, [8], QK)
        at += 18
        zero_row = cut(at, [J2], P)
        at += J2
        qk_sb = [cut(at + i * 4 * C * 2, [4 * C * 2]) for i in range(2)]
        at += 16 * C
        assert at <= 13300, at
        kept = [cut(i * CHUNK, [CHUNK], P) for i in range(2)]
        nat = [cut((2 + i) * CHUNK, [CHUNK], P) for i in range(2)]
        swap_tmp = cut(4 * CHUNK, [NB, 64], P)
        toks = image[:, 0:NB * TCOLS].rearrange("p (b n) -> p b n", b=NB)
        xn = image[:, NB * TCOLS:NB * TCOLS + TCOLS]
        hid = image[:, COLS - 2048:COLS]
        x_t = [cut(i * 512, [512]) for i in range(2)]
        at = 1024
        w1_sb = cut(at, [2 * HID], 97)
        at += 2 * HID
        pw_k = cut(at, [G, WQ])
        at += 128
        w2_k = cut(at, [TOK, WQ])
        at += TOK * WQ
        n_pad = cut(at, [G, GW])
        at += G * GW
        dev, dev2, n_t, g_t, chm, spm = (cut(at + i * 1024, [1024]) for i in range(6))
        at += 6 * 1024
        s1, s2, s3, s4, s5 = (cut(at + i * 128, [128]) for i in range(5))
        at += 5 * 128
        assert at <= 13300, at
        gdw_sb = gates[:, 0:72]
        gam_sb, bet_sb, dwb_sb, pwb_sb, pwr_sb = (gates[:, 72 + 8 * i:80 + 8 * i] for i in range(5))
        band_tmp = [sb(f"band_tmp{i}", [128, 128])[:, :] for i in range(2)]
        w2r_sb = sb("w2r_sb", [128, TOK])
        b2_sb = sb("b2_sb", [128, TOK])

        bank = [ctx.enter_context(nc.psum_tensor(f"bank{i}", [128, 512], F32)) for i in range(8)]
        bank_gram, bank_small, bank_wt = bank[2], bank[3], bank[4]
        bank_out = bank[5:7]
        bank_gn = bank[7]

        s_const = sem("s_const")
        s_gate_zero = sem("s_gate_zero")
        s_gate_const = sem("s_gate_const")
        s_pool = sem("s_pool")
        s_gap = sem("s_gap")
        s_zero = sem("s_zero")
        s_border = sem("s_border")
        s_load = [sem(f"s_load{i}") for i in range(2)]
        s_split = sem("s_split")
        s_stat = sem("s_stat")
        s_dve = sem("s_dve")
        s_gn_v = sem("s_gn_v")
        s_gn_mm = sem("s_gn_mm")
        s_gn_std = sem("s_gn_std")
        s_gn = sem("s_gn")
        s_wts = sem("s_wts")
        s_stage = sem("s_stage")
        s_qk = sem("s_qk")
        s_qk_sb = sem("s_qk_sb")
        s_gram = sem("s_gram")
        s_sm_v = sem("s_sm_v")
        s_sm_a = sem("s_sm_a")
        s_sm_t = sem("s_sm_t")
        s_outw = sem("s_outw")
        s_conv = sem("s_conv")
        s_x1 = sem("s_x1")
        s_save = sem("s_save")
        s_scan_w = sem("s_scan_w")
        s_scan_c = sem("s_scan_c")
        s_prod = [sem(f"s_prod{g}") for g in range(2)]
        s_state = [sem(f"s_state{g}") for g in range(2)]
        s_swap = sem("s_swap")
        s_back = [sem(f"s_back{i}") for i in range(2)]
        s_res = sem("s_res")
        s_flat = [sem(f"s_flat{i}") for i in range(2)]
        s_tok = [sem(f"s_tok{b}") for b in range(NB)]
        s_band = sem("s_band")
        s_xn = sem("s_xn")
        s_xt_p = sem("s_xt_p")
        s_xt_a = sem("s_xt_a")
        s_xt_v = sem("s_xt_v")
        s_hid = sem("s_hid")
        s_gelu = sem("s_gelu")
        s_ln = sem("s_ln")
        s_ln_a = sem("s_ln_a")
        s_gt_p = sem("s_gt_p")
        s_gt_a = sem("s_gt_a")
        s_gate = sem("s_gate")
        s_proj = sem("s_proj")
        s_add = sem("s_add")
        s_res3 = sem("s_res3")
        s_b2 = sem("s_b2")
        s_out = sem("s_out")

        block = ctx.enter_context(nc.Block())

        def own_wait(eng, semaphore, value):
            value = eng.compute_val(value)
            eng.wait_ge(s_gap, 2)
            eng.wait_ge(semaphore, value)

        SCANS = [(True, False, 0, False), (False, False, 0, True), (True, True, 1, False), (False, True, 2, False)]

        def line(g, along_w, sub, i):
            v = image5[:, 2 * g:2 * g + 2, sub, :, ds(i, 1)] if along_w else image5[:, 2 * g:2 * g + 2, sub, ds(i, 1), :]
            return v.rearrange("p b k j -> p b (k j)")

        def step_at(forward, k, u):
            if forward:
                return ((0, k), (1, k)) if u == 0 else ((1, k), (0, k + 1))
            return ((1, k), (0, k)) if u == 0 else ((0, k), (1, k - 1))

        TAPS = [(LO, 0, 0, 1), (LO, 1, 0, 0), (HI, 0, 0, 2), (HI, 1, 0, 1), (LO, 1, 1, 2), (HI, 0, 1, 0)]

        def conv_rows(sub):
            return [(0, 1, -1), (1, 0, 0), (2, 1, 0)] if sub == 0 else [(0, 0, 0), (1, 1, 0), (2, 0, 1)]

        @block.sync
        def _(sp):
            rows = x.rearrange("b c h w -> b c (h w)")
            sp.wait_ge(s_gap, 2)
            with sp.Fori(0, NB) as b:
                with sp.Fori(0, LOADS // 2) as q:
                    for m in range(2):
                        sp.wait_ge(s_split, b * LOADS + q * 2 + m + 1)
                        src = rows[ds(b, 1), :, ds(q * 2 * IN_COLS + m * IN_COLS, IN_COLS)]
                        sp.dma_start(rows_in[m][LO, :], src.rearrange("b c n -> (b c) n")).then_inc(s_load[m], 16)
                        src = rows[ds(b, 1), :, ds(q * 2 * IN_COLS + m * IN_COLS + 1, IN_COLS - 1)]
                        sp.dma_start(rows_in[m][HI, 0:IN_COLS - 1],
                                     src.rearrange("b c n -> (b c) n")).then_inc(s_load[m], 16)
            for b in range(NB):
                sp.wait_ge(s_x1, TWO + (b + 1) * 2 * NBLK)
                sp.dma_start(saved[0][:, b * IMG:(b + 1) * IMG],
                             image[0:P, b * IMG:(b + 1) * IMG]).then_inc(s_save, 16)
            sp.wait_ge(s_save, 16 * NB)
            with sp.Fori(0, NCH // 2) as t:
                for m in range(2):
                    sp.wait_ge(s_res, 2 * t + m + 1)
                    sp.dma_start(kept[m], saved[0][:, ds(t * 2 * CHUNK + m * CHUNK, CHUNK)]).then_inc(s_back[m], 16)
            sp.wait_ge(s_res, TWO + NCH)
            for b in range(NB):
                sp.dma_start(saved[1][:, b * IMG:(b + 1) * IMG],
                             image[0:P, b * IMG:(b + 1) * IMG]).then_inc(s_save, 16)
            sp.wait_ge(s_save, 32 * NB)
            kept_rows = saved[1].rearrange("p (b s n) -> p b s n", b=NB, s=2)
            with sp.Fori(0, NB // 2) as bp:
                with sp.Fori(0, NBLK // 2) as q:
                    for m in range(2):
                        sp.wait_ge(s_res, bp * NBLK + 2 * q + (NCH + m + 1))
                        src = kept_rows[:, ds(2 * bp, 2), :, ds(q * 2 * BN + m * BN, BN)]
                        sp.dma_start(kept[m].rearrange("p (a n) -> p a n", a=4),
                                     src.rearrange("p b s n -> p (b s) n")).then_inc(s_back[m], 16)
            for m in range(2):
                sp.wait_ge(s_flat[m], 32 + 32 * NCH // 2)
            for b in range(NB):
                sp.dma_start(toks[:, b, :], flat[b].rearrange("(p n) -> p n", p=128)).then_inc(s_tok[b], 16)
            grid = flat.rearrange("b (c h w) -> b h c w", c=C, h=H)
            grid_out = out.rearrange("b c h w -> b h c w")
            for b in range(NB):
                sp.wait_ge(s_xn, b + 1)
                dst = toks[:, b, :].rearrange("p (c w) -> p c w", c=C)
                sp.dma_start(dst, grid[b]).then_inc(s_res3, 16)
                sp.wait_ge(s_add, TWO + (b + 1) * 2 * NQ)
                sp.dma_start(grid_out[b], dst).then_inc(s_out, 16)
            sp.wait_ge(s_out, 16 * NB)

        @block.gpsimd
        def _(pool):
            pool_chain = Chain(pool, s_pool)

            def ms(v, value):
                pool_chain.link(nc.gpsimd.memset(v, value))

            for s, n in ((s_split, TWO), (s_qk_sb, TWO), (s_gram, TWO), (s_x1, TWO), (s_res, TWO),
                         (s_conv, 2 * NBLK), (s_qk, 4), (s_swap, 1), (s_add, TWO), (s_flat[0], 32), (s_flat[1], 32)):
                pool.sem_inc(s, n)
            for m in range(2):
                nc.gpsimd.memset(rows_in[m][32:HALF, :], 0.0).then_inc(s_gap, 1)
            pool.wait_ge(s_gap, 2)
            ms(ones, 1.0)
            ms(zero_row, 0.0)
            ms(qk_w[0], 0.0)
            ms(qk_w[1], 0.0)
            ms(v_taps, 0.0)
            ms(out_w[0], 0.0)
            nc.gpsimd.memset(out_w[1], 0.0).then_inc(s_zero, 1)
            pool.wait_ge(s_zero, 1)
            ms(scan_bias[:, :], 0.0)
            nc.gpsimd.memset(scan_wt[:, :, :, :], 0.0).then_inc(s_scan_w, 1)
            pool.wait_ge(s_scan_w, 1)
            pool.wait_ge(s_split, TWO + NB * LOADS)
            for m in range(2):
                ms(blk_n[m], 0.0)
                nc.gpsimd.memset(blk_z[m], 0.0).then_inc(s_border, 1)
                pool.wait_ge(s_border, m + 1)
            pool.wait_ge(s_const, 16 * N_CONST)
            n = 0
            for c in range(G):
                for dx in range(3):
                    for dy in range(3):
                        tap = gdw_sb[:, c * 9 + dy * 3 + dx:c * 9 + dy * 3 + dx + 1]
                        if dy:
                            pool.wait_ge(s_band, n)
                            ins = nc.gpsimd.tensor_scalar(band_tmp[dy - 1], identp[:, dy:dy + 128], tap, None, ALU.mult)
                            ins.then_inc(s_band, 1)
                            pool.wait_ge(s_band, n + 1)
                            nc.gpsimd.tensor_tensor(band[:, c * 3 + dx, :], band[:, c * 3 + dx, :], band_tmp[dy - 1],
                                                    ALU.add).then_inc(s_band, 1)
                            n += 2
                        else:
                            nc.gpsimd.tensor_scalar(band[:, c * 3 + dx, :], identp[:, 0:128], tap, None,
                                                    ALU.mult).then_inc(s_band, 1)
                            n += 1
            assert n == N_BAND
            pool.wait_ge(s_flat[0], 32 + 32 * NCH // 2)
            pool.wait_ge(s_flat[1], 32 + 32 * NCH // 2)
            ms(w1_sb, 0.0)
            ms(n_pad, 0.0)
            for m in range(2):
                nc.gpsimd.memset(x_t[m][96:128, :], 1.0).then_inc(s_gate_zero, 1)
            pool.wait_ge(s_gate_zero, 2)
            pool.dma_start(w1_sb[0:TOK, 0:HID], w1).then_inc(s_gate_const, 16)
            pool.dma_start(w1_sb[TOK:2 * TOK, HID:2 * HID], w1).then_inc(s_gate_const, 16)
            pool.dma_start(w1_sb[96:97, 0:HID], b1).then_inc(s_gate_const, 16)
            pool.dma_start(w1_sb[96:97, HID:2 * HID], b1).then_inc(s_gate_const, 16)
            pool.wait_ge(s_band, N_BAND)
            nc.gpsimd.tensor_copy(s1[:, 0:WQ], ident[:, 0:WQ]).then_inc(s_band, 1)
            n = N_BAND + 1
            for c in range(1, G):
                pool.wait_ge(s_band, n)
                nc.gpsimd.tensor_tensor(s1[:, 0:WQ], s1[:, 0:WQ], ident[:, c * WQ:(c + 1) * WQ],
                                        ALU.add).then_inc(s_band, 1)
                n += 1
            pool.wait_ge(s_band, n)
            for o in range(G):
                nc.gpsimd.tensor_scalar(pw_k[:, o, :], s1[:, 0:WQ], pwr_sb[:, o:o + 1], None, ALU.mult)
            for e in range(TOK):
                last = nc.gpsimd.tensor_scalar(w2_k[:, e, :], s1[:, 0:WQ], w2r_sb[:, e:e + 1], None, ALU.mult)
            last.then_inc(s_band, 1)
            with pool.Fori(0, NB) as b:
                pool.wait_ge(s_res3, 16 * b + 16)
                v = toks[:, ds(b, 1), :].rearrange("p b (c w) -> p (b c) w", c=C)
                nc.gpsimd.tensor_tensor(v, v, b2_sb[:, :].unsqueeze(2).to_broadcast([128, C, W]),
                                        ALU.add).then_inc(s_b2, 1)

        @block.scalar
        def _(act):
            consts = [(identp[:, :], ident_c), (group_half[:, :], group_half_c), (group_flat[:, :], group_flat_c),
                      (qkv_sb[LO, :], qkv_t), (qkv_sb[HI, :], qkv_t),
                      (dw_sb[LO].rearrange("p a b -> p (a b)"), dw_t.partition_broadcast(C)),
                      (dw_sb[HI].rearrange("p a b -> p (a b)"), dw_t.partition_broadcast(C)),
                      (v_sb, v_w), (dwv_sb, dw_v), (proj_sb, proj_t), (temp_sb, temp.partition_broadcast(C)),
                      (gdw_sb, gdw.partition_broadcast(128)), (gam_sb, gamma.partition_broadcast(128)),
                      (bet_sb, beta.partition_broadcast(128)), (dwb_sb, gdw_b.partition_broadcast(128)),
                      (pwb_sb, gpw_b.partition_broadcast(128)), (b2_sb[:, :], b2.partition_broadcast(128))]
            for c in range(G):
                consts.append((pwr_sb[c * WQ:(c + 1) * WQ, :], gpw_t[c].partition_broadcast(WQ)))
                consts.append((w2r_sb[c * WQ:(c + 1) * WQ, :], w2[c].partition_broadcast(WQ)))
            assert len(consts) == N_CONST
            for dst, src in consts:
                act.dma_start(dst, src).then_inc(s_const, 16)

            with act.Fori(0, NB) as b:
                with act.Fori(0, LOADS // 2) as q:
                    for m in range(2):
                        own_wait(act, s_load[m], b * (LOADS * 16) + q * 32 + 32)
                        src = rows_in[m].rearrange("p (k s j q) -> p s k j q", k=BLK, s=2, j=J2)[:, :, :, :, 0]
                        dst = image5[:, ds(b, 1), :, ds(q * 2 * BLK + m * BLK, BLK), :]
                        nc.scalar.copy(dst.rearrange("p b s k j -> p (b s) k j"), src).then_inc(s_split, 1)

            act.wait_ge(s_scan_w, 1)
            n_dma = 0
            for half in (LO, HI):
                act.dma_start(scan_bias[half, :], scan_b).then_inc(s_scan_c, 16)
                n_dma += 1
            for t in range(6):
                for qi, rows in enumerate((LO, HI)):
                    for qo, cols in enumerate((LO, HI)):
                        shifts = [m for m in (-1, 0, 1) if 0 <= 2 * m + qi - qo + 2 < 5]
                        for m in shifts:
                            act.dma_start(scan_wt[rows, t, m + 1, cols],
                                          scan_w[t][:, 2 * m + qi - qo + 2, :]).then_inc(s_scan_c, 16)
                            n_dma += 1
            assert n_dma == N_SCAN_DMA

            def deviation(r):
                act.wait_ge(s_gn_v, 3 * r + 3)
                nc.scalar.activation(gn_std[:, :], gn_var[:, :], ACT.Sqrt).then_inc(s_gn_std, 1)

            deviation(0)

            def stage(b, n, m):
                for sub in range(2):
                    kk0, rows = 1 - sub, BLK + 1
                    top = isinstance(n, int) and n == 0 and sub == 1
                    bottom = isinstance(n, int) and n == NBLK - 1 and sub == 0
                    if top or bottom:
                        o = sub * ZSUB + (0 if top else BLK + 1) * J2
                        nc.scalar.copy(blk_z[m][:, o:o + J2], zero_row)
                        nc.scalar.copy(blk_n[m][:, o:o + J2], zero_row)
                        rows = BLK
                        kk0 += top
                    for buf, part, d, e in ((blk_z, slice(0, P), (0, J2), (0, J2)),
                                            (blk_n, LO, (0, J2 - 1), (1, J2)), (blk_n, HI, (1, J2), (0, J2 - 1))):
                        dst = buf[m][part, sub * ZSUB + kk0 * J2:sub * ZSUB + (kk0 + rows) * J2]
                        src = image5[part, ds(b, 1), sub, ds(n * BLK - 1 + kk0, rows), e[0]:e[1]]
                        last = nc.scalar.activation(dst.rearrange("p (k j) -> p k j", j=J2)[:, :, d[0]:d[1]],
                                                    src.rearrange("p b k j -> p (b k) j"), ACT.Identity,
                                                    bias=gn_shift[part, ds(b, 1)], scale=gn_scale[part, ds(b, 1)])
                last.then_inc(s_stage, 1)

            act.wait_ge(s_gn, 1)
            act.wait_ge(s_border, 2)
            with act.Fori(0, NB) as b:
                own_wait(act, s_conv, b * 2 * NBLK + 2 * NBLK - 2)
                stage(b, 0, 0)
                act.wait_ge(s_conv, b * 2 * NBLK + 2 * NBLK)
                with act.Fori(0, NBLK // 2 - 1) as h:
                    for u in range(2):
                        own_wait(act, s_qk, b * PAIRS + 8 * h + 4 * (u + 1))
                        stage(b, 2 * h + (1 + u), 1 - u)
                own_wait(act, s_qk, b * PAIRS + 4 * (NBLK - 1))
                stage(b, NBLK - 1, 1)
                own_wait(act, s_qk, b * PAIRS + 4 * NBLK)
                stage(b, 0, 0)
                act.wait_ge(s_sm_v, 5 * b + 1)
                nc.scalar.activation(col[:, 2:3], col[:, 1:2], ACT.Sqrt).then_inc(s_sm_a, 1)
                act.wait_ge(s_sm_v, 5 * b + 3)
                nc.scalar.activation(probs, logits, ACT.Exp, bias=col[0:C, 5:6],
                                     accum_out=col[0:C, 6:7]).then_inc(s_sm_a, 1)
                act.wait_ge(s_qk, b * PAIRS + 4 * NBLK + 4)
                with act.Fori(0, NBLK // 2 - 1) as h:
                    for u in range(2):
                        own_wait(act, s_conv, b * 2 * NBLK + 4 * h + (2 * NBLK + 2 * u))
                        stage(b, 2 * h + (1 + u), 1 - u)
                own_wait(act, s_conv, b * 2 * NBLK + 2 * NBLK + 2 * (NBLK - 2))
                stage(b, NBLK - 1, 1)

            def normalise(layer):
                act.wait_ge(s_gn, layer + 2)
                act.wait_ge(s_save, (layer + 1) * 16 * NB)
                for b in (2, 3):
                    v = image[0:P, b * IMG:(b + 1) * IMG]
                    last = nc.scalar.activation(v, v, ACT.Identity, bias=gn_shift[0:P, b:b + 1],
                                                scale=gn_scale[0:P, b:b + 1])
                last.then_inc(s_state[1], 1)

            def exchange(along_w, i, n):
                def part(rows, s):
                    v = image5[rows, :, s, :, ds(i, 1)] if along_w else image5[rows, :, s, ds(i, 1), :]
                    return v.rearrange("p b k j -> p b (k j)")
                own_wait(act, s_swap, n + 1)
                nc.scalar.copy(swap_tmp[HI], part(LO, 1)).then_inc(s_swap, 1)
                own_wait(act, s_swap, n + 2)
                nc.scalar.copy(part(LO, 1), part(HI, 0)).then_inc(s_swap, 1)
                own_wait(act, s_swap, n + 3)
                nc.scalar.copy(part(HI, 0), swap_tmp[HI]).then_inc(s_swap, 1)

            for layer in range(2):
                deviation(layer + 1)
                normalise(layer)
                for g in range(2):
                    act.wait_ge(s_prod[g], layer * PASSES * STEPS + 1)
                n0 = layer * 2 * 3 * K2
                prod0 = layer * PASSES * STEPS + STEPS
                with act.Fori(0, K2 - 2) as i:
                    for g in range(2):
                        own_wait(act, s_prod[g], 2 * i + (prod0 + 4))
                    exchange(False, K2 - 2 - i, 3 * i + n0)
                for g in range(2):
                    act.wait_ge(s_state[g], layer * (PASSES * STEPS + 1) + 1 + 2 * STEPS)
                exchange(False, 0, n0 + 3 * (K2 - 2))
                exchange(False, K2 - 1, n0 + 3 * (K2 - 1))
                n0 += 3 * K2
                prod0 += 2 * STEPS
                with act.Fori(0, K2 - 1) as i:
                    for g in range(2):
                        own_wait(act, s_prod[g], 2 * i + (prod0 + 2))
                    exchange(True, K2 - 1 - i, 3 * i + n0)
                for g in range(2):
                    act.wait_ge(s_state[g], (layer + 1) * (PASSES * STEPS + 1))
                exchange(True, 0, n0 + 3 * (K2 - 1))
            rows = flat.rearrange("b (c n) -> b c n", c=C)
            with act.Fori(0, NB // 2) as bp:
                with act.Fori(0, NBLK // 2) as q:
                    for m in range(2):
                        act.wait_ge(s_res, bp * NBLK + 2 * q + (TWO + NCH + m + 1))
                        for i, part in enumerate((LO, HI)):
                            dst = rows[ds(2 * bp + i, 1), :, ds(q * 2 * CHUNK + m * CHUNK, CHUNK)]
                            act.dma_start(dst.rearrange("b c n -> (b c) n"), nat[m][part, :]).then_inc(s_flat[m], 16)
            deviation(3)

            with act.Fori(0, NB) as b:
                for g in range(0, GROUPS, 2):
                    act.wait_ge(s_xt_p, b * GROUPS + g + 1)
                    nc.scalar.copy(x_t[0][0:96, :], bank[0][0:96, :]).then_inc(s_xt_a, 1)
                for i in range(4):
                    act.wait_ge(s_hid, b * GROUPS + 4 * (i + 1))
                    nc.scalar.activation(hid[:, i * 512:(i + 1) * 512], bank[2 + i][:, :], ACT.Gelu).then_inc(s_gelu, 1)
                act.wait_ge(s_gelu, b * 5 + 4)
                nc.scalar.activation(hid, hid, ACT.Gelu).then_inc(s_gelu, 1)
                act.wait_ge(s_ln, b * 2 + 1)
                nc.scalar.activation(s4, s3, ACT.Sqrt).then_inc(s_ln_a, 1)
                act.wait_ge(s_ln, b * 2 + 2)
                act.wait_ge(s_gate_zero, 2)
                nc.scalar.copy(n_pad[:, :, 1:1 + W].rearrange("p c (q w) -> p q c w", q=NQ),
                               spm.rearrange("p (q c w) -> p q c w", q=NQ, c=G)).then_inc(s_ln_a, 1)
                for first, dst in ((1, n_t), (7, g_t)):
                    for i in range(2):
                        act.wait_ge(s_gt_p, b * 8 + first + i)
                        nc.scalar.copy(dst[:, i * 512:(i + 1) * 512], bank[i][:, :]).then_inc(s_gt_a, 1)

        @block.tensor
        def _(pe):
            mm = nc.tensor.matmul

            def group_sums(r, parts, groups):
                pe.wait_ge(s_gn_v, 3 * r + 1)
                mm(bank_gn[0:parts, 0:NB], groups, mean_var[0:parts, :, 0], start=True, stop=True).then_inc(s_gn_mm, 1)
                pe.wait_ge(s_gn_v, 3 * r + 2)
                mm(bank_gn[0:parts, NB:2 * NB], groups, gn_sq[0:parts, :], start=True, stop=True).then_inc(s_gn_mm, 1)

            pe.wait_ge(s_const, 16 * N_CONST)
            group_sums(0, P, group_half[:, :])
            pe.wait_ge(s_wts, 1)

            with pe.Fori(0, NB) as b:
                def conv_pair(i):
                    n, sub, kp = i // 4, (i // 2) % 2, 2 * (i % 2)
                    if i % 4 == 0:
                        pe.wait_ge(s_stage, b * 2 * NBLK + n + 1)
                    pe.wait_ge(s_qk_sb, b * PAIRS + i + 1)
                    for c in range(2):
                        dst = bank[i % 2][:, c * 2 * QK:(c + 1) * 2 * QK]
                        prods = [(buf, dy, s, dk) for buf in range(2) for dy, s, dk in conv_rows(sub)]
                        for t, (buf, dy, s, dk) in enumerate(prods):
                            o = s * ZSUB + (1 + 2 * (kp + c) + dk) * J2
                            last = mm(dst, (blk_z, blk_n)[buf][n % 2][:, o:o + 2 * J2],
                                      qk_w[buf][:, dy].rearrange("p a b -> p (a b)"),
                                      start=(t == 0), stop=(t == len(prods) - 1))
                    last.then_inc(s_qk, 1)

                def gram_pair(i):
                    pe.wait_ge(s_qk_sb, b * PAIRS + i + 1 + TWO)
                    for c in range(4):
                        v = qk_sb[i % 2][:, c * QK:(c + 1) * QK]
                        last = mm(bank_gram[0:QK, 0:QK], v, v, start=(i == 0 and c == 0),
                                  stop=(i == PAIRS - 1 and c == 3))
                    last.then_inc(s_gram, 1)

                for i in range(PAIRS + 1):
                    if i < PAIRS:
                        conv_pair(i)
                    if i:
                        gram_pair(i - 1)
                own_wait(pe, s_sm_v, 5 * b + 2)
                mm(bank_small[0:C, 0:C], ones, gram_d[:, C:QK], start=True, stop=True).then_inc(s_sm_t, 1)
                own_wait(pe, s_sm_v, 5 * b + 4)
                mm(bank_small[0:C, 64:64 + C], probs_n, proj_sb, start=True, stop=True).then_inc(s_sm_t, 1)
                pe.wait_ge(s_sm_v, 5 * b + 5)
                for t in range(9):
                    last = mm(bank_wt[0:P, t * C:(t + 1) * C], v_taps[:, t, :], mix_t, start=True, stop=True)
                last.then_inc(s_sm_t, 1)
                pe.wait_ge(s_outw, b + 1)
                for n in range(NBLK):
                    pe.wait_ge(s_stage, b * 2 * NBLK + NBLK + n + 1)
                    for sub in range(2):
                        pe.wait_ge(s_x1, b * 2 * NBLK + 2 * n + sub + 1)
                        prods = [(buf, dy, s, dk) for buf in range(2) for dy, s, dk in conv_rows(sub)]
                        for t, (buf, dy, s, dk) in enumerate(prods):
                            o = s * ZSUB + (1 + dk) * J2
                            last = mm(bank_out[sub][0:P, :], out_w[buf][:, dy, :],
                                      (blk_z, blk_n)[buf][n % 2][:, o:o + BLK * J2],
                                      start=(t == 0), stop=(t == len(prods) - 1))
                        last.then_inc(s_conv, 1)

            def step(layer, done, scan, k, u):
                forward, along_w, kind, _ = SCANS[scan]
                (sub, at), _ = step_at(forward, k, u)
                wt = scan_wt[:, 3 * layer + kind]
                for g in range(2):
                    pe.wait_ge(s_state[g], done + (layer * (PASSES * STEPS + 1) + 1))
                    src = line(g, along_w, sub, at)
                    dst = bank[g][0:P, 0:2 * J2].rearrange("p (b j) -> p b j", b=2)
                    mm(dst, wt[:, 1], src, start=True, stop=False)
                    mm(dst[:, :, 1:J2], wt[:, 0], src[:, :, 0:J2 - 1], start=False, stop=False)
                    mm(dst[:, :, 0:J2 - 1], wt[:, 2], src[:, :, 1:J2], start=False, stop=True).then_inc(s_prod[g], 1)

            for layer in range(2):
                group_sums(layer + 1, P, group_half[:, :])
                if layer == 0:
                    pe.wait_ge(s_scan_c, 16 * N_SCAN_DMA)
                for scan in range(PASSES):
                    if scan == 2:
                        pe.wait_ge(s_swap, (2 * layer + 1) * 3 * K2 + 1)
                    with pe.Fori(0, K2 - 1) as i:
                        k = i if SCANS[scan][0] else pe.compute_val(K2 - 1 - i)
                        for u in range(2):
                            step(layer, 2 * i + (scan * STEPS + u), scan, k, u)
                    step(layer, scan * STEPS + STEPS - 1, scan, K2 - 1 if SCANS[scan][0] else 0, 0)

            group_sums(3, 128, group_flat[:, :])
            pe.wait_ge(s_gate_const, 16 * 4)
            pe.wait_ge(s_band, N_BAND + G + 1)
            with pe.Fori(0, NB) as b:
                def turn_tokens(g):
                    if g >= 2:
                        pe.wait_ge((s_xt_a, s_xt_v)[g % 2], b * (GROUPS // 2) + g // 2)
                    for t in range(4):
                        o = (4 * g + t) * 2 * TOK
                        last = nc.tensor.transpose(bank[g % 2][0:2 * TOK, t * 128:(t + 1) * 128],
                                                   xn[:, o:o + 2 * TOK], ident)
                    last.then_inc(s_xt_p, 1)

                def hidden(g):
                    pe.wait_ge((s_xt_a, s_xt_v)[g % 2], b * (GROUPS // 2) + g // 2 + 1)
                    for t in range(4):
                        o = (g % 4 * 4 + t) * 2 * HID
                        last = mm(bank[2 + g // 4][:, o:o + 2 * HID], x_t[g % 2][0:97, t * 128:(t + 1) * 128],
                                  w1_sb, start=True, stop=True)
                    last.then_inc(s_hid, 1)

                pe.wait_ge(s_xn, b + 1)
                turn_tokens(0)
                pe.wait_ge(s_add, b * 2 * NQ + TWO)
                for g in range(1, GROUPS + 1):
                    if g < GROUPS:
                        turn_tokens(g)
                    hidden(g - 1)
                pe.wait_ge(s_ln, b * 2 + 2)
                for q in range(NQ):
                    last = nc.tensor.transpose(bank[q // 4][:, q % 4 * 128:(q % 4 + 1) * 128],
                                               spm[:, q * 128:(q + 1) * 128], ident)
                    if q % 4 == 3:
                        last.then_inc(s_gt_p, 1)
                pe.wait_ge(s_ln_a, b * 2 + 2)
                for c in range(G):
                    for dx in range(3):
                        last = mm(bank[6 + c // 4][:, c % 4 * 128:(c % 4 + 1) * 128], band[:, c * 3 + dx, :],
                                  n_pad[:, c, dx:dx + W], start=(dx == 0), stop=(dx == 2))
                    if c % 4 == 3:
                        last.then_inc(s_gt_p, 1)
                for q in range(NQ):
                    if q % 4 == 0:
                        pe.wait_ge(s_gt_a, b * 4 + q // 4 + 1)
                    last = mm(bank[2 + q // 4][:, q % 4 * 128:(q % 4 + 1) * 128], n_t[:, q * 128:(q + 1) * 128],
                              pw_k.rearrange("p a b -> p (a b)"), start=True, stop=True)
                    if q % 4 == 3:
                        last.then_inc(s_gt_p, 1)
                pe.wait_ge(s_gate, b + 1)
                for q in range(NQ):
                    last = nc.tensor.transpose(bank[q // 4][:, q % 4 * 128:(q % 4 + 1) * 128],
                                               chm[:, q * 128:(q + 1) * 128], ident)
                    if q % 4 == 3:
                        last.then_inc(s_gt_p, 1)
                for q in range(NQ):
                    if q % 4 == 0:
                        pe.wait_ge(s_gt_a, b * 4 + q // 4 + 3)
                    for f in range(2):
                        pe.wait_ge(s_add, b * 2 * NQ + 2 * q + f + 1)
                        mm(bank[4 + f][:, 0:TOK // 2 * WQ], g_t[:, q * 128:(q + 1) * 128],
                           w2_k[:, f * TOK // 2:(f + 1) * TOK // 2, :].rearrange("p a b -> p (a b)"),
                           start=True, stop=True).then_inc(s_proj, 1)

        @block.vector
        def _(dve):
            chain = Chain(dve, s_dve)
            link = chain.link
            v = nc.vector
            stat6 = stats[:, :].rearrange("p (b n) -> p b n", b=NB)

            def take_stats(parts, b, c, src):
                dst = stat6[0:parts, ds(b, 1), ds(c * 6, 6)].rearrange("p b n -> p (b n)")
                return v.bn_stats(dst, src)

            def group_norm(r, parts, n_stat):
                p = slice(0, parts)
                for b in range(NB):
                    last = v.bn_aggr(mean_var[p, b, :], stat6[p, b, 0:6 * n_stat])
                last.then_inc(s_gn_v, 1)
                dve.wait_ge(s_gn_mm, 2 * r + 1)
                link(v.tensor_copy(gn_mean[p, :], bank_gn[p, 0:NB]))
                link(v.tensor_tensor(gn_off[p, :], mean_var[p, :, 0], gn_mean[p, :], ALU.subtract))
                link(v.tensor_tensor(gn_sq[p, :], gn_off[p, :], gn_off[p, :], ALU.mult))
                v.tensor_tensor(gn_sq[p, :], gn_sq[p, :], mean_var[p, :, 1], ALU.add).then_inc(s_gn_v, 1)
                dve.wait_ge(s_gn_mm, 2 * r + 2)
                v.tensor_scalar(gn_var[p, :], bank_gn[p, NB:2 * NB], GN_EPS, None, ALU.add).then_inc(s_gn_v, 1)
                dve.wait_ge(s_gn_std, r + 1)
                link(v.reciprocal(gn_scale[p, :], gn_std[p, :]))
                v.scalar_tensor_tensor(out=gn_shift[p, :], in0=gn_mean[p, :], scalar=-1.0, in1=gn_scale[p, :],
                                       op0=ALU.mult, op1=ALU.mult).then_inc(s_gn, 1)
                dve.wait_ge(s_gn, r + 1)

            v.memset(gn_std[:, :], 1.0)
            v.memset(gn_var[:, :], 1.0).then_inc(s_stat, 1)
            with dve.Fori(0, NB) as b:
                with dve.Fori(0, LOADS // 2) as q:
                    for m in range(2):
                        dve.wait_ge(s_split, b * LOADS + 2 * q + (m + 1 + TWO))
                        for s in range(2):
                            src = image5[:, ds(b, 1), s, ds(q * 2 * BLK + m * BLK, BLK), :]
                            last = take_stats(P, b, q * 4 + m * 2 + s, src.rearrange("p b k j -> p (b k j)"))
                    last.then_inc(s_stat, 1)
            dve.wait_ge(s_const, 16 * N_CONST)
            dve.wait_ge(s_zero, 1)
            for rows, pos, buf, dx in TAPS:
                for dy in range(3):
                    v.tensor_tensor(qk_w[buf][rows, dy, pos, :], qkv_sb[rows, 0:QK], dw_sb[rows, dy * 3 + dx, 0:QK],
                                    ALU.mult)
            for t in range(9):
                for cols in (LO, HI):
                    last = v.tensor_scalar(v_taps[:, t, cols], v_sb, dwv_sb[:, t:t + 1], None, ALU.mult)
            last.then_inc(s_wts, 1)
            dve.wait_ge(s_stat, X_STATS)
            group_norm(0, P, NSTAT)

            with dve.Fori(0, NB) as b:
                chain.enter(b, ATT_LINKS)
                for i in range(PAIRS):
                    dve.wait_ge(s_qk, b * PAIRS + i + 1 + 4)
                    dve.wait_ge(s_gram, b * PAIRS + i + 1)
                    v.tensor_copy(qk_sb[i % 2], bank[i % 2][:, 0:4 * QK]).then_inc(s_qk_sb, 1)
                dve.wait_ge(s_gram, b * PAIRS + PAIRS + TWO)
                link(v.tensor_copy(gram, bank_gram[0:QK, 0:QK]))
                link(v.tensor_tensor(gram_d, gram, ident[0:QK, 0:QK], ALU.mult))
                link(v.tensor_reduce(col[:, 0:1], gram_d, AX, ALU.add))
                v.tensor_scalar(col[:, 1:2], col[:, 0:1], NORM_FLOOR_SQ, None, ALU.max).then_inc(s_sm_v, 1)
                dve.wait_ge(s_sm_a, 2 * b + 1)
                link(v.reciprocal(col[:, 3:4], col[:, 2:3]))
                v.tensor_scalar(gram_d, ident[0:QK, 0:QK], col[:, 3:4], None, ALU.mult).then_inc(s_sm_v, 1)
                dve.wait_ge(s_sm_t, 3 * b + 1)
                link(v.scalar_tensor_tensor(out=logits, in0=gram[0:C, C:QK], scalar=col[0:C, 3:4],
                                            in1=bank_small[0:C, 0:C], op0=ALU.mult, op1=ALU.mult))
                link(v.tensor_scalar(logits, logits, temp_sb, None, ALU.mult))
                link(v.tensor_reduce(col[0:C, 4:5], logits, AX, ALU.max))
                v.tensor_scalar(col[0:C, 5:6], col[0:C, 4:5], -1.0, None, ALU.mult).then_inc(s_sm_v, 1)
                dve.wait_ge(s_sm_a, 2 * b + 2)
                link(v.reciprocal(col[0:C, 7:8], col[0:C, 6:7]))
                v.tensor_scalar(probs_n, probs, col[0:C, 7:8], None, ALU.mult).then_inc(s_sm_v, 1)
                dve.wait_ge(s_sm_t, 3 * b + 2)
                v.tensor_copy(mix_t, bank_small[0:C, 64:64 + C]).then_inc(s_sm_v, 1)
                dve.wait_ge(s_sm_t, 3 * b + 3)
                taps = bank_wt[:, 0:9 * C].rearrange("p (y x c) -> p y x c", y=3, x=3)
                for rows, pos, buf, dx in TAPS:
                    last = v.tensor_copy(out_w[buf][rows, :, (LO, HI)[pos]], taps[rows, :, dx, :])
                last.then_inc(s_outw, 1)
                def add_block(n):
                    for sub in range(2):
                        dve.wait_ge(s_conv, b * 2 * NBLK + 2 * n + (2 * NBLK + sub + 1))
                        if not isinstance(n, int):
                            dve.wait_ge(s_stage, b * 2 * NBLK + n + (NBLK + 2))
                        dst = image5[:, ds(b, 1), sub, ds(n * BLK, BLK), :].rearrange("p b k j -> p (b k j)")
                        v.tensor_tensor(dst, dst, bank_out[sub][0:P, :], ALU.add).then_inc(s_x1, 1)
                        dve.wait_ge(s_x1, b * 2 * NBLK + 2 * n + (sub + 1 + TWO))
                        last = take_stats(P, b, 2 * n + sub, dst)
                    return last

                with dve.Fori(0, NBLK - 1) as n:
                    add_block(n)
                last = add_block(NBLK - 1)
                last.then_inc(s_stat, 1)
                chain.leave(NB)

            def step(layer, done, scan, k, u):
                forward, along_w, kind, ahead = SCANS[scan]
                _, (sub, at) = step_at(forward, k, u)
                if not ahead:
                    src = (sub, at)
                elif u == 0:
                    src = (1, K2 - 1) if isinstance(k, int) else (1, at - 1)
                else:
                    src = (0, at)
                for g in range(2):
                    dve.wait_ge(s_prod[g], done + (layer * PASSES * STEPS + 1))
                    prod = bank[g][0:P, 0:2 * J2].rearrange("p (b j) -> p b j", b=2)
                    v.scalar_tensor_tensor(out=line(g, along_w, sub, at), in0=prod,
                                           scalar=scan_bias[:, 3 * layer + kind:3 * layer + kind + 1],
                                           in1=line(g, along_w, *src), op0=ALU.add, op1=ALU.add).then_inc(s_state[g], 1)

            for layer in range(2):
                n_res = layer * NCH
                dve.wait_ge(s_stat, X_STATS + (1 + layer) * NB)
                group_norm(layer + 1, P, NSTAT)
                dve.wait_ge(s_save, (layer + 1) * 16 * NB)
                for b in range(2):
                    cols = image[0:P, b * IMG:(b + 1) * IMG]
                    last = v.tensor_scalar(cols, cols, gn_scale[0:P, b:b + 1], gn_shift[0:P, b:b + 1],
                                           ALU.mult, ALU.add)
                last.then_inc(s_state[0], 1)
                dve.wait_ge(s_scan_c, 16 * N_SCAN_DMA)
                for scan in range(PASSES):
                    with dve.Fori(0, K2 - 1) as i:
                        k = i if SCANS[scan][0] else dve.compute_val(K2 - 1 - i)
                        for u in range(2):
                            step(layer, 2 * i + (scan * STEPS + u), scan, k, u)
                    step(layer, scan * STEPS + STEPS - 1, scan, K2 - 1 if SCANS[scan][0] else 0, 0)
                dve.wait_ge(s_swap, (layer + 1) * 6 * K2 + 1)
                if layer == 0:
                    with dve.Fori(0, NCH // 4) as t:
                        for m in range(4):
                            dve.wait_ge(s_back[m % 2], t * 32 + (m // 2 + 1) * 16)
                            dst = image[0:P, ds(t * 4 * CHUNK + m * CHUNK, CHUNK)]
                            v.tensor_tensor(dst, dst, kept[m % 2], ALU.add).then_inc(s_res, 1)
                            dve.wait_ge(s_res, 4 * t + (m + 1 + TWO))
                            for c in range(4):
                                src = image[0:P, ds(t * 4 * CHUNK + (m * CHUNK + c * BN), BN)]
                                last = take_stats(P, t, m * 4 + c, src)
                        last.then_inc(s_stat, 1)
                else:
                    with dve.Fori(0, NB // 2) as bp:
                        with dve.Fori(0, NBLK // 2) as q:
                            for m in range(2):
                                dve.wait_ge(s_back[m], bp * (NBLK * 8) + q * 16 + (8 * NCH + 16))
                                dve.wait_ge(s_flat[m], bp * (NBLK * 16) + q * 32 + 32)
                                for a in range(2):
                                    for half, src in enumerate((LO, HI)):
                                        lanes = (LO, HI)[a]
                                        o = nat[m][lanes, :].rearrange("p (k s j q) -> p s k j q", k=BLK, s=2, j=J2)
                                        i0 = image5[src, ds(2 * bp + a, 1), :, ds(q * 2 * BLK + m * BLK, BLK), :]
                                        i1 = kept[m][src, a * 2 * BN:(a + 1) * 2 * BN]
                                        last = v.tensor_tensor(
                                            o[:, :, :, :, half], i0.rearrange("p b s k j -> p (b s) k j"),
                                            i1.rearrange("p (s k j) -> p s k j", s=2, k=BLK), ALU.add)
                                last.then_inc(s_res, 1)

            for b in range(NB):
                dve.wait_ge(s_tok[b], 16)
                for c in range(TCOLS // BN):
                    last = take_stats(128, b, c, toks[:, b, c * BN:(c + 1) * BN])
            last.then_inc(s_stat, 1)
            dve.wait_ge(s_stat, X_STATS + 2 * NB + 1)
            group_norm(3, 128, TCOLS // BN)
            per_w = [128, W, G]
            x1 = hid.rearrange("p (w f) -> p w f", f=HID)[:, :, 0:G]
            x2 = hid.rearrange("p (w f) -> p w f", f=HID)[:, :, G:HID]
            dev_v = dev.rearrange("p (w f) -> p w f", f=G)
            dev2_v = dev2.rearrange("p (w f) -> p w f", f=G)
            chm_v = chm.rearrange("p (q c w) -> p q c w", q=NQ, c=G)
            spm_v = spm.rearrange("p (q c w) -> p q c w", q=NQ, c=G)

            with dve.Fori(0, NB) as b:
                chain.enter(b, MLP_LINKS)
                v.tensor_scalar(xn, toks[:, ds(b, 1), :].rearrange("p b n -> p (b n)"), gn_scale[:, ds(b, 1)],
                                gn_shift[:, ds(b, 1)], ALU.mult, ALU.add).then_inc(s_xn, 1)
                for g in range(1, GROUPS, 2):
                    dve.wait_ge(s_xt_p, b * GROUPS + g + 1)
                    if g == 1:
                        dve.wait_ge(s_gate_zero, 2)
                    v.tensor_copy(x_t[1][0:96, :], bank[1][0:96, :]).then_inc(s_xt_v, 1)
                dve.wait_ge(s_gelu, 5 * b + 5)
                link(v.tensor_reduce(s1, x2, AX, ALU.add))
                link(v.scalar_tensor_tensor(out=dev_v, in0=s1.unsqueeze(2).to_broadcast(per_w), scalar=-1.0 / G,
                                            in1=x2, op0=ALU.mult, op1=ALU.add))
                link(v.tensor_tensor(dev2, dev, dev, ALU.mult))
                link(v.tensor_reduce(s2, dev2_v, AX, ALU.add))
                v.tensor_scalar(s3, s2, 1.0 / G, LN_EPS, ALU.mult, ALU.add).then_inc(s_ln, 1)
                dve.wait_ge(s_ln_a, 2 * b + 1)
                link(v.reciprocal(s5, s4))
                link(v.tensor_tensor(dev2_v, dev_v, s5.unsqueeze(2).to_broadcast(per_w), ALU.mult))
                link(v.tensor_tensor(dev2_v, dev2_v, gam_sb.unsqueeze(1).to_broadcast(per_w), ALU.mult))
                v.tensor_tensor(spm_v.rearrange("p q c w -> p q w c"),
                                dev2.rearrange("p (q w f) -> p q w f", q=NQ, f=G),
                                bet_sb.unsqueeze(1).unsqueeze(1).to_broadcast([128, NQ, WQ, G]),
                                ALU.add).then_inc(s_ln, 1)
                dve.wait_ge(s_gt_p, 8 * b + 6)
                for i in range(2):
                    q4 = [128, 4, G, WQ]
                    link(v.tensor_tensor(chm_v[:, 4 * i:4 * i + 4],
                                         bank[2 + i][:, :].rearrange("p (q c w) -> p q c w", q=4, c=G),
                                         pwb_sb.unsqueeze(1).unsqueeze(3).to_broadcast(q4), ALU.add))
                    c4 = [128, NQ, 4, WQ]
                    link(v.tensor_tensor(spm_v[:, :, 4 * i:4 * i + 4, :],
                                         bank[6 + i][:, :].rearrange("p (c q w) -> p q c w", c=4, q=NQ),
                                         dwb_sb[:, 4 * i:4 * i + 4].unsqueeze(1).unsqueeze(3).to_broadcast(c4),
                                         ALU.add))
                link(v.tensor_tensor(chm, chm, spm, ALU.mult))
                v.tensor_tensor(chm_v, chm_v, x1.rearrange("p (q w) c -> p q c w", q=NQ), ALU.mult)\
                    .then_inc(s_gate, 1)
                dve.wait_ge(s_b2, b + 1)
                for q in range(NQ):
                    for f in range(2):
                        dve.wait_ge(s_proj, b * 2 * NQ + 2 * q + f + 1)
                        dst = toks[:, ds(b, 1), :].rearrange("p b (c w) -> p (b c) w", c=C)
                        dst = dst[:, f * TOK // 2:(f + 1) * TOK // 2, q * WQ:(q + 1) * WQ]
                        v.tensor_tensor(dst, dst, bank[4 + f][:, 0:TOK // 2 * WQ].rearrange("p (c w) -> p c w", w=WQ),
                                        ALU.add).then_inc(s_add, 1)
                chain.leave(NB)


def kernel(**inputs):
    import numpy as np
    import concourse.bacc as bacc
    from concourse.bass_utils import run_bass_kernel_spmd as run

    nc = bacc.Bacc("TRN2", target_bir_lowering=False, num_devices=1)
    a = {k: np.asarray(t) for k, t in inputs.items()}
    half = np.concatenate([np.arange(C) // 3, np.full(HALF - C, -1), np.arange(C) // 3])
    flat_group = np.arange(128) // 8
    scans = [a[f"L{n}_conv_{d}_w"] for n in (1, 2) for d in ("down", "right", "left")]
    biases = [a[f"L{n}_conv_{d}_b"] for n in (1, 2) for d in ("down", "right", "left")]
    dw = a["L0_conv_dw_w"].reshape(3 * C, 9)
    arrays = {
        "x": a["x"],
        "qkv_t": a["L0_conv_qkv_w"].reshape(3 * C, C).T,
        "v_w": a["L0_conv_qkv_w"].reshape(3 * C, C)[2 * C:],
        "dw_t": dw.T.reshape(-1),
        "dw_v": dw[2 * C:],
        "proj_t": a["L0_conv_proj_w"].reshape(C, C).T,
        "temp": a["L0_conv_temperature"].reshape(1),
        "scan_w": np.stack([w.transpose(1, 2, 0) for w in scans]),
        "scan_b": np.stack(biases, axis=1),
        "w1": a["L3_conv_W1"], "b1": a["L3_conv_b1"].reshape(1, HID),
        "gamma": a["L3_conv_gamma"], "beta": a["L3_conv_beta"],
        "gdw": a["L3_conv_dw_w"].reshape(-1), "gdw_b": a["L3_conv_dw_b"],
        "gpw_t": a["L3_conv_pw_w"].reshape(G, G).T, "gpw_b": a["L3_conv_pw_b"],
        "w2": a["L3_conv_W2"], "b2": a["L3_conv_b2"],
        "ident_c": np.eye(128, 130, 1, dtype=np.float32),
        "group_half_c": ((half[:, None] == half[None]) & (half[:, None] >= 0)).astype(np.float32) / np.float32(6),
        "group_flat_c": (flat_group[:, None] == flat_group[None]).astype(np.float32) / np.float32(8),
    }
    arrays = {k: np.ascontiguousarray(t) for k, t in arrays.items()}
    aps = {k: nc.dram_tensor(f"in_{k}", t.shape, F32, kind="ExternalInput").ap() for k, t in arrays.items()}
    saved = [nc.dram_tensor(f"saved{i}", (P, COLS), F32).ap() for i in range(2)]
    flat = nc.dram_tensor("flat_rows", (NB, C * H * W), F32).ap()
    out = nc.dram_tensor("out_0", (NB, C, H, W), F32, kind="ExternalOutput").ap()
    build(nc, saved=saved, flat=flat, out=out, **aps)
    r = run(nc, [{f"in_{k}": t for k, t in arrays.items()}], core_ids=[0])
    return r.results[0]["out_0"]
```

```python
from contextlib import ExitStack

import concourse.bass as bass
from concourse import mybir

ALU = mybir.AluOpType
ACT = mybir.ActivationFunctionType
AX = mybir.AxisListType.X
F32 = mybir.dt.float32
ds = bass.ds

NB, C, H, W = 4, 48, 128, 128
HALF = 64
P = HALF + C
LO, HI = slice(0, C), slice(HALF, P)
K2, J2 = H // 2, W // 2
SUB = K2 * J2
IMG = 2 * SUB
COLS = NB * IMG
BN = 512
NSTAT = IMG // BN
GN_EPS = 1e-5
NORM_FLOOR_SQ = 1e-24

IN_ROWS = 16
IN_COLS = IN_ROWS * W
LOADS = H // IN_ROWS

BLK = 8
NBLK = K2 // BLK
ZSUB = (BLK + 2) * J2
PAIRS = 4 * NBLK
QK = 2 * C

STEPS = H - 1
PASSES = 4
CHUNK = 2048
NCH = COLS // CHUNK

TOK = 48
HID = 16
G = HID // 2
TCOLS = H * W * C // 128
TPAIRS = TCOLS // (2 * TOK)
GROUPS = TPAIRS // 4
GW = W + 2
WQ = 16
NQ = W // WQ
LN_EPS = 1e-5

TWO = 2


X_STATS = 1 + NB * LOADS
SLOTS = (0, 2, 5, 8, 11, 14)
N_CONST = 17 + 2 * G
N_SCAN_DMA = 2 + 6 * 10
N_BAND = G * 3 * 5
ATT_LINKS = 8
MLP_LINKS = 12


class Chain:

    def __init__(self, eng, sem):
        self.eng, self.sem, self.links, self.turn = eng, sem, 0, None

    def enter(self, turn, rate):
        self.turn, self.rate, self.first = turn, rate, self.links

    def leave(self, turns):
        assert self.links == self.first + self.rate, (self.links - self.first, self.rate)
        self.links, self.turn = self.first + turns * self.rate, None

    def link(self, ins):
        ins.then_inc(self.sem, 1)
        self.links += 1
        self.eng.wait_ge(self.sem, self.links if self.turn is None else self.turn * self.rate + self.links)


def build(nc, x, qkv_t, v_w, dw_t, dw_v, proj_t, temp, scan_w, scan_b,
          w1, b1, gamma, beta, gdw, gdw_b, gpw_t, gpw_b, w2, b2,
          ident_c, group_half_c, group_flat_c, saved, flat, out):
    with ExitStack() as ctx:
        def sb(name, shape):
            return ctx.enter_context(nc.sbuf_tensor(name, shape, F32))

        def sem(name):
            return ctx.enter_context(nc.semaphore(name))

        image = sb("image", [128, COLS])
        identp = sb("identp", [128, 130])
        group_half = sb("group_half", [P, P])
        group_flat = sb("group_flat", [128, 128])
        stats = sb("stats", [128, NB * NSTAT * 6])
        mean_var = sb("mean_var", [128, NB, 2])
        gn_mean = sb("gn_mean", [128, NB])
        gn_off = sb("gn_off", [128, NB])
        gn_sq = sb("gn_sq", [128, NB])
        gn_var = sb("gn_var", [128, NB])
        gn_std = sb("gn_std", [128, NB])
        gn_scale = sb("gn_scale", [128, NB])
        gn_shift = sb("gn_shift", [128, NB])
        scan_bias = sb("scan_bias", [P, 6])
        scan_wt = sb("scan_wt", [P, 6, 3, P])
        band = sb("band", [128, 3 * G, 128])
        gates = sb("gates", [128, 8 * G + 9 * G])
        work = sb("work", [128, 13300])
        ident = identp[:, 1:129]
        image5 = image[0:P, :].rearrange("p (b s k j) -> p b s k j", b=NB, s=2, k=K2)

        def cut(at, dims, parts=128):
            n = 1
            for m in dims:
                n *= m
            v = work[0:parts, at:at + n]
            if len(dims) == 2:
                v = v.rearrange("p (a b) -> p a b", a=dims[0])
            elif len(dims) == 3:
                v = v.rearrange("p (a b c) -> p a b c", a=dims[0], b=dims[1])
            return v

        rows_in = [band[0:P, :, :].rearrange("p a b -> p (a b)")[:, 0:IN_COLS], cut(13300 - IN_COLS, [IN_COLS], P)]
        blk_z = [cut(i * 2 * ZSUB, [2 * ZSUB], P) for i in range(2)]
        blk_n = [cut((2 + i) * 2 * ZSUB, [2 * ZSUB], P) for i in range(2)]
        at = 8 * ZSUB
        qkv_sb = cut(at, [3 * C], P)
        at += 3 * C
        qk_w = [cut(at + i * 6 * QK, [3, 2, QK], P) for i in range(2)]
        at += 12 * QK
        v_taps = cut(at, [9, P], C)
        at += 9 * P
        out_w = [cut(at + i * 3 * P, [3, P], P) for i in range(2)]
        at += 6 * P
        dw_sb = cut(at, [9, 3 * C], P)
        at += 27 * C
        gram = cut(at, [QK], QK)
        gram_d = cut(at + QK, [QK], QK)
        at += 2 * QK
        v_sb, proj_sb, logits, probs, probs_n, mix_t = (cut(at + i * C, [C], C) for i in range(6))
        ones = cut(at + 6 * C, [C], QK)
        at += 7 * C
        dwv_sb, temp_sb, col = cut(at, [9], C), cut(at + 9, [1], C), cut(at + 10, [8], QK)
        at += 18
        zero_row = cut(at, [J2], P)
        at += J2
        qk_sb = [cut(at + i * 4 * C * 2, [4 * C * 2]) for i in range(2)]
        at += 16 * C
        assert at <= 13300 - IN_COLS, at
        kept = [cut(i * CHUNK, [CHUNK], P) for i in range(2)]
        nat = [cut((2 + i) * CHUNK, [CHUNK], P) for i in range(2)]
        swap_tmp = cut(4 * CHUNK, [NB, 64], P)
        toks = image[:, 0:NB * TCOLS].rearrange("p (b n) -> p b n", b=NB)
        xn = image[:, NB * TCOLS:NB * TCOLS + TCOLS]
        hid = image[:, COLS - 2048:COLS]
        x_t = [cut(i * 512, [512]) for i in range(2)]
        at = 1024
        w1_sb = cut(at, [2 * HID], 97)
        at += 2 * HID
        pw_k = cut(at, [G, WQ])
        at += 128
        w2_k = cut(at, [TOK, WQ])
        at += TOK * WQ
        n_pad = cut(at, [G, GW])
        at += G * GW
        dev, dev2, n_t, g_t, chm, spm = (cut(at + i * 1024, [1024]) for i in range(6))
        at += 6 * 1024
        s1, s2, s3, s4, s5 = (cut(at + i * 128, [128]) for i in range(5))
        at += 5 * 128
        assert at <= 13300, at
        gdw_sb = gates[:, 0:72]
        gam_sb, bet_sb, dwb_sb, pwb_sb, pwr_sb = (gates[:, 72 + 8 * i:80 + 8 * i] for i in range(5))
        band_tmp = [sb(f"band_tmp{i}", [128, 128])[:, :] for i in range(2)]
        w2r_sb = sb("w2r_sb", [128, TOK])
        b2_sb = sb("b2_sb", [128, TOK])

        bank = [ctx.enter_context(nc.psum_tensor(f"bank{i}", [128, 512], F32)) for i in range(8)]
        bank_gram, bank_small, bank_wt = bank[2], bank[3], bank[4]
        bank_out = bank[5:7]
        bank_gn = bank[7]

        s_const = sem("s_const")
        s_gate_zero = sem("s_gate_zero")
        s_gate_const = sem("s_gate_const")
        s_pool = sem("s_pool")
        s_gap = sem("s_gap")
        s_zero = sem("s_zero")
        s_border = sem("s_border")
        s_load = [sem(f"s_load{i}") for i in range(2)]
        s_split = sem("s_split")
        s_stat = sem("s_stat")
        s_dve = sem("s_dve")
        s_gn_v = sem("s_gn_v")
        s_gn_mm = sem("s_gn_mm")
        s_gn_std = sem("s_gn_std")
        s_gn = sem("s_gn")
        s_wts = sem("s_wts")
        s_stage = sem("s_stage")
        s_qk = sem("s_qk")
        s_qk_sb = sem("s_qk_sb")
        s_gram = sem("s_gram")
        s_sm_v = sem("s_sm_v")
        s_sm_a = sem("s_sm_a")
        s_sm_t = sem("s_sm_t")
        s_outw = sem("s_outw")
        s_conv = sem("s_conv")
        s_x1 = sem("s_x1")
        s_save = sem("s_save")
        s_scan_w = sem("s_scan_w")
        s_scan_c = sem("s_scan_c")
        s_prod = [sem(f"s_prod{g}") for g in range(2)]
        s_state = [sem(f"s_state{g}") for g in range(2)]
        s_swap = sem("s_swap")
        s_back = [sem(f"s_back{i}") for i in range(2)]
        s_res = sem("s_res")
        s_flat = [sem(f"s_flat{i}") for i in range(2)]
        s_tok = [sem(f"s_tok{b}") for b in range(NB)]
        s_band = sem("s_band")
        s_xn = sem("s_xn")
        s_xt_p = sem("s_xt_p")
        s_xt_a = sem("s_xt_a")
        s_xt_v = sem("s_xt_v")
        s_hid = sem("s_hid")
        s_gelu = sem("s_gelu")
        s_ln = sem("s_ln")
        s_ln_a = sem("s_ln_a")
        s_gt_p = sem("s_gt_p")
        s_gt_a = sem("s_gt_a")
        s_gate = sem("s_gate")
        s_proj = sem("s_proj")
        s_add = sem("s_add")
        s_res3 = sem("s_res3")
        s_b2 = sem("s_b2")
        s_out = sem("s_out")

        block = ctx.enter_context(nc.Block())

        def own_wait(eng, semaphore, value):
            value = eng.compute_val(value)
            eng.wait_ge(s_gap, 2)
            eng.wait_ge(semaphore, value)

        SCANS = [(True, False, 0, False), (False, False, 0, True), (True, True, 1, False), (False, True, 2, False)]

        def line(g, along_w, at):
            b = slice(2 * g, 2 * g + 2)
            return image5[:, b, at % 2, :, at // 2] if along_w else image5[:, b, at % 2, at // 2, :]

        def step_at(forward, n):
            return (n, n + 1) if forward else (STEPS - n, STEPS - 1 - n)

        TAPS = [(LO, 0, 0, 1), (LO, 1, 0, 0), (HI, 0, 0, 2), (HI, 1, 0, 1), (LO, 1, 1, 2), (HI, 0, 1, 0)]

        def conv_rows(sub):
            return [(0, 1, -1), (1, 0, 0), (2, 1, 0)] if sub == 0 else [(0, 0, 0), (1, 1, 0), (2, 0, 1)]

        @block.sync
        def _(sp):
            rows = x.rearrange("b c h w -> b c (h w)")
            sp.wait_ge(s_gap, 2)
            with sp.Fori(0, NB) as b:
                with sp.Fori(0, LOADS // 2) as q:
                    for m in range(2):
                        sp.wait_ge(s_split, b * LOADS + q * 2 + m + 1)
                        src = rows[ds(b, 1), :, ds(q * 2 * IN_COLS + m * IN_COLS, IN_COLS)]
                        sp.dma_start(rows_in[m][LO, :], src.rearrange("b c n -> (b c) n")).then_inc(s_load[m], 16)
                        src = rows[ds(b, 1), :, ds(q * 2 * IN_COLS + m * IN_COLS + 1, IN_COLS - 1)]
                        sp.dma_start(rows_in[m][HI, 0:IN_COLS - 1],
                                     src.rearrange("b c n -> (b c) n")).then_inc(s_load[m], 16)
            for b in range(NB):
                sp.wait_ge(s_x1, TWO + (b + 1) * 2 * NBLK)
                sp.dma_start(saved[0][:, b * IMG:(b + 1) * IMG],
                             image[0:P, b * IMG:(b + 1) * IMG]).then_inc(s_save, 16)
            sp.wait_ge(s_save, 16 * NB)
            with sp.Fori(0, NCH // 2) as t:
                for m in range(2):
                    sp.wait_ge(s_res, 2 * t + m + 1)
                    sp.dma_start(kept[m], saved[0][:, ds(t * 2 * CHUNK + m * CHUNK, CHUNK)]).then_inc(s_back[m], 16)
            sp.wait_ge(s_res, TWO + NCH)
            for b in range(NB):
                sp.dma_start(saved[1][:, b * IMG:(b + 1) * IMG],
                             image[0:P, b * IMG:(b + 1) * IMG]).then_inc(s_save, 16)
            sp.wait_ge(s_save, 32 * NB)
            kept_rows = saved[1].rearrange("p (b s n) -> p b s n", b=NB, s=2)
            with sp.Fori(0, NB // 2) as bp:
                with sp.Fori(0, NBLK // 2) as q:
                    for m in range(2):
                        sp.wait_ge(s_res, bp * NBLK + 2 * q + (NCH + m + 1))
                        src = kept_rows[:, ds(2 * bp, 2), :, ds(q * 2 * BN + m * BN, BN)]
                        sp.dma_start(kept[m].rearrange("p (a n) -> p a n", a=4),
                                     src.rearrange("p b s n -> p (b s) n")).then_inc(s_back[m], 16)
            for m in range(2):
                sp.wait_ge(s_flat[m], 32 + 32 * NCH // 2)
            for b in range(NB):
                sp.dma_start(toks[:, b, :], flat[b].rearrange("(p n) -> p n", p=128)).then_inc(s_tok[b], 16)
            grid = flat.rearrange("b (c h w) -> b h c w", c=C, h=H)
            grid_out = out.rearrange("b c h w -> b h c w")
            for b in range(NB):
                sp.wait_ge(s_xn, b + 1)
                dst = toks[:, b, :].rearrange("p (c w) -> p c w", c=C)
                sp.dma_start(dst, grid[b]).then_inc(s_res3, 16)
                sp.wait_ge(s_add, TWO + (b + 1) * 2 * NQ)
                sp.dma_start(grid_out[b], dst).then_inc(s_out, 16)
            sp.wait_ge(s_out, 16 * NB)

        @block.gpsimd
        def _(pool):
            pool_chain = Chain(pool, s_pool)

            def ms(v, value):
                pool_chain.link(nc.gpsimd.memset(v, value))

            for s, n in ((s_split, TWO), (s_qk_sb, TWO), (s_gram, TWO), (s_x1, TWO), (s_res, TWO),
                         (s_conv, 2 * NBLK), (s_qk, 4), (s_swap, 1), (s_add, TWO), (s_flat[0], 32), (s_flat[1], 32)):
                pool.sem_inc(s, n)
            for m in range(2):
                nc.gpsimd.memset(rows_in[m][32:HALF, :], 0.0).then_inc(s_gap, 1)
            pool.wait_ge(s_gap, 2)
            for m in range(2):
                ms(blk_n[m], 0.0)
                nc.gpsimd.memset(blk_z[m], 0.0).then_inc(s_border, 1)
                pool.wait_ge(s_border, m + 1)
            ms(ones, 1.0)
            ms(zero_row, 0.0)
            ms(qk_w[0], 0.0)
            ms(qk_w[1], 0.0)
            ms(v_taps, 0.0)
            ms(out_w[0], 0.0)
            nc.gpsimd.memset(out_w[1], 0.0).then_inc(s_zero, 1)
            pool.wait_ge(s_zero, 1)
            ms(scan_bias[:, :], 0.0)
            nc.gpsimd.memset(scan_wt[:, :, :, :], 0.0).then_inc(s_scan_w, 1)
            pool.wait_ge(s_scan_w, 1)
            pool.wait_ge(s_split, TWO + NB * LOADS)
            pool.wait_ge(s_const, 16 * N_CONST)
            n = 0
            for c in range(G):
                for dx in range(3):
                    for dy in range(3):
                        tap = gdw_sb[:, c * 9 + dy * 3 + dx:c * 9 + dy * 3 + dx + 1]
                        if dy:
                            pool.wait_ge(s_band, n)
                            ins = nc.gpsimd.tensor_scalar(band_tmp[dy - 1], identp[:, dy:dy + 128], tap, None, ALU.mult)
                            ins.then_inc(s_band, 1)
                            pool.wait_ge(s_band, n + 1)
                            nc.gpsimd.tensor_tensor(band[:, c * 3 + dx, :], band[:, c * 3 + dx, :], band_tmp[dy - 1],
                                                    ALU.add).then_inc(s_band, 1)
                            n += 2
                        else:
                            nc.gpsimd.tensor_scalar(band[:, c * 3 + dx, :], identp[:, 0:128], tap, None,
                                                    ALU.mult).then_inc(s_band, 1)
                            n += 1
            assert n == N_BAND
            pool.wait_ge(s_flat[0], 32 + 32 * NCH // 2)
            pool.wait_ge(s_flat[1], 32 + 32 * NCH // 2)
            ms(w1_sb, 0.0)
            ms(n_pad, 0.0)
            for m in range(2):
                nc.gpsimd.memset(x_t[m][96:128, :], 1.0).then_inc(s_gate_zero, 1)
            pool.wait_ge(s_gate_zero, 2)
            pool.dma_start(w1_sb[0:TOK, 0:HID], w1).then_inc(s_gate_const, 16)
            pool.dma_start(w1_sb[TOK:2 * TOK, HID:2 * HID], w1).then_inc(s_gate_const, 16)
            pool.dma_start(w1_sb[96:97, 0:HID], b1).then_inc(s_gate_const, 16)
            pool.dma_start(w1_sb[96:97, HID:2 * HID], b1).then_inc(s_gate_const, 16)
            pool.wait_ge(s_band, N_BAND)
            nc.gpsimd.tensor_copy(s1[:, 0:WQ], ident[:, 0:WQ]).then_inc(s_band, 1)
            n = N_BAND + 1
            for c in range(1, G):
                pool.wait_ge(s_band, n)
                nc.gpsimd.tensor_tensor(s1[:, 0:WQ], s1[:, 0:WQ], ident[:, c * WQ:(c + 1) * WQ],
                                        ALU.add).then_inc(s_band, 1)
                n += 1
            pool.wait_ge(s_band, n)
            for o in range(G):
                nc.gpsimd.tensor_scalar(pw_k[:, o, :], s1[:, 0:WQ], pwr_sb[:, o:o + 1], None, ALU.mult)
            for e in range(TOK):
                last = nc.gpsimd.tensor_scalar(w2_k[:, e, :], s1[:, 0:WQ], w2r_sb[:, e:e + 1], None, ALU.mult)
            last.then_inc(s_band, 1)
            with pool.Fori(0, NB) as b:
                pool.wait_ge(s_res3, 16 * b + 16)
                v = toks[:, ds(b, 1), :].rearrange("p b (c w) -> p (b c) w", c=C)
                nc.gpsimd.tensor_tensor(v, v, b2_sb[:, :].unsqueeze(2).to_broadcast([128, C, W]),
                                        ALU.add).then_inc(s_b2, 1)

        @block.scalar
        def _(act):
            consts = [(identp[:, :], ident_c), (group_half[:, :], group_half_c), (group_flat[:, :], group_flat_c),
                      (qkv_sb[LO, :], qkv_t), (qkv_sb[HI, :], qkv_t),
                      (dw_sb[LO].rearrange("p a b -> p (a b)"), dw_t.partition_broadcast(C)),
                      (dw_sb[HI].rearrange("p a b -> p (a b)"), dw_t.partition_broadcast(C)),
                      (v_sb, v_w), (dwv_sb, dw_v), (proj_sb, proj_t), (temp_sb, temp.partition_broadcast(C)),
                      (gdw_sb, gdw.partition_broadcast(128)), (gam_sb, gamma.partition_broadcast(128)),
                      (bet_sb, beta.partition_broadcast(128)), (dwb_sb, gdw_b.partition_broadcast(128)),
                      (pwb_sb, gpw_b.partition_broadcast(128)), (b2_sb[:, :], b2.partition_broadcast(128))]
            for c in range(G):
                consts.append((pwr_sb[c * WQ:(c + 1) * WQ, :], gpw_t[c].partition_broadcast(WQ)))
                consts.append((w2r_sb[c * WQ:(c + 1) * WQ, :], w2[c].partition_broadcast(WQ)))
            assert len(consts) == N_CONST
            for dst, src in consts:
                act.dma_start(dst, src).then_inc(s_const, 16)

            def split(c):
                m, b, k0 = c % 2, c // LOADS, c % LOADS * BLK
                act.wait_ge(s_load[m], 32 * (c // 2 + 1))
                src = rows_in[m].rearrange("p (k s j q) -> p s k j q", k=BLK, s=2, j=J2)[:, :, :, :, 0]
                nc.scalar.copy(image5[:, b, :, k0:k0 + BLK, :], src).then_inc(s_split, 1)

            for c in range(LOADS):
                split(c)

            def deviation(r, c0=0, c1=NB):
                act.wait_ge(s_gn_v, 3 * r + 3)
                nc.scalar.activation(gn_std[:, c0:c1], gn_var[:, c0:c1], ACT.Sqrt).then_inc(s_gn_std, 1)

            deviation(0, 0, 1)

            def stage(b, n, m):
                for sub in range(2):
                    kk0, rows = 1 - sub, BLK + 1
                    top = isinstance(n, int) and n == 0 and sub == 1
                    bottom = isinstance(n, int) and n == NBLK - 1 and sub == 0
                    if top or bottom:
                        o = sub * ZSUB + (0 if top else BLK + 1) * J2
                        nc.scalar.copy(blk_z[m][:, o:o + J2], zero_row)
                        nc.scalar.copy(blk_n[m][:, o:o + J2], zero_row)
                        rows = BLK
                        kk0 += top
                    for buf, part, d, e in ((blk_z, slice(0, P), (0, J2), (0, J2)),
                                            (blk_n, LO, (0, J2 - 1), (1, J2)), (blk_n, HI, (1, J2), (0, J2 - 1))):
                        dst = buf[m][part, sub * ZSUB + kk0 * J2:sub * ZSUB + (kk0 + rows) * J2]
                        src = image5[part, ds(b, 1), sub, ds(n * BLK - 1 + kk0, rows), e[0]:e[1]]
                        last = nc.scalar.activation(dst.rearrange("p (k j) -> p k j", j=J2)[:, :, d[0]:d[1]],
                                                    src.rearrange("p b k j -> p (b k) j"), ACT.Identity,
                                                    bias=gn_shift[part, ds(b, 1)], scale=gn_scale[part, ds(b, 1)])
                last.then_inc(s_stage, 1)

            def norms(b):
                act.wait_ge(s_sm_v, 5 * b + 1)
                nc.scalar.activation(col[:, 2:3], col[:, 1:2], ACT.Sqrt).then_inc(s_sm_a, 1)

            def exponentials(b):
                act.wait_ge(s_sm_v, 5 * b + 3)
                nc.scalar.activation(probs, logits, ACT.Exp, bias=col[0:C, 5:6],
                                     accum_out=col[0:C, 6:7]).then_inc(s_sm_a, 1)

            act.wait_ge(s_gn, 1)
            act.wait_ge(s_border, 2)
            for n in range(NBLK):
                if n >= 2:
                    act.wait_ge(s_qk, 4 * n)
                stage(0, n, n % 2)
                for c in range(3):
                    split(LOADS + 3 * n + c)
            deviation(1, 1, NB)
            act.wait_ge(s_gn, 2)
            with act.Fori(0, NB - 1) as b:
                for n in range(2):
                    own_wait(act, s_conv, b * 2 * NBLK + (2 * NBLK - 2 + 2 * n))
                    own_wait(act, s_qk, b * PAIRS + (PAIRS + 4 * n))
                    stage(b + 1, n, n)
                norms(b)
                own_wait(act, s_qk, b * PAIRS + (PAIRS + 8))
                stage(b + 1, 2, 0)
                exponentials(b)
                own_wait(act, s_qk, b * PAIRS + (PAIRS + 12))
                stage(b + 1, 3, 1)
                with act.Fori(2, NBLK // 2 - 1) as h:
                    for u in range(2):
                        own_wait(act, s_qk, b * PAIRS + 8 * h + (PAIRS + 4 * u))
                        stage(b + 1, 2 * h + u, u)
                for n in range(NBLK - 2, NBLK):
                    own_wait(act, s_qk, b * PAIRS + (PAIRS + 4 * n))
                    stage(b + 1, n, n % 2)
                for n in range(2):
                    own_wait(act, s_qk, b * PAIRS + (2 * PAIRS + 4 * n))
                    stage(b, n, n)
                with act.Fori(1, NBLK // 2 - 1) as h:
                    for u in range(2):
                        own_wait(act, s_conv, b * 2 * NBLK + 4 * h + (2 * NBLK + 2 * u - 2))
                        stage(b, 2 * h + u, u)
                for n in range(NBLK - 2, NBLK):
                    own_wait(act, s_conv, b * 2 * NBLK + (2 * NBLK + 2 * n - 2))
                    stage(b, n, n % 2)
            norms(NB - 1)
            exponentials(NB - 1)
            for n in range(NBLK):
                act.wait_ge(s_conv, (NB - 1 if n < 2 else NB) * 2 * NBLK + 2 * n - 2)
                stage(NB - 1, n, n % 2)

            act.wait_ge(s_scan_w, 1)
            n_dma = 0
            for half in (LO, HI):
                act.dma_start(scan_bias[half, :], scan_b).then_inc(s_scan_c, 16)
                n_dma += 1
            for t in range(6):
                for qi, rows in enumerate((LO, HI)):
                    for qo, cols in enumerate((LO, HI)):
                        shifts = [m for m in (-1, 0, 1) if 0 <= 2 * m + qi - qo + 2 < 5]
                        for m in shifts:
                            act.dma_start(scan_wt[rows, t, m + 1, cols],
                                          scan_w[t][:, 2 * m + qi - qo + 2, :]).then_inc(s_scan_c, 16)
                            n_dma += 1
            assert n_dma == N_SCAN_DMA

            def normalise(layer):
                act.wait_ge(s_gn, layer + 3)
                act.wait_ge(s_save, (layer + 1) * 16 * NB)
                for b in (2, 3):
                    v = image[0:P, b * IMG:(b + 1) * IMG]
                    last = nc.scalar.activation(v, v, ACT.Identity, bias=gn_shift[0:P, b:b + 1],
                                                scale=gn_scale[0:P, b:b + 1])
                last.then_inc(s_state[1], 1)

            def exchange(along_w, i, n):
                def part(rows, s):
                    v = image5[rows, :, s, :, ds(i, 1)] if along_w else image5[rows, :, s, ds(i, 1), :]
                    return v.rearrange("p b k j -> p b (k j)")
                own_wait(act, s_swap, n + 1)
                nc.scalar.copy(swap_tmp[HI], part(LO, 1)).then_inc(s_swap, 1)
                own_wait(act, s_swap, n + 2)
                nc.scalar.copy(part(LO, 1), part(HI, 0)).then_inc(s_swap, 1)
                own_wait(act, s_swap, n + 3)
                nc.scalar.copy(part(HI, 0), swap_tmp[HI]).then_inc(s_swap, 1)

            for layer in range(2):
                deviation(layer + 2)
                normalise(layer)
                for g in range(2):
                    act.wait_ge(s_prod[g], layer * PASSES * STEPS + 1)
                n0 = layer * 2 * 3 * K2
                prod0 = layer * PASSES * STEPS + STEPS
                with act.Fori(0, K2 - 2) as i:
                    for g in range(2):
                        own_wait(act, s_prod[g], 2 * i + (prod0 + 4))
                    exchange(False, K2 - 2 - i, 3 * i + n0)
                for g in range(2):
                    act.wait_ge(s_state[g], layer * (PASSES * STEPS + 1) + 1 + 2 * STEPS)
                exchange(False, 0, n0 + 3 * (K2 - 2))
                exchange(False, K2 - 1, n0 + 3 * (K2 - 1))
                n0 += 3 * K2
                prod0 += 2 * STEPS
                with act.Fori(0, K2 - 1) as i:
                    for g in range(2):
                        own_wait(act, s_prod[g], 2 * i + (prod0 + 2))
                    exchange(True, K2 - 1 - i, 3 * i + n0)
                for g in range(2):
                    act.wait_ge(s_state[g], (layer + 1) * (PASSES * STEPS + 1))
                exchange(True, 0, n0 + 3 * (K2 - 1))
            rows = flat.rearrange("b (c n) -> b c n", c=C)
            with act.Fori(0, NB // 2) as bp:
                with act.Fori(0, NBLK // 2) as q:
                    for m in range(2):
                        act.wait_ge(s_res, bp * NBLK + 2 * q + (TWO + NCH + m + 1))
                        for i, part in enumerate((LO, HI)):
                            dst = rows[ds(2 * bp + i, 1), :, ds(q * 2 * CHUNK + m * CHUNK, CHUNK)]
                            act.dma_start(dst.rearrange("b c n -> (b c) n"), nat[m][part, :]).then_inc(s_flat[m], 16)
            deviation(4)

            with act.Fori(0, NB) as b:
                for g in range(0, GROUPS, 2):
                    act.wait_ge(s_xt_p, b * GROUPS + g + 1)
                    nc.scalar.copy(x_t[0][0:96, :], bank[0][0:96, :]).then_inc(s_xt_a, 1)
                for i in range(4):
                    act.wait_ge(s_hid, b * GROUPS + 4 * (i + 1))
                    nc.scalar.activation(hid[:, i * 512:(i + 1) * 512], bank[2 + i][:, :], ACT.Gelu).then_inc(s_gelu, 1)
                act.wait_ge(s_gelu, b * 5 + 4)
                nc.scalar.activation(hid, hid, ACT.Gelu).then_inc(s_gelu, 1)
                act.wait_ge(s_ln, b * 2 + 1)
                nc.scalar.activation(s4, s3, ACT.Sqrt).then_inc(s_ln_a, 1)
                act.wait_ge(s_ln, b * 2 + 2)
                act.wait_ge(s_gate_zero, 2)
                nc.scalar.copy(n_pad[:, :, 1:1 + W].rearrange("p c (q w) -> p q c w", q=NQ),
                               spm.rearrange("p (q c w) -> p q c w", q=NQ, c=G)).then_inc(s_ln_a, 1)
                for first, dst in ((1, n_t), (7, g_t)):
                    for i in range(2):
                        act.wait_ge(s_gt_p, b * 8 + first + i)
                        nc.scalar.copy(dst[:, i * 512:(i + 1) * 512], bank[i][:, :]).then_inc(s_gt_a, 1)

        @block.tensor
        def _(pe):
            mm = nc.tensor.matmul

            def group_sums(r, parts, groups, c0=0, c1=NB):
                pe.wait_ge(s_gn_v, 3 * r + 1)
                mm(bank_gn[0:parts, c0:c1], groups, mean_var[0:parts, c0:c1, 0], start=True, stop=True).then_inc(s_gn_mm, 1)
                pe.wait_ge(s_gn_v, 3 * r + 2)
                mm(bank_gn[0:parts, NB + c0:NB + c1], groups, gn_sq[0:parts, c0:c1], start=True, stop=True).then_inc(s_gn_mm, 1)

            pe.wait_ge(s_const, 16 * N_CONST)
            group_sums(0, P, group_half[:, :], 0, 1)
            pe.wait_ge(s_wts, 1)

            def query_keys(stages, pairs, slots, gram_free):
                def conv_pair(i):
                    n, sub, kp = i // 4, (i // 2) % 2, 2 * (i % 2)
                    if i % 4 == 0:
                        pe.wait_ge(s_stage, stages + (n + 1))
                    pe.wait_ge(s_qk_sb, pairs + (i + 1))
                    for c in range(2):
                        dst = bank[i % 2][:, c * 2 * QK:(c + 1) * 2 * QK]
                        prods = [(buf, dy, s, dk) for buf in range(2) for dy, s, dk in conv_rows(sub)]
                        for t, (buf, dy, s, dk) in enumerate(prods):
                            o = s * ZSUB + (1 + 2 * (kp + c) + dk) * J2
                            last = mm(dst, (blk_z, blk_n)[buf][n % 2][:, o:o + 2 * J2],
                                      qk_w[buf][:, dy].rearrange("p a b -> p (a b)"),
                                      start=(t == 0), stop=(t == len(prods) - 1))
                    last.then_inc(s_qk, 1)

                def gram_pair(i):
                    pe.wait_ge(s_qk_sb, pairs + (i + 1 + TWO))
                    if i == 0:
                        gram_free()
                    for c in range(4):
                        v = qk_sb[i % 2][:, c * QK:(c + 1) * QK]
                        last = mm(bank_gram[0:QK, 0:QK], v, v, start=(i == 0 and c == 0),
                                  stop=(i == PAIRS - 1 and c == 3))
                    last.then_inc(s_gram, 1)

                for i in range(PAIRS + 1):
                    if i < PAIRS:
                        conv_pair(i)
                    if i:
                        gram_pair(i - 1)
                    if i in slots:
                        slots[i]()

            def key_norms(b):
                own_wait(pe, s_sm_v, 5 * b + 2)
                mm(bank_small[0:C, 0:C], ones, gram_d[:, C:QK], start=True, stop=True).then_inc(s_sm_t, 1)

            def mixing(b):
                own_wait(pe, s_sm_v, 5 * b + 4)
                mm(bank_small[0:C, 64:64 + C], probs_n, proj_sb, start=True, stop=True).then_inc(s_sm_t, 1)

            def tap_weights(b):
                pe.wait_ge(s_sm_v, 5 * b + 5)
                for t in range(9):
                    last = mm(bank_wt[0:P, t * C:(t + 1) * C], v_taps[:, t, :], mix_t, start=True, stop=True)
                last.then_inc(s_sm_t, 1)

            def output_conv(b, stages):
                pe.wait_ge(s_outw, b + 1)
                for n in range(NBLK):
                    pe.wait_ge(s_stage, stages + (n + 1))
                    for sub in range(2):
                        pe.wait_ge(s_x1, b * 2 * NBLK + (2 * n + sub + 1))
                        prods = [(buf, dy, s, dk) for buf in range(2) for dy, s, dk in conv_rows(sub)]
                        for t, (buf, dy, s, dk) in enumerate(prods):
                            o = s * ZSUB + (1 + dk) * J2
                            last = mm(bank_out[sub][0:P, :], out_w[buf][:, dy, :],
                                      (blk_z, blk_n)[buf][n % 2][:, o:o + BLK * J2],
                                      start=(t == 0), stop=(t == len(prods) - 1))
                        last.then_inc(s_conv, 1)

            query_keys(0, 0, {PAIRS - 2: lambda: group_sums(1, P, group_half[:, :], 1, NB)}, lambda: None)
            with pe.Fori(0, NB - 1) as b:
                query_keys(b * 2 * NBLK + NBLK, b * PAIRS + PAIRS,
                           {SLOTS[2] - 1: lambda: key_norms(b), SLOTS[4] - 1: lambda: mixing(b),
                            SLOTS[5] - 1: lambda: tap_weights(b)},
                           lambda: pe.wait_ge(s_sm_v, 5 * b + 1))
                output_conv(b, b * 2 * NBLK + 2 * NBLK)
            key_norms(NB - 1)
            mixing(NB - 1)
            tap_weights(NB - 1)
            output_conv(NB - 1, (2 * NB - 1) * NBLK)

            def step(layer, done, scan, n):
                forward, along_w, kind, _ = SCANS[scan]
                at, _ = step_at(forward, n)
                wt = scan_wt[:, 3 * layer + kind]
                for g in range(2):
                    pe.wait_ge(s_state[g], done + (layer * (PASSES * STEPS + 1) + 1))
                    src = line(g, along_w, at)
                    dst = bank[g][0:P, 0:2 * J2].rearrange("p (b j) -> p b j", b=2)
                    mm(dst, wt[:, 1], src, start=True, stop=False)
                    mm(dst[:, :, 1:J2], wt[:, 0], src[:, :, 0:J2 - 1], start=False, stop=False)
                    mm(dst[:, :, 0:J2 - 1], wt[:, 2], src[:, :, 1:J2], start=False, stop=True).then_inc(s_prod[g], 1)

            for layer in range(2):
                group_sums(layer + 2, P, group_half[:, :])
                if layer == 0:
                    pe.wait_ge(s_scan_c, 16 * N_SCAN_DMA)
                for scan in range(PASSES):
                    if scan == 2:
                        pe.wait_ge(s_swap, (2 * layer + 1) * 3 * K2 + 1)
                    for n in range(STEPS):
                        step(layer, scan * STEPS + n, scan, n)

            group_sums(4, 128, group_flat[:, :])
            pe.wait_ge(s_gate_const, 16 * 4)
            pe.wait_ge(s_band, N_BAND + G + 1)
            with pe.Fori(0, NB) as b:
                def turn_tokens(g):
                    if g >= 2:
                        pe.wait_ge((s_xt_a, s_xt_v)[g % 2], b * (GROUPS // 2) + g // 2)
                    for t in range(4):
                        o = (4 * g + t) * 2 * TOK
                        last = nc.tensor.transpose(bank[g % 2][0:2 * TOK, t * 128:(t + 1) * 128],
                                                   xn[:, o:o + 2 * TOK], ident)
                    last.then_inc(s_xt_p, 1)

                def hidden(g):
                    pe.wait_ge((s_xt_a, s_xt_v)[g % 2], b * (GROUPS // 2) + g // 2 + 1)
                    for t in range(4):
                        o = (g % 4 * 4 + t) * 2 * HID
                        last = mm(bank[2 + g // 4][:, o:o + 2 * HID], x_t[g % 2][0:97, t * 128:(t + 1) * 128],
                                  w1_sb, start=True, stop=True)
                    last.then_inc(s_hid, 1)

                pe.wait_ge(s_xn, b + 1)
                turn_tokens(0)
                pe.wait_ge(s_add, b * 2 * NQ + TWO)
                for g in range(1, GROUPS + 1):
                    if g < GROUPS:
                        turn_tokens(g)
                    hidden(g - 1)
                pe.wait_ge(s_ln, b * 2 + 2)
                for q in range(NQ):
                    last = nc.tensor.transpose(bank[q // 4][:, q % 4 * 128:(q % 4 + 1) * 128],
                                               spm[:, q * 128:(q + 1) * 128], ident)
                    if q % 4 == 3:
                        last.then_inc(s_gt_p, 1)
                pe.wait_ge(s_ln_a, b * 2 + 2)
                for c in range(G):
                    for dx in range(3):
                        last = mm(bank[6 + c // 4][:, c % 4 * 128:(c % 4 + 1) * 128], band[:, c * 3 + dx, :],
                                  n_pad[:, c, dx:dx + W], start=(dx == 0), stop=(dx == 2))
                    if c % 4 == 3:
                        last.then_inc(s_gt_p, 1)
                for q in range(NQ):
                    if q % 4 == 0:
                        pe.wait_ge(s_gt_a, b * 4 + q // 4 + 1)
                    last = mm(bank[2 + q // 4][:, q % 4 * 128:(q % 4 + 1) * 128], n_t[:, q * 128:(q + 1) * 128],
                              pw_k.rearrange("p a b -> p (a b)"), start=True, stop=True)
                    if q % 4 == 3:
                        last.then_inc(s_gt_p, 1)
                pe.wait_ge(s_gate, b + 1)
                for q in range(NQ):
                    last = nc.tensor.transpose(bank[q // 4][:, q % 4 * 128:(q % 4 + 1) * 128],
                                               chm[:, q * 128:(q + 1) * 128], ident)
                    if q % 4 == 3:
                        last.then_inc(s_gt_p, 1)
                for q in range(NQ):
                    if q % 4 == 0:
                        pe.wait_ge(s_gt_a, b * 4 + q // 4 + 3)
                    for f in range(2):
                        pe.wait_ge(s_add, b * 2 * NQ + 2 * q + f + 1)
                        mm(bank[4 + f][:, 0:TOK // 2 * WQ], g_t[:, q * 128:(q + 1) * 128],
                           w2_k[:, f * TOK // 2:(f + 1) * TOK // 2, :].rearrange("p a b -> p (a b)"),
                           start=True, stop=True).then_inc(s_proj, 1)

        @block.vector
        def _(dve):
            chain = Chain(dve, s_dve)
            link = chain.link
            v = nc.vector
            stat6 = stats[:, :].rearrange("p (b n) -> p b n", b=NB)

            def take_stats(parts, b, c, src):
                dst = stat6[0:parts, ds(b, 1), ds(c * 6, 6)].rearrange("p b n -> p (b n)")
                return v.bn_stats(dst, src)

            def group_norm(r, parts, n_stat, c0=0, c1=NB):
                p, c = slice(0, parts), slice(c0, c1)
                for b in range(c0, c1):
                    last = v.bn_aggr(mean_var[p, b, :], stat6[p, b, 0:6 * n_stat])
                last.then_inc(s_gn_v, 1)
                dve.wait_ge(s_gn_mm, 2 * r + 1)
                link(v.tensor_copy(gn_mean[p, c], bank_gn[p, c]))
                link(v.tensor_tensor(gn_off[p, c], mean_var[p, c, 0], gn_mean[p, c], ALU.subtract))
                link(v.tensor_tensor(gn_sq[p, c], gn_off[p, c], gn_off[p, c], ALU.mult))
                v.tensor_tensor(gn_sq[p, c], gn_sq[p, c], mean_var[p, c, 1], ALU.add).then_inc(s_gn_v, 1)
                dve.wait_ge(s_gn_mm, 2 * r + 2)
                v.tensor_scalar(gn_var[p, c], bank_gn[p, NB + c0:NB + c1], GN_EPS, None, ALU.add).then_inc(s_gn_v, 1)
                dve.wait_ge(s_gn_std, r + 1)
                link(v.reciprocal(gn_scale[p, c], gn_std[p, c]))
                v.scalar_tensor_tensor(out=gn_shift[p, c], in0=gn_mean[p, c], scalar=-1.0, in1=gn_scale[p, c],
                                       op0=ALU.mult, op1=ALU.mult).then_inc(s_gn, 1)
                dve.wait_ge(s_gn, r + 1)

            v.memset(gn_std[:, :], 1.0)
            v.memset(gn_var[:, :], 1.0).then_inc(s_stat, 1)
            dve.wait_ge(s_const, 16 * N_CONST)
            dve.wait_ge(s_zero, 1)
            for rows, pos, buf, dx in TAPS:
                for dy in range(3):
                    v.tensor_tensor(qk_w[buf][rows, dy, pos, :], qkv_sb[rows, 0:QK], dw_sb[rows, dy * 3 + dx, 0:QK],
                                    ALU.mult)
            for t in range(9):
                for cols in (LO, HI):
                    last = v.tensor_scalar(v_taps[:, t, cols], v_sb, dwv_sb[:, t:t + 1], None, ALU.mult)
            last.then_inc(s_wts, 1)
            def x_stats(c):
                dve.wait_ge(s_split, c + 1 + TWO)
                for s in range(2):
                    at = c // LOADS * IMG + s * SUB + c % LOADS * BN
                    last = take_stats(P, c // LOADS, c % LOADS * 2 + s, image[0:P, at:at + BN])
                last.then_inc(s_stat, 1)

            for c in range(LOADS):
                x_stats(c)
            dve.wait_ge(s_stat, 1 + LOADS)
            group_norm(0, P, NSTAT, 0, 1)

            def take_pair(pairs, i):
                dve.wait_ge(s_qk, pairs + (i + 1 + 4))
                dve.wait_ge(s_gram, pairs + (i + 1))
                v.tensor_copy(qk_sb[i % 2], bank[i % 2][:, 0:4 * QK]).then_inc(s_qk_sb, 1)

            def softmax_step(b, t):
                if t == 0:
                    dve.wait_ge(s_gram, b * PAIRS + (PAIRS + TWO))
                    link(v.tensor_copy(gram, bank_gram[0:QK, 0:QK]))
                    link(v.tensor_tensor(gram_d, gram, ident[0:QK, 0:QK], ALU.mult))
                    link(v.tensor_reduce(col[:, 0:1], gram_d, AX, ALU.add))
                    v.tensor_scalar(col[:, 1:2], col[:, 0:1], NORM_FLOOR_SQ, None, ALU.max).then_inc(s_sm_v, 1)
                elif t == 1:
                    dve.wait_ge(s_sm_a, 2 * b + 1)
                    link(v.reciprocal(col[:, 3:4], col[:, 2:3]))
                    v.tensor_scalar(gram_d, ident[0:QK, 0:QK], col[:, 3:4], None, ALU.mult).then_inc(s_sm_v, 1)
                elif t == 2:
                    dve.wait_ge(s_sm_t, 3 * b + 1)
                    link(v.scalar_tensor_tensor(out=logits, in0=gram[0:C, C:QK], scalar=col[0:C, 3:4],
                                                in1=bank_small[0:C, 0:C], op0=ALU.mult, op1=ALU.mult))
                    link(v.tensor_scalar(logits, logits, temp_sb, None, ALU.mult))
                    link(v.tensor_reduce(col[0:C, 4:5], logits, AX, ALU.max))
                    v.tensor_scalar(col[0:C, 5:6], col[0:C, 4:5], -1.0, None, ALU.mult).then_inc(s_sm_v, 1)
                elif t == 3:
                    dve.wait_ge(s_sm_a, 2 * b + 2)
                    link(v.reciprocal(col[0:C, 7:8], col[0:C, 6:7]))
                    v.tensor_scalar(probs_n, probs, col[0:C, 7:8], None, ALU.mult).then_inc(s_sm_v, 1)
                elif t == 4:
                    dve.wait_ge(s_sm_t, 3 * b + 2)
                    v.tensor_copy(mix_t, bank_small[0:C, 64:64 + C]).then_inc(s_sm_v, 1)
                else:
                    dve.wait_ge(s_sm_t, 3 * b + 3)
                    taps = bank_wt[:, 0:9 * C].rearrange("p (y x c) -> p y x c", y=3, x=3)
                    for rows, pos, buf, dx in TAPS:
                        last = v.tensor_copy(out_w[buf][rows, :, (LO, HI)[pos]], taps[rows, :, dx, :])
                    last.then_inc(s_outw, 1)

            def add_block(b, n, staged):
                for sub in range(2):
                    dve.wait_ge(s_conv, b * 2 * NBLK + 2 * n + (2 * NBLK + sub + 1))
                    if staged is not None:
                        dve.wait_ge(s_stage, staged)
                    dst = image5[:, ds(b, 1), sub, ds(n * BLK, BLK), :].rearrange("p b k j -> p (b k j)")
                    v.tensor_tensor(dst, dst, bank_out[sub][0:P, :], ALU.add).then_inc(s_x1, 1)
                    dve.wait_ge(s_x1, b * 2 * NBLK + 2 * n + (sub + 1 + TWO))
                    last = take_stats(P, b, 2 * n + sub, dst)
                return last

            for i in range(PAIRS):
                take_pair(0, i)
                if 1 <= i <= (NB - 1) * LOADS:
                    x_stats(LOADS + i - 1)
                if i == PAIRS - 3:
                    dve.wait_ge(s_stat, X_STATS)
                    group_norm(1, P, NSTAT, 1, NB)
            with dve.Fori(0, NB - 1) as b:
                chain.enter(b, ATT_LINKS)
                for i in range(PAIRS):
                    take_pair(b * PAIRS + PAIRS, i)
                    if i in SLOTS:
                        softmax_step(b, SLOTS.index(i))
                with dve.Fori(0, NBLK - 1) as n:
                    add_block(b, n, b * 2 * NBLK + n + (2 * NBLK + 2))
                add_block(b, NBLK - 1, None).then_inc(s_stat, 1)
                chain.leave(NB - 1)
            for t in range(len(SLOTS)):
                softmax_step(NB - 1, t)
            for n in range(NBLK):
                last = add_block(NB - 1, n, (2 * NB - 1) * NBLK + n + 2 if n < NBLK - 1 else None)
            last.then_inc(s_stat, 1)

            def step(layer, done, scan, n):
                forward, along_w, kind, ahead = SCANS[scan]
                _, at = step_at(forward, n)
                src = (at - 1) % H if ahead else at
                for g in range(2):
                    dve.wait_ge(s_prod[g], done + (layer * PASSES * STEPS + 1))
                    prod = bank[g][0:P, 0:2 * J2].rearrange("p (b j) -> p b j", b=2)
                    v.scalar_tensor_tensor(out=line(g, along_w, at), in0=prod,
                                           scalar=scan_bias[:, 3 * layer + kind:3 * layer + kind + 1],
                                           in1=line(g, along_w, src), op0=ALU.add, op1=ALU.add).then_inc(s_state[g], 1)

            for layer in range(2):
                n_res = layer * NCH
                dve.wait_ge(s_stat, X_STATS + (1 + layer) * NB)
                group_norm(layer + 2, P, NSTAT)
                dve.wait_ge(s_save, (layer + 1) * 16 * NB)
                for b in range(2):
                    cols = image[0:P, b * IMG:(b + 1) * IMG]
                    last = v.tensor_scalar(cols, cols, gn_scale[0:P, b:b + 1], gn_shift[0:P, b:b + 1],
                                           ALU.mult, ALU.add)
                last.then_inc(s_state[0], 1)
                dve.wait_ge(s_scan_c, 16 * N_SCAN_DMA)
                for scan in range(PASSES):
                    for n in range(STEPS):
                        step(layer, scan * STEPS + n, scan, n)
                dve.wait_ge(s_swap, (layer + 1) * 6 * K2 + 1)
                if layer == 0:
                    with dve.Fori(0, NCH // 4) as t:
                        for m in range(4):
                            dve.wait_ge(s_back[m % 2], t * 32 + (m // 2 + 1) * 16)
                            dst = image[0:P, ds(t * 4 * CHUNK + m * CHUNK, CHUNK)]
                            v.tensor_tensor(dst, dst, kept[m % 2], ALU.add).then_inc(s_res, 1)
                            dve.wait_ge(s_res, 4 * t + (m + 1 + TWO))
                            for c in range(4):
                                src = image[0:P, ds(t * 4 * CHUNK + (m * CHUNK + c * BN), BN)]
                                last = take_stats(P, t, m * 4 + c, src)
                        last.then_inc(s_stat, 1)
                else:
                    with dve.Fori(0, NB // 2) as bp:
                        with dve.Fori(0, NBLK // 2) as q:
                            for m in range(2):
                                dve.wait_ge(s_back[m], bp * (NBLK * 8) + q * 16 + (8 * NCH + 16))
                                dve.wait_ge(s_flat[m], bp * (NBLK * 16) + q * 32 + 32)
                                for a in range(2):
                                    for half, src in enumerate((LO, HI)):
                                        lanes = (LO, HI)[a]
                                        o = nat[m][lanes, :].rearrange("p (k s j q) -> p s k j q", k=BLK, s=2, j=J2)
                                        i0 = image5[src, ds(2 * bp + a, 1), :, ds(q * 2 * BLK + m * BLK, BLK), :]
                                        i1 = kept[m][src, a * 2 * BN:(a + 1) * 2 * BN]
                                        last = v.tensor_tensor(
                                            o[:, :, :, :, half], i0.rearrange("p b s k j -> p (b s) k j"),
                                            i1.rearrange("p (s k j) -> p s k j", s=2, k=BLK), ALU.add)
                                last.then_inc(s_res, 1)

            for b in range(NB):
                dve.wait_ge(s_tok[b], 16)
                for c in range(TCOLS // BN):
                    last = take_stats(128, b, c, toks[:, b, c * BN:(c + 1) * BN])
            last.then_inc(s_stat, 1)
            dve.wait_ge(s_stat, X_STATS + 2 * NB + 1)
            group_norm(4, 128, TCOLS // BN)
            per_w = [128, W, G]
            x1 = hid.rearrange("p (w f) -> p w f", f=HID)[:, :, 0:G]
            x2 = hid.rearrange("p (w f) -> p w f", f=HID)[:, :, G:HID]
            dev_v = dev.rearrange("p (w f) -> p w f", f=G)
            dev2_v = dev2.rearrange("p (w f) -> p w f", f=G)
            chm_v = chm.rearrange("p (q c w) -> p q c w", q=NQ, c=G)
            spm_v = spm.rearrange("p (q c w) -> p q c w", q=NQ, c=G)

            with dve.Fori(0, NB) as b:
                chain.enter(b, MLP_LINKS)
                v.tensor_scalar(xn, toks[:, ds(b, 1), :].rearrange("p b n -> p (b n)"), gn_scale[:, ds(b, 1)],
                                gn_shift[:, ds(b, 1)], ALU.mult, ALU.add).then_inc(s_xn, 1)
                for g in range(1, GROUPS, 2):
                    dve.wait_ge(s_xt_p, b * GROUPS + g + 1)
                    if g == 1:
                        dve.wait_ge(s_gate_zero, 2)
                    v.tensor_copy(x_t[1][0:96, :], bank[1][0:96, :]).then_inc(s_xt_v, 1)
                dve.wait_ge(s_gelu, 5 * b + 5)
                link(v.tensor_reduce(s1, x2, AX, ALU.add))
                link(v.scalar_tensor_tensor(out=dev_v, in0=s1.unsqueeze(2).to_broadcast(per_w), scalar=-1.0 / G,
                                            in1=x2, op0=ALU.mult, op1=ALU.add))
                link(v.tensor_tensor(dev2, dev, dev, ALU.mult))
                link(v.tensor_reduce(s2, dev2_v, AX, ALU.add))
                v.tensor_scalar(s3, s2, 1.0 / G, LN_EPS, ALU.mult, ALU.add).then_inc(s_ln, 1)
                dve.wait_ge(s_ln_a, 2 * b + 1)
                link(v.reciprocal(s5, s4))
                link(v.tensor_tensor(dev2_v, dev_v, s5.unsqueeze(2).to_broadcast(per_w), ALU.mult))
                link(v.tensor_tensor(dev2_v, dev2_v, gam_sb.unsqueeze(1).to_broadcast(per_w), ALU.mult))
                v.tensor_tensor(spm_v.rearrange("p q c w -> p q w c"),
                                dev2.rearrange("p (q w f) -> p q w f", q=NQ, f=G),
                                bet_sb.unsqueeze(1).unsqueeze(1).to_broadcast([128, NQ, WQ, G]),
                                ALU.add).then_inc(s_ln, 1)
                dve.wait_ge(s_gt_p, 8 * b + 6)
                for i in range(2):
                    q4 = [128, 4, G, WQ]
                    link(v.tensor_tensor(chm_v[:, 4 * i:4 * i + 4],
                                         bank[2 + i][:, :].rearrange("p (q c w) -> p q c w", q=4, c=G),
                                         pwb_sb.unsqueeze(1).unsqueeze(3).to_broadcast(q4), ALU.add))
                    c4 = [128, NQ, 4, WQ]
                    link(v.tensor_tensor(spm_v[:, :, 4 * i:4 * i + 4, :],
                                         bank[6 + i][:, :].rearrange("p (c q w) -> p q c w", c=4, q=NQ),
                                         dwb_sb[:, 4 * i:4 * i + 4].unsqueeze(1).unsqueeze(3).to_broadcast(c4),
                                         ALU.add))
                link(v.tensor_tensor(chm, chm, spm, ALU.mult))
                v.tensor_tensor(chm_v, chm_v, x1.rearrange("p (q w) c -> p q c w", q=NQ), ALU.mult)\
                    .then_inc(s_gate, 1)
                dve.wait_ge(s_b2, b + 1)
                for q in range(NQ):
                    for f in range(2):
                        dve.wait_ge(s_proj, b * 2 * NQ + 2 * q + f + 1)
                        dst = toks[:, ds(b, 1), :].rearrange("p b (c w) -> p (b c) w", c=C)
                        dst = dst[:, f * TOK // 2:(f + 1) * TOK // 2, q * WQ:(q + 1) * WQ]
                        v.tensor_tensor(dst, dst, bank[4 + f][:, 0:TOK // 2 * WQ].rearrange("p (c w) -> p c w", w=WQ),
                                        ALU.add).then_inc(s_add, 1)
                chain.leave(NB)


def kernel(**inputs):
    import numpy as np
    import concourse.bacc as bacc
    from concourse.bass_utils import run_bass_kernel_spmd as run

    nc = bacc.Bacc("TRN2", target_bir_lowering=False, num_devices=1)
    a = {k: np.asarray(t) for k, t in inputs.items()}
    half = np.concatenate([np.arange(C) // 3, np.full(HALF - C, -1), np.arange(C) // 3])
    flat_group = np.arange(128) // 8
    scans = [a[f"L{n}_conv_{d}_w"] for n in (1, 2) for d in ("down", "right", "left")]
    biases = [a[f"L{n}_conv_{d}_b"] for n in (1, 2) for d in ("down", "right", "left")]
    dw = a["L0_conv_dw_w"].reshape(3 * C, 9)
    arrays = {
        "x": a["x"],
        "qkv_t": a["L0_conv_qkv_w"].reshape(3 * C, C).T,
        "v_w": a["L0_conv_qkv_w"].reshape(3 * C, C)[2 * C:],
        "dw_t": dw.T.reshape(-1),
        "dw_v": dw[2 * C:],
        "proj_t": a["L0_conv_proj_w"].reshape(C, C).T,
        "temp": a["L0_conv_temperature"].reshape(1),
        "scan_w": np.stack([w.transpose(1, 2, 0) for w in scans]),
        "scan_b": np.stack(biases, axis=1),
        "w1": a["L3_conv_W1"], "b1": a["L3_conv_b1"].reshape(1, HID),
        "gamma": a["L3_conv_gamma"], "beta": a["L3_conv_beta"],
        "gdw": a["L3_conv_dw_w"].reshape(-1), "gdw_b": a["L3_conv_dw_b"],
        "gpw_t": a["L3_conv_pw_w"].reshape(G, G).T, "gpw_b": a["L3_conv_pw_b"],
        "w2": a["L3_conv_W2"], "b2": a["L3_conv_b2"],
        "ident_c": np.eye(128, 130, 1, dtype=np.float32),
        "group_half_c": ((half[:, None] == half[None]) & (half[:, None] >= 0)).astype(np.float32) / np.float32(6),
        "group_flat_c": (flat_group[:, None] == flat_group[None]).astype(np.float32) / np.float32(8),
    }
    arrays = {k: np.ascontiguousarray(t) for k, t in arrays.items()}
    aps = {k: nc.dram_tensor(f"in_{k}", t.shape, F32, kind="ExternalInput").ap() for k, t in arrays.items()}
    saved = [nc.dram_tensor(f"saved{i}", (P, COLS), F32).ap() for i in range(2)]
    flat = nc.dram_tensor("flat_rows", (NB, C * H * W), F32).ap()
    out = nc.dram_tensor("out_0", (NB, C, H, W), F32, kind="ExternalOutput").ap()
    build(nc, saved=saved, flat=flat, out=out, **aps)
    r = run(nc, [{f"in_{k}": t for k, t in arrays.items()}], core_ids=[0])
    return r.results[0]["out_0"]
```

```python
from contextlib import ExitStack

import concourse.bass as bass
from concourse import mybir

ALU = mybir.AluOpType
ACT = mybir.ActivationFunctionType
AX = mybir.AxisListType.X
F32 = mybir.dt.float32
ds = bass.ds

NB, C, H, W = 4, 48, 128, 128
HALF = 64
P = HALF + C
LO, HI = slice(0, C), slice(HALF, P)
K2, J2 = H // 2, W // 2
SUB = K2 * J2
IMG = 2 * SUB
COLS = NB * IMG
BN = 512
NSTAT = IMG // BN
GN_EPS = 1e-5
NORM_FLOOR_SQ = 1e-24

IN_ROWS = 16
IN_COLS = IN_ROWS * W
LOADS = H // IN_ROWS

BLK = 8
NBLK = K2 // BLK
ZSUB = (BLK + 2) * J2
PAIRS = 4 * NBLK
QK = 2 * C

STEPS = H - 1
PASSES = 4
CHUNK = 2048
NCH = COLS // CHUNK
PER = IMG // CHUNK
VCH = 2
V_COLS = 5120

TOK = 48
HID = 16
G = HID // 2
TCOLS = H * W * C // 128
TPAIRS = TCOLS // (2 * TOK)
GROUPS = TPAIRS // 4
GW = W + 2
WQ = 16
NQ = W // WQ
LN_EPS = 1e-5

TWO = 2


X_STATS = 1 + NB * LOADS
SLOTS = (0, 2, 5, 8, 11, 14)
N_CONST = 11
N_GATE = 6 + 2 * G
N_SCAN_DMA = 2 + 6 * 10
N_BAND = G * 3 * 5
ATT_LINKS = 8
MLP_LINKS = 10
EARLY = 10


class Chain:

    def __init__(self, eng, sem):
        self.eng, self.sem, self.links, self.turn = eng, sem, 0, None

    def enter(self, turn, rate):
        self.turn, self.rate, self.first = turn, rate, self.links

    def leave(self, turns):
        assert self.links == self.first + self.rate, (self.links - self.first, self.rate)
        self.links, self.turn = self.first + turns * self.rate, None

    def link(self, ins):
        ins.then_inc(self.sem, 1)
        self.links += 1
        self.eng.wait_ge(self.sem, self.links if self.turn is None else self.turn * self.rate + self.links)


def build(nc, x, qkv_t, v_w, dw_t, dw_v, proj_t, temp, scan_w, scan_b,
          w1, b1, gamma, beta, gdw, gdw_b, gpw_t, gpw_b, w2, b2,
          ident_c, group_half_c, group_flat_c, saved, flat, out):
    with ExitStack() as ctx:
        def sb(name, shape):
            return ctx.enter_context(nc.sbuf_tensor(name, shape, F32))

        def sem(name):
            return ctx.enter_context(nc.semaphore(name))

        image = sb("image", [128, COLS])
        identp = sb("identp", [128, 130])
        group_half = sb("group_half", [P, P])
        group_flat = sb("group_flat", [128, 128])
        stats = sb("stats", [128, NB * NSTAT * 6])
        mean_var = sb("mean_var", [128, NB, 2])
        gn_mean = sb("gn_mean", [128, NB])
        gn_off = sb("gn_off", [128, NB])
        gn_sq = sb("gn_sq", [128, NB])
        gn_var = sb("gn_var", [128, NB])
        gn_std = sb("gn_std", [128, NB])
        gn_scale = sb("gn_scale", [128, NB])
        gn_shift = sb("gn_shift", [128, NB])
        scan_bias = sb("scan_bias", [P, 6])
        scan_wt = sb("scan_wt", [P, 6, 3, P])
        band = sb("band", [128, 3 * G, 128])
        gates = sb("gates", [128, 8 * G + 9 * G])
        work = sb("work", [128, 13300])
        ident = identp[:, 1:129]
        image5 = image[0:P, :].rearrange("p (b s k j) -> p b s k j", b=NB, s=2, k=K2)

        def cut(at, dims, parts=128):
            n = 1
            for m in dims:
                n *= m
            v = work[0:parts, at:at + n]
            if len(dims) == 2:
                v = v.rearrange("p (a b) -> p a b", a=dims[0])
            elif len(dims) == 3:
                v = v.rearrange("p (a b c) -> p a b c", a=dims[0], b=dims[1])
            return v

        rows_in = [band[0:P, :, :].rearrange("p a b -> p (a b)")[:, 0:IN_COLS], cut(13300 - IN_COLS, [IN_COLS], P)]
        blk_z = [cut(i * 2 * ZSUB, [2 * ZSUB], P) for i in range(2)]
        blk_n = [cut((2 + i) * 2 * ZSUB, [2 * ZSUB], P) for i in range(2)]
        blk_2 = [r.rearrange("p (e s n) -> p e s n", e=2, s=2) for r in rows_in]
        at = 8 * ZSUB
        qkv_sb = cut(at, [3 * C], P)
        at += 3 * C
        qk_w = [cut(at + i * 6 * QK, [3, 2, QK], P) for i in range(2)]
        at += 12 * QK
        qk_w2 = cut(at, [2, QK], P)
        at += 2 * QK
        v_taps = cut(at, [9, P], C)
        at += 9 * P
        out_w = [cut(at + i * 3 * P, [3, P], P) for i in range(2)]
        at += 6 * P
        dw_sb = cut(at, [9, 3 * C], P)
        at += 27 * C
        gram = cut(at, [QK], QK)
        gram_d = cut(at + QK, [QK], QK)
        at += 2 * QK
        v_sb, proj_sb, logits, probs, probs_n, mix_t = (cut(at + i * C, [C], C) for i in range(6))
        ones = cut(at + 6 * C, [C], QK)
        at += 7 * C
        dwv_sb, temp_sb, col = cut(at, [9], C), cut(at + 9, [1], C), cut(at + 10, [8], QK)
        at += 18
        zero_row = cut(at, [J2], P)
        at += J2
        qk_sb = [cut(at + i * 4 * C * 2, [4 * C * 2]) for i in range(2)]
        at += 16 * C
        assert at <= 13300 - IN_COLS, at
        back = [cut(i * CHUNK, [CHUNK], P) for i in range(PER)]
        nat = [cut((PER + i) * CHUNK, [CHUNK], P) for i in range(2)]
        swap_tmp = cut((PER + 2) * CHUNK, [NB, 64], P)
        toks = image[:, 0:NB * TCOLS].rearrange("p (b n) -> p b n", b=NB)
        xn = image[:, NB * TCOLS:NB * TCOLS + TCOLS]
        hid = image[:, COLS - 2048:COLS]
        x_t = [cut(i * 512, [512]) for i in range(2)]
        at = 1024
        w1_sb = cut(at, [2 * HID], 97)
        at += 2 * HID
        pw_k = cut(at, [G, WQ])
        at += 128
        w2_k = cut(at, [TOK, WQ])
        at += TOK * WQ
        n_pad = cut(at, [G, GW])
        at += G * GW
        hid_t = cut(at, [2048])
        at += 2048
        dev, dev2, n_t, g_t, chm, spm = (cut(at + i * 1024, [1024]) for i in range(6))
        at += 6 * 1024
        s1, s2, s3, s4, s5 = (cut(at + i * 128, [128]) for i in range(5))
        at += 5 * 128
        assert at <= 13300, at
        gdw_sb = gates[:, 0:72]
        gam_sb, bet_sb, dwb_sb, pwb_sb, pwr_sb = (gates[:, 72 + 8 * i:80 + 8 * i] for i in range(5))
        band_tmp = [sb(f"band_tmp{i}", [128, 128])[:, :] for i in range(2)]
        w2r_sb = sb("w2r_sb", [128, TOK])
        b2_sb = sb("b2_sb", [128, TOK])

        bank = [ctx.enter_context(nc.psum_tensor(f"bank{i}", [128, 512], F32)) for i in range(8)]
        bank_gram, bank_small, bank_wt = bank[2], bank[3], bank[4]
        bank_out = bank[5:7]
        bank_gn = bank[7]

        s_const = sem("s_const")
        s_gate_w = sem("s_gate_w")
        s_back_gap = sem("s_back_gap")
        s_gate_zero = sem("s_gate_zero")
        s_gate_const = sem("s_gate_const")
        s_pool = sem("s_pool")
        s_gap = sem("s_gap")
        s_zero = sem("s_zero")
        s_border = sem("s_border")
        s_load = [sem(f"s_load{i}") for i in range(2)]
        s_split = sem("s_split")
        s_stat = sem("s_stat")
        s_dve = sem("s_dve")
        s_gn_v = sem("s_gn_v")
        s_gn_mm = sem("s_gn_mm")
        s_gn_std = sem("s_gn_std")
        s_gn = sem("s_gn")
        s_wts = sem("s_wts")
        s_stage = sem("s_stage")
        s_pack = sem("s_pack")
        s_qk = sem("s_qk")
        s_qk_sb = sem("s_qk_sb")
        s_gram = sem("s_gram")
        s_sm_v = sem("s_sm_v")
        s_sm_a = sem("s_sm_a")
        s_sm_t = sem("s_sm_t")
        s_outw = sem("s_outw")
        s_conv = sem("s_conv")
        s_x1 = sem("s_x1")
        s_save = [sem(f"s_save{b}") for b in range(NB)]
        s_scan_w = sem("s_scan_w")
        s_scan_c = sem("s_scan_c")
        s_prod = [sem(f"s_prod{g}") for g in range(2)]
        s_state = [sem(f"s_state{g}") for g in range(2)]
        s_swap = sem("s_swap")
        s_tail = sem("s_tail")
        s_back = [sem(f"s_back{i}") for i in range(PER)]
        s_kept_v = sem("s_kept_v")
        s_kept_p = sem("s_kept_p")
        s_res = sem("s_res")
        s_res_p = sem("s_res_p")
        s_flat = [sem(f"s_flat{i}") for i in range(2)]
        s_tok = [sem(f"s_tok{b}") for b in range(NB)]
        s_band = sem("s_band")
        s_xn = sem("s_xn")
        s_xt_p = sem("s_xt_p")
        s_xt_a = sem("s_xt_a")
        s_xt_v = sem("s_xt_v")
        s_hid = sem("s_hid")
        s_gelu = sem("s_gelu")
        s_hid_t = sem("s_hid_t")
        s_hid_a = sem("s_hid_a")
        s_hid_v = sem("s_hid_v")
        s_ln = sem("s_ln")
        s_ln_a = sem("s_ln_a")
        s_gt_p = sem("s_gt_p")
        s_gt_a = sem("s_gt_a")
        s_pw_used = sem("s_pw_used")
        s_gate = sem("s_gate")
        s_proj = sem("s_proj")
        s_add = sem("s_add")
        s_res3 = [sem(f"s_res3_{i}") for i in range(2)]
        s_b2 = sem("s_b2")
        s_out = sem("s_out")

        block = ctx.enter_context(nc.Block())

        def own_wait(eng, semaphore, value):
            value = eng.compute_val(value)
            eng.wait_ge(s_gap, 2)
            eng.wait_ge(semaphore, value)

        SCANS = [(True, False, 0, False), (False, False, 0, True), (True, True, 1, False), (False, True, 2, False)]

        def line(g, along_w, at):
            b = slice(2 * g, 2 * g + 2)
            return image5[:, b, at % 2, :, at // 2] if along_w else image5[:, b, at % 2, at // 2, :]

        def step_at(forward, n):
            return (n, n + 1) if forward else (STEPS - n, STEPS - 1 - n)

        def natural(eng, bp, q, m, a, half):
            src, lanes = (LO, HI)[half], (LO, HI)[a]
            o = nat[m % 2][lanes, :].rearrange("p (k s j q) -> p s k j q", k=BLK, s=2, j=J2)
            i0 = image5[src, ds(2 * bp + a, 1), :, ds(q * PER * BLK + m * BLK, BLK), :]
            i1 = back[m][src, a * 2 * BN:(a + 1) * 2 * BN]
            return eng.tensor_tensor(o[:, :, :, :, half], i0.rearrange("p b s k j -> p (b s) k j"),
                                     i1.rearrange("p (s k j) -> p s k j", s=2, k=BLK), ALU.add)

        def hidden_views(i):
            return (hid[:, i * 512:(i + 1) * 512].rearrange("p (g t c) -> p t g c", g=4, t=4),
                    bank[2 + i][:, :].rearrange("p (t g c) -> p t g c", t=4, g=4))

        TAPS = [(LO, 0, 0, 1), (LO, 1, 0, 0), (HI, 0, 0, 2), (HI, 1, 0, 1), (LO, 1, 1, 2), (HI, 0, 1, 0)]

        def conv_rows(sub):
            return [(0, 1, -1), (1, 0, 0), (2, 1, 0)] if sub == 0 else [(0, 0, 0), (1, 1, 0), (2, 0, 1)]

        @block.sync
        def _(sp):
            rows = x.rearrange("b c h w -> b c (h w)")
            sp.wait_ge(s_gap, 2)
            with sp.Fori(0, NB) as b:
                with sp.Fori(0, LOADS // 2) as q:
                    for m in range(2):
                        sp.wait_ge(s_split, b * LOADS + q * 2 + m + 1)
                        src = rows[ds(b, 1), :, ds(q * 2 * IN_COLS + m * IN_COLS, IN_COLS)]
                        sp.dma_start(rows_in[m][LO, :], src.rearrange("b c n -> (b c) n")).then_inc(s_load[m], 16)
                        src = rows[ds(b, 1), :, ds(q * 2 * IN_COLS + m * IN_COLS + 1, IN_COLS - 1)]
                        sp.dma_start(rows_in[m][HI, 0:IN_COLS - 1],
                                     src.rearrange("b c n -> (b c) n")).then_inc(s_load[m], 16)
            gate_consts = [(gdw_sb, gdw.partition_broadcast(128)), (gam_sb, gamma.partition_broadcast(128)),
                           (bet_sb, beta.partition_broadcast(128)), (dwb_sb, gdw_b.partition_broadcast(128)),
                           (pwb_sb, gpw_b.partition_broadcast(128)), (b2_sb[:, :], b2.partition_broadcast(128))]
            for c in range(G):
                gate_consts.append((pwr_sb[c * WQ:(c + 1) * WQ, :], gpw_t[c].partition_broadcast(WQ)))
                gate_consts.append((w2r_sb[c * WQ:(c + 1) * WQ, :], w2[c].partition_broadcast(WQ)))
            assert len(gate_consts) == N_GATE
            for dst, src in gate_consts:
                sp.dma_start(dst, src).then_inc(s_gate_w, 16)
            sp.wait_ge(s_scan_w, 1)
            n_dma = 0
            for half in (LO, HI):
                sp.dma_start(scan_bias[half, :], scan_b).then_inc(s_scan_c, 16)
                n_dma += 1
            for t in range(6):
                for qi, rows in enumerate((LO, HI)):
                    for qo, cols in enumerate((LO, HI)):
                        shifts = [m for m in (-1, 0, 1) if 0 <= 2 * m + qi - qo + 2 < 5]
                        for m in shifts:
                            sp.dma_start(scan_wt[rows, t, m + 1, cols],
                                         scan_w[t][:, 2 * m + qi - qo + 2, :]).then_inc(s_scan_c, 16)
                            n_dma += 1
            assert n_dma == N_SCAN_DMA
            for b in range(NB - 1):
                sp.wait_ge(s_x1, TWO + (b + 1) * 2 * NBLK)
                for half, rows in enumerate((LO, HI)):
                    sp.dma_start(saved[0][half, :, b * IMG:(b + 1) * IMG],
                                 image[rows, b * IMG:(b + 1) * IMG]).then_inc(s_save[b], 16)
            for i in range(2):
                sp.wait_ge(s_x1, TWO + (NB - 1) * 2 * NBLK + (i + 1) * NBLK)
                for half, rows in enumerate((LO, HI)):
                    dst, src = (v.rearrange("p (s n) -> p s n", s=2)[:, :, i * SUB // 2:(i + 1) * SUB // 2]
                                for v in (saved[0][half, :, (NB - 1) * IMG:], image[rows, (NB - 1) * IMG:]))
                    sp.dma_start(dst, src).then_inc(s_save[NB - 1], 16)
            for b in range(NB):
                sp.wait_ge(s_save[b], 64 if b == NB - 1 else 32)
            sp.wait_ge(s_back_gap, PER)

            def bring(c):
                for half, rows in enumerate((LO, HI)):
                    sp.dma_start(back[c % PER][rows, :],
                                 saved[0][half, :, c * CHUNK:(c + 1) * CHUNK]).then_inc(s_back[c % PER], 16)

            def save_columns(b, c0, c1):
                for half, rows in enumerate((LO, HI)):
                    sp.dma_start(saved[1][half, :, b * IMG + c0:b * IMG + c1],
                                 image[rows, b * IMG + c0:b * IMG + c1]).then_inc(s_save[b], 16)

            for c in range(PER):
                bring(c)
            for b in range(NB - 1):
                for m in range(PER):
                    if m < VCH:
                        sp.wait_ge(s_kept_v, b * VCH + m + 1)
                    else:
                        sp.wait_ge(s_kept_p, b * (PER - VCH) + m - VCH + 1)
                    bring((b + 1) * PER + m)
                save_columns(b, 0, IMG)
            sp.wait_ge(s_kept_v, NB * VCH)
            save_columns(NB - 1, 0, VCH * CHUNK)
            sp.wait_ge(s_kept_p, NB * (PER - VCH))
            save_columns(NB - 1, VCH * CHUNK, IMG)
            for b in range(NB):
                sp.wait_ge(s_save[b], 128 if b == NB - 1 else 64)
            with sp.Fori(0, NB // 2) as bp:
                with sp.Fori(0, NBLK // PER) as q:
                    for m in range(PER):
                        sp.wait_ge(s_res, bp * NBLK + PER * q + (m + 1))
                        sp.wait_ge(s_res_p, bp * NBLK + PER * q + (m + 1))
                        for half, rows in enumerate((LO, HI)):
                            kept_rows = saved[1][half].rearrange("p (b s n) -> p b s n", b=NB, s=2)
                            src = kept_rows[:, ds(2 * bp, 2), :, ds(q * PER * BN + m * BN, BN)]
                            sp.dma_start(back[m][rows, :].rearrange("p (a n) -> p a n", a=4),
                                         src.rearrange("p b s n -> p (b s) n")).then_inc(s_back[m], 16)
            for b in range(NB):
                for m in range(2):
                    sp.wait_ge(s_flat[m], 32 + 8 * NCH * (b // 2 + 1))
                if b == 1:
                    sp.wait_ge(s_res, PER + NCH - 1)
                sp.dma_start(toks[:, b, :], flat[b].rearrange("(p n) -> p n", p=128)).then_inc(s_tok[b], 16)
            grid = flat.rearrange("b (c h w) -> b h c w", c=C, h=H)
            grid_out = out.rearrange("b c h w -> b h c w")

            def residual(b):
                sp.wait_ge(s_xn, b + 1)
                sp.dma_start(toks[:, b, :].rearrange("p (c w) -> p c w", c=C), grid[b]).then_inc(s_res3[b % 2], 16)

            residual(0)
            residual(1)
            for b in range(NB):
                if b + 2 < NB:
                    sp.wait_ge(s_b2, b + 1)
                    residual(b + 2)
                for f in range(2):
                    sp.wait_ge(s_add, TWO + (2 * b + f + 1) * NQ)
                    part = slice(f * TOK // 2, (f + 1) * TOK // 2)
                    sp.dma_start(grid_out[b][:, part, :],
                                 toks[:, b, :].rearrange("p (c w) -> p c w", c=C)[:, part, :]).then_inc(s_out, 16)
            sp.wait_ge(s_out, 32 * NB)

        @block.gpsimd
        def _(pool):
            pool_chain = Chain(pool, s_pool)

            def ms(v, value):
                pool_chain.link(nc.gpsimd.memset(v, value))

            for s, n in ((s_split, TWO), (s_qk_sb, TWO), (s_gram, TWO), (s_x1, TWO), (s_res, PER), (s_res_p, PER),
                         (s_conv, 2 * NBLK), (s_qk, 4), (s_swap, 1), (s_add, TWO), (s_flat[0], 32), (s_flat[1], 32)):
                pool.sem_inc(s, n)
            for m in range(2):
                nc.gpsimd.memset(rows_in[m][32:HALF, :], 0.0).then_inc(s_gap, 1)
            pool.wait_ge(s_gap, 2)
            for m in range(2):
                ms(blk_n[m], 0.0)
                nc.gpsimd.memset(blk_z[m], 0.0).then_inc(s_border, 1)
                pool.wait_ge(s_border, m + 1)
            ms(ones, 1.0)
            ms(zero_row, 0.0)
            ms(qk_w[0], 0.0)
            ms(qk_w[1], 0.0)
            ms(qk_w2, 0.0)
            ms(v_taps, 0.0)
            ms(out_w[0], 0.0)
            nc.gpsimd.memset(out_w[1], 0.0).then_inc(s_zero, 1)
            pool.wait_ge(s_zero, 1)
            ms(scan_bias[:, :], 0.0)
            nc.gpsimd.memset(scan_wt[:, :, :, :], 0.0).then_inc(s_scan_w, 1)
            pool.wait_ge(s_scan_w, 1)
            for g in range(2):
                pool.wait_ge(s_state[g], 1)
            for m in range(PER):
                nc.gpsimd.memset(back[m][32:HALF, :], 0.0).then_inc(s_back_gap, 1)
            pool.wait_ge(s_back_gap, PER)
            pool.wait_ge(s_const, 16 * N_CONST)
            pool.wait_ge(s_gate_w, 16 * N_GATE)
            n = 0
            for c in range(G):
                for dx in range(3):
                    for dy in range(3):
                        tap = gdw_sb[:, c * 9 + dy * 3 + dx:c * 9 + dy * 3 + dx + 1]
                        if dy:
                            pool.wait_ge(s_band, n)
                            ins = nc.gpsimd.tensor_scalar(band_tmp[dy - 1], identp[:, dy:dy + 128], tap, None, ALU.mult)
                            ins.then_inc(s_band, 1)
                            pool.wait_ge(s_band, n + 1)
                            nc.gpsimd.tensor_tensor(band[:, c * 3 + dx, :], band[:, c * 3 + dx, :], band_tmp[dy - 1],
                                                    ALU.add).then_inc(s_band, 1)
                            n += 2
                        else:
                            nc.gpsimd.tensor_scalar(band[:, c * 3 + dx, :], identp[:, 0:128], tap, None,
                                                    ALU.mult).then_inc(s_band, 1)
                            n += 1
            assert n == N_BAND
            pool.wait_ge(s_band, N_BAND)
            pool.wait_ge(s_swap, 6 * K2 + 1)
            for g in range(2):
                pool.wait_ge(s_state[g], PASSES * STEPS + 1)
            with pool.Fori(0, NB) as b:
                for m in range(VCH, PER):
                    pool.wait_ge(s_back[m], b * 32 + 32)
                    dst = image[0:P, ds(b * IMG + m * CHUNK, CHUNK)]
                    nc.gpsimd.tensor_tensor(dst, dst, back[m], ALU.add).then_inc(s_kept_p, 1)
            pool.wait_ge(s_swap, 2 * 6 * K2 + 1)
            for g in range(2):
                pool.wait_ge(s_state[g], 2 * (PASSES * STEPS + 1))
            with pool.Fori(0, NB // 2) as bp:
                with pool.Fori(0, NBLK // PER) as q:
                    for m in range(PER):
                        pool.wait_ge(s_back[m], bp * (NBLK * 8) + q * 32 + (32 * NB + 32))
                        pool.wait_ge(s_flat[m % 2], bp * (NBLK * 16) + q * 64 + (m // 2 * 32 + 32))
                        natural(nc.gpsimd, bp, q, m, 1, 1).then_inc(s_res_p, 1)
            pool.wait_ge(s_flat[0], 32 + 32 * NCH // 2)
            pool.wait_ge(s_flat[1], 32 + 32 * NCH // 2)
            ms(w1_sb, 0.0)
            ms(n_pad, 0.0)
            for m in range(2):
                nc.gpsimd.memset(x_t[m][96:128, :], 1.0).then_inc(s_gate_zero, 1)
            pool.wait_ge(s_gate_zero, 2)
            pool.dma_start(w1_sb[0:TOK, 0:HID], w1).then_inc(s_gate_const, 16)
            pool.dma_start(w1_sb[TOK:2 * TOK, HID:2 * HID], w1).then_inc(s_gate_const, 16)
            pool.dma_start(w1_sb[96:97, 0:HID], b1).then_inc(s_gate_const, 16)
            pool.dma_start(w1_sb[96:97, HID:2 * HID], b1).then_inc(s_gate_const, 16)
            pool.wait_ge(s_band, N_BAND)
            nc.gpsimd.tensor_copy(s1[:, 0:WQ], ident[:, 0:WQ]).then_inc(s_band, 1)
            n = N_BAND + 1
            for c in range(1, G):
                pool.wait_ge(s_band, n)
                nc.gpsimd.tensor_tensor(s1[:, 0:WQ], s1[:, 0:WQ], ident[:, c * WQ:(c + 1) * WQ],
                                        ALU.add).then_inc(s_band, 1)
                n += 1
            pool.wait_ge(s_band, n)
            for o in range(G):
                nc.gpsimd.tensor_scalar(pw_k[:, o, :], s1[:, 0:WQ], pwr_sb[:, o:o + 1], None, ALU.mult)
            for e in range(TOK):
                last = nc.gpsimd.tensor_scalar(w2_k[:, e, :], s1[:, 0:WQ], w2r_sb[:, e:e + 1], None, ALU.mult)
            last.then_inc(s_band, 1)
            with pool.Fori(0, NB // 2) as t:
                for m in range(2):
                    pool.wait_ge(s_res3[m], 16 * t + 16)
                    v = toks[:, ds(2 * t + m, 1), :].rearrange("p b (c w) -> p (b c) w", c=C)
                    nc.gpsimd.tensor_tensor(v, v, b2_sb[:, :].unsqueeze(2).to_broadcast([128, C, W]),
                                            ALU.add).then_inc(s_b2, 1)

        @block.scalar
        def _(act):
            consts = [(identp[:, :], ident_c), (group_half[:, :], group_half_c), (group_flat[:, :], group_flat_c),
                      (qkv_sb[LO, :], qkv_t), (qkv_sb[HI, :], qkv_t),
                      (dw_sb[LO].rearrange("p a b -> p (a b)"), dw_t.partition_broadcast(C)),
                      (dw_sb[HI].rearrange("p a b -> p (a b)"), dw_t.partition_broadcast(C)),
                      (v_sb, v_w), (dwv_sb, dw_v), (proj_sb, proj_t), (temp_sb, temp.partition_broadcast(C))]
            assert len(consts) == N_CONST
            for dst, src in consts:
                act.dma_start(dst, src).then_inc(s_const, 16)

            def split(c):
                m, b, k0 = c % 2, c // LOADS, c % LOADS * BLK
                act.wait_ge(s_load[m], 32 * (c // 2 + 1))
                src = rows_in[m].rearrange("p (k s j q) -> p s k j q", k=BLK, s=2, j=J2)[:, :, :, :, 0]
                nc.scalar.copy(image5[:, b, :, k0:k0 + BLK, :], src).then_inc(s_split, 1)

            for c in range(LOADS):
                split(c)

            def deviation(r, c0=0, c1=NB):
                act.wait_ge(s_gn_v, 3 * r + 3)
                nc.scalar.activation(gn_std[:, c0:c1], gn_var[:, c0:c1], ACT.Sqrt).then_inc(s_gn_std, 1)

            deviation(0, 0, 1)

            def stage(b, n, m):
                for sub in range(2):
                    kk0, rows = 1 - sub, BLK + 1
                    top = isinstance(n, int) and n == 0 and sub == 1
                    bottom = isinstance(n, int) and n == NBLK - 1 and sub == 0
                    if top or bottom:
                        o = sub * ZSUB + (0 if top else BLK + 1) * J2
                        nc.scalar.copy(blk_z[m][:, o:o + J2], zero_row)
                        nc.scalar.copy(blk_n[m][:, o:o + J2], zero_row)
                        rows = BLK
                        kk0 += top
                    for buf, part, d, e in ((blk_z, slice(0, P), (0, J2), (0, J2)),
                                            (blk_n, LO, (0, J2 - 1), (1, J2)), (blk_n, HI, (1, J2), (0, J2 - 1))):
                        dst = buf[m][part, sub * ZSUB + kk0 * J2:sub * ZSUB + (kk0 + rows) * J2]
                        src = image5[part, ds(b, 1), sub, ds(n * BLK - 1 + kk0, rows), e[0]:e[1]]
                        last = nc.scalar.activation(dst.rearrange("p (k j) -> p k j", j=J2)[:, :, d[0]:d[1]],
                                                    src.rearrange("p b k j -> p (b k) j"), ACT.Identity,
                                                    bias=gn_shift[part, ds(b, 1)], scale=gn_scale[part, ds(b, 1)])
                last.then_inc(s_stage, 1)

            def norms(b):
                act.wait_ge(s_sm_v, 5 * b + 1)
                nc.scalar.activation(col[:, 2:3], col[:, 1:2], ACT.Sqrt).then_inc(s_sm_a, 1)

            def exponentials(b):
                act.wait_ge(s_sm_v, 5 * b + 3)
                nc.scalar.activation(probs, logits, ACT.Exp, bias=col[0:C, 5:6],
                                     accum_out=col[0:C, 6:7]).then_inc(s_sm_a, 1)

            act.wait_ge(s_gn, 1)
            act.wait_ge(s_border, 2)
            for n in range(NBLK):
                if n >= 2:
                    act.wait_ge(s_qk, 4 * n)
                stage(0, n, n % 2)
                for c in range(3):
                    split(LOADS + 3 * n + c)
            deviation(1, 1, NB)
            act.wait_ge(s_gn, 2)
            def attention(b, last=False):
                for n in range(2):
                    own_wait(act, s_conv, b * 2 * NBLK + (2 * NBLK - 2 + 2 * n))
                    own_wait(act, s_qk, b * PAIRS + (PAIRS + 4 * n))
                    stage(b + 1, n, n)
                norms(b)
                own_wait(act, s_qk, b * PAIRS + (PAIRS + 8))
                stage(b + 1, 2, 0)
                exponentials(b)
                own_wait(act, s_qk, b * PAIRS + (PAIRS + 12))
                stage(b + 1, 3, 1)
                with act.Fori(2, NBLK // 2 - 1) as h:
                    for u in range(2):
                        own_wait(act, s_qk, b * PAIRS + 8 * h + (PAIRS + 4 * u))
                        stage(b + 1, 2 * h + u, u)
                for n in range(NBLK - 2, NBLK):
                    own_wait(act, s_qk, b * PAIRS + (PAIRS + 4 * n))
                    stage(b + 1, n, n % 2)
                for n in range(2):
                    own_wait(act, s_qk, b * PAIRS + (2 * PAIRS + 4 * n))
                    stage(b, n, n)
                if last:
                    for n in range(2, NBLK):
                        own_wait(act, s_conv, b * 2 * NBLK + (2 * NBLK + 2 * n - 2))
                        stage(b, n, n % 2)
                        if n in (2, 4):
                            (norms if n == 2 else exponentials)(b + 1)
                    return
                with act.Fori(1, NBLK // 2 - 1) as h:
                    for u in range(2):
                        own_wait(act, s_conv, b * 2 * NBLK + 4 * h + (2 * NBLK + 2 * u - 2))
                        stage(b, 2 * h + u, u)
                for n in range(NBLK - 2, NBLK):
                    own_wait(act, s_conv, b * 2 * NBLK + (2 * NBLK + 2 * n - 2))
                    stage(b, n, n % 2)

            with act.Fori(0, NB - 2) as b:
                attention(b)
            attention(NB - 2, True)

            def normalise(layer, b, c0, c1):
                act.wait_ge(s_gn, 2 * layer + 3 + b // 2)
                act.wait_ge(s_save[b], (layer + 1) * (64 if b == NB - 1 else 32))
                v = image[0:P, b * IMG + c0:b * IMG + c1]
                return nc.scalar.activation(v, v, ACT.Identity, bias=gn_shift[0:P, b:b + 1],
                                            scale=gn_scale[0:P, b:b + 1])

            for n in range(NBLK):
                act.wait_ge(s_conv, NB * 2 * NBLK + 2 * n - 2)
                stage(NB - 1, n, n % 2)
                if n == 0:
                    deviation(2, 0, 2)
                elif 2 <= n < 6:
                    last = normalise(0, n // 2 - 1, n % 2 * SUB, (n % 2 + 1) * SUB)
            last.then_inc(s_state[0], 1)

            def exchange(along_w, i, n):
                def part(rows, s):
                    v = image5[rows, :, s, :, ds(i, 1)] if along_w else image5[rows, :, s, ds(i, 1), :]
                    return v.rearrange("p b k j -> p b (k j)")
                own_wait(act, s_swap, n + 1)
                nc.scalar.copy(swap_tmp[HI], part(LO, 1)).then_inc(s_swap, 1)
                own_wait(act, s_swap, n + 2)
                nc.scalar.copy(part(LO, 1), part(HI, 0)).then_inc(s_swap, 1)
                own_wait(act, s_swap, n + 3)
                nc.scalar.copy(part(HI, 0), swap_tmp[HI]).then_inc(s_swap, 1)

            for layer in range(2):
                if layer:
                    deviation(2 * layer + 2, 0, 2)
                    for b in range(2):
                        last = normalise(layer, b, 0, IMG)
                    last.then_inc(s_state[0], 1)
                deviation(2 * layer + 3, 2, NB)
                for b in (2, 3):
                    last = normalise(layer, b, V_COLS, IMG)
                last.then_inc(s_tail, 1)
                for g in range(2):
                    act.wait_ge(s_prod[g], layer * PASSES * STEPS + 1)
                n0 = layer * 2 * 3 * K2
                prod0 = layer * PASSES * STEPS + STEPS
                with act.Fori(0, K2 - 2) as i:
                    for g in range(2):
                        own_wait(act, s_prod[g], 2 * i + (prod0 + 4))
                    exchange(False, K2 - 2 - i, 3 * i + n0)
                for g in range(2):
                    act.wait_ge(s_state[g], layer * (PASSES * STEPS + 1) + 1 + 2 * STEPS)
                exchange(False, 0, n0 + 3 * (K2 - 2))
                exchange(False, K2 - 1, n0 + 3 * (K2 - 1))
                n0 += 3 * K2
                prod0 += 2 * STEPS
                with act.Fori(0, K2 - 1) as i:
                    for g in range(2):
                        own_wait(act, s_prod[g], 2 * i + (prod0 + 2))
                    exchange(True, K2 - 1 - i, 3 * i + n0)
                for g in range(2):
                    act.wait_ge(s_state[g], (layer + 1) * (PASSES * STEPS + 1))
                exchange(True, 0, n0 + 3 * (K2 - 1))
            rows = flat.rearrange("b (c n) -> b c n", c=C)
            with act.Fori(0, NB // 2) as bp:
                with act.Fori(0, NBLK // PER) as q:
                    for m in range(PER):
                        act.wait_ge(s_res, bp * NBLK + PER * q + (PER + m + 1))
                        act.wait_ge(s_res_p, bp * NBLK + PER * q + (PER + m + 1))
                        for i, part in enumerate((LO, HI)):
                            dst = rows[ds(2 * bp + i, 1), :, ds(q * PER * CHUNK + m * CHUNK, CHUNK)]
                            act.dma_start(dst.rearrange("b c n -> (b c) n"), nat[m % 2][part, :]).then_inc(s_flat[m % 2], 16)
            deviation(6)

            def take_tokens(b, g):
                act.wait_ge(s_xt_p, b * GROUPS + (g + 1))
                nc.scalar.copy(x_t[0][0:96, :], bank[0][0:96, :]).then_inc(s_xt_a, 1)

            def gelu_twice(b):
                for i in range(4):
                    act.wait_ge(s_hid, b * GROUPS + 4 * (i + 1))
                    nc.scalar.activation(hid_t[:, i * 512:(i + 1) * 512], bank[2 + i][:, :], ACT.Gelu).then_inc(s_gelu, 1)
                act.wait_ge(s_gelu, b * 5 + 4)
                nc.scalar.activation(hid_t, hid_t, ACT.Gelu).then_inc(s_gelu, 1)

            def take_turned(b, first, dst):
                for i in range(2):
                    act.wait_ge(s_gt_p, b * 8 + (first + i))
                    nc.scalar.copy(dst[:, i * 512:(i + 1) * 512], bank[i][:, :]).then_inc(s_gt_a, 1)

            def mlp(b, more):
                for i in range(2):
                    act.wait_ge(s_hid_t, b * 4 + (i + 1))
                    nc.scalar.copy(*hidden_views(i)).then_inc(s_hid_a, 1)
                for g in range(0, 4 if more else 0, 2):
                    take_tokens(b + 1, g)
                act.wait_ge(s_ln, b * 2 + 1)
                nc.scalar.activation(s4, s3, ACT.Sqrt).then_inc(s_ln_a, 1)
                for g in range(4, EARLY if more else 0, 2):
                    take_tokens(b + 1, g)
                act.wait_ge(s_ln, b * 2 + 2)
                nc.scalar.copy(n_pad[:, :, 1:1 + W].rearrange("p c (q w) -> p q c w", q=NQ),
                               spm.rearrange("p (q c w) -> p q c w", q=NQ, c=G)).then_inc(s_ln_a, 1)
                take_turned(b, 1, n_t)
                for g in range(EARLY, GROUPS if more else 0, 2):
                    take_tokens(b + 1, g)
                take_turned(b, 7, g_t)
                if more:
                    gelu_twice(b + 1)

            for g in range(0, GROUPS, 2):
                take_tokens(0, g)
            act.wait_ge(s_gate_zero, 2)
            gelu_twice(0)
            with act.Fori(0, NB - 1) as b:
                mlp(b, True)
            mlp(NB - 1, False)

        @block.tensor
        def _(pe):
            mm = nc.tensor.matmul

            def group_sums(r, parts, groups, c0=0, c1=NB, which=(0, 1)):
                for i in which:
                    pe.wait_ge(s_gn_v, 3 * r + 1 + i)
                    operand = (mean_var[:, :, 0], gn_sq[:, :])[i]
                    mm(bank_gn[0:parts, i * NB + c0:i * NB + c1], groups, operand[0:parts, c0:c1],
                       start=True, stop=True).then_inc(s_gn_mm, 1)

            pe.wait_ge(s_const, 16 * N_CONST)
            group_sums(0, P, group_half[:, :], 0, 1)
            pe.wait_ge(s_wts, 1)

            def query_keys(stages, pairs, slots, gram_free, packed):
                def conv_pair(i):
                    n, sub, kp = i // 4, (i // 2) % 2, 2 * (i % 2)
                    if i % 4 == 0:
                        pe.wait_ge(s_stage, stages + (n + 1))
                        if packed is not None:
                            pe.wait_ge(s_pack, packed + (2 * n + 2))
                    pe.wait_ge(s_qk_sb, pairs + (i + 1))
                    for c in range(2):
                        dst = bank[i % 2][:, c * 2 * QK:(c + 1) * 2 * QK]
                        prods = [(buf, dy, s, dk) for buf in range(2) for dy, s, dk in conv_rows(sub)
                                 if packed is None or buf == 0 or dy == 2]
                        for t, (buf, dy, s, dk) in enumerate(prods):
                            o = s * ZSUB + (1 + 2 * (kp + c) + dk) * J2
                            last = mm(dst, (blk_z, blk_n)[buf][n % 2][:, o:o + 2 * J2],
                                      qk_w[buf][:, dy].rearrange("p a b -> p (a b)"),
                                      start=(t == 0), stop=(packed is None and t == len(prods) - 1))
                        for side in range(0 if packed is None else 2):
                            o = (kp + c) * 2 * J2
                            last = mm(dst[:, side * QK:(side + 1) * QK], blk_2[n % 2][:, side, sub, o:o + 2 * J2],
                                      qk_w2[:, side, :], start=False, stop=(side == 1))
                    last.then_inc(s_qk, 1)

                def gram_pair(i):
                    pe.wait_ge(s_qk_sb, pairs + (i + 1 + TWO))
                    if i == 0:
                        gram_free()
                    for c in range(4):
                        v = qk_sb[i % 2][:, c * QK:(c + 1) * QK]
                        last = mm(bank_gram[0:QK, 0:QK], v, v, start=(i == 0 and c == 0),
                                  stop=(i == PAIRS - 1 and c == 3))
                    last.then_inc(s_gram, 1)

                for i in range(PAIRS + 1):
                    if i < PAIRS:
                        conv_pair(i)
                    if i:
                        gram_pair(i - 1)
                    if i in slots:
                        slots[i]()

            def key_norms(b):
                own_wait(pe, s_sm_v, 5 * b + 2)
                mm(bank_small[0:C, 0:C], ones, gram_d[:, C:QK], start=True, stop=True).then_inc(s_sm_t, 1)

            def mixing(b):
                own_wait(pe, s_sm_v, 5 * b + 4)
                mm(bank_small[0:C, 64:64 + C], probs_n, proj_sb, start=True, stop=True).then_inc(s_sm_t, 1)

            def tap_weights(b):
                pe.wait_ge(s_sm_v, 5 * b + 5)
                for t in range(9):
                    last = mm(bank_wt[0:P, t * C:(t + 1) * C], v_taps[:, t, :], mix_t, start=True, stop=True)
                last.then_inc(s_sm_t, 1)

            def output_conv(b, stages, behind={}):
                pe.wait_ge(s_outw, b + 1)
                for n in range(NBLK):
                    pe.wait_ge(s_stage, stages + (n + 1))
                    for sub in range(2):
                        pe.wait_ge(s_x1, b * 2 * NBLK + (2 * n + sub + 1))
                        prods = [(buf, dy, s, dk) for buf in range(2) for dy, s, dk in conv_rows(sub)]
                        for t, (buf, dy, s, dk) in enumerate(prods):
                            o = s * ZSUB + (1 + dk) * J2
                            last = mm(bank_out[sub][0:P, :], out_w[buf][:, dy, :],
                                      (blk_z, blk_n)[buf][n % 2][:, o:o + BLK * J2],
                                      start=(t == 0), stop=(t == len(prods) - 1))
                        last.then_inc(s_conv, 1)
                        if (n, sub) in behind:
                            behind[n, sub]()

            query_keys(0, 0, {PAIRS - 2: lambda: group_sums(1, P, group_half[:, :], 1, NB)}, lambda: None, None)
            def next_query_keys(b):
                query_keys(b * 2 * NBLK + NBLK, b * PAIRS + PAIRS,
                           {SLOTS[2] - 1: lambda: key_norms(b), SLOTS[4] - 1: lambda: mixing(b),
                            SLOTS[5] - 1: lambda: tap_weights(b)},
                           lambda: pe.wait_ge(s_sm_v, 5 * b + 1),
                           b * 2 * NBLK)

            with pe.Fori(0, NB - 2) as b:
                next_query_keys(b)
                output_conv(b, b * 2 * NBLK + 2 * NBLK)
            next_query_keys(NB - 2)
            output_conv(NB - 2, (2 * NB - 2) * NBLK,
                        {(2, 0): lambda: key_norms(NB - 1), (5, 0): lambda: mixing(NB - 1),
                         (6, 0): lambda: tap_weights(NB - 1),
                         (6, 1): lambda: group_sums(2, P, group_half[:, :], 0, 2, (0,)),
                         (7, 1): lambda: group_sums(2, P, group_half[:, :], 0, 2, (1,))})
            output_conv(NB - 1, (2 * NB - 1) * NBLK)

            def step(layer, done, scan, n):
                forward, along_w, kind, _ = SCANS[scan]
                at, _ = step_at(forward, n)
                wt = scan_wt[:, 3 * layer + kind]
                for g in range(2):
                    pe.wait_ge(s_state[g], done + (layer * (PASSES * STEPS + 1) + 1))
                    src = line(g, along_w, at)
                    dst = bank[g][0:P, 0:2 * J2].rearrange("p (b j) -> p b j", b=2)
                    mm(dst, wt[:, 1], src, start=True, stop=False)
                    mm(dst[:, :, 1:J2], wt[:, 0], src[:, :, 0:J2 - 1], start=False, stop=False)
                    mm(dst[:, :, 0:J2 - 1], wt[:, 2], src[:, :, 1:J2], start=False, stop=True).then_inc(s_prod[g], 1)

            for layer in range(2):
                if layer:
                    group_sums(2 * layer + 2, P, group_half[:, :], 0, 2)
                group_sums(2 * layer + 3, P, group_half[:, :], 2, NB)
                pe.wait_ge(s_tail, layer + 1)
                if layer == 0:
                    pe.wait_ge(s_scan_c, 16 * N_SCAN_DMA)
                for scan in range(PASSES):
                    if scan == 2:
                        pe.wait_ge(s_swap, (2 * layer + 1) * 3 * K2 + 1)
                    for n in range(STEPS):
                        step(layer, scan * STEPS + n, scan, n)

            group_sums(6, 128, group_flat[:, :])
            pe.wait_ge(s_gate_const, 16 * 4)

            def tokens(b, g0, g1, after=True):
                def turn_tokens(g):
                    if g >= 2:
                        pe.wait_ge((s_xt_a, s_xt_v)[g % 2], b * (GROUPS // 2) + g // 2)
                    for t in range(4):
                        o = (4 * g + t) * 2 * TOK
                        last = nc.tensor.transpose(bank[g % 2][0:2 * TOK, t * 128:(t + 1) * 128],
                                                   xn[:, o:o + 2 * TOK], ident)
                    last.then_inc(s_xt_p, 1)

                def hidden(g):
                    pe.wait_ge((s_xt_a, s_xt_v)[g % 2], b * (GROUPS // 2) + (g // 2 + 1))
                    if after and g % 8 == 0:
                        pe.wait_ge((s_hid_a, s_hid_v)[g // 8], b * 2)
                    lanes = slice(g % 4 * 2 * HID, (g % 4 + 1) * 2 * HID)
                    last = mm(bank[2 + g // 4][lanes, :], w1_sb, x_t[g % 2][0:97, :], start=True, stop=True)
                    last.then_inc(s_hid, 1)

                turn_tokens(g0)
                for g in range(g0 + 1, g1 + 1):
                    if g < g1:
                        turn_tokens(g)
                    hidden(g - 1)

            def mlp(b, more):
                pe.wait_ge(s_gelu, b * 5 + 5)
                for i in range(4):
                    for t in range(4):
                        o = i * 512 + t * 128
                        last = nc.tensor.transpose(bank[2 + i][:, t * 128:(t + 1) * 128], hid_t[:, o:o + 128], ident)
                    last.then_inc(s_hid_t, 1)
                if more:
                    pe.wait_ge(s_xn, b + 2)
                    tokens(b + 1, 0, EARLY)
                pe.wait_ge(s_ln, b * 2 + 2)
                for q in range(NQ):
                    last = nc.tensor.transpose(bank[q // 4][:, q % 4 * 128:(q % 4 + 1) * 128],
                                               spm[:, q * 128:(q + 1) * 128], ident)
                    if q % 4 == 3:
                        last.then_inc(s_gt_p, 1)
                pe.wait_ge(s_add, b * 2 * NQ + TWO)
                pe.wait_ge(s_ln_a, b * 2 + 2)
                for c in range(G):
                    for dx in range(3):
                        last = mm(bank[6 + c // 4][:, c % 4 * 128:(c % 4 + 1) * 128], band[:, c * 3 + dx, :],
                                  n_pad[:, c, dx:dx + W], start=(dx == 0), stop=(dx == 2))
                    if c % 4 == 3:
                        last.then_inc(s_gt_p, 1)
                for q in range(NQ):
                    if q % 4 == 0:
                        pe.wait_ge(s_gt_a, b * 4 + (q // 4 + 1))
                    last = mm(bank[q // 4][:, q % 4 * 128:(q % 4 + 1) * 128], n_t[:, q * 128:(q + 1) * 128],
                              pw_k.rearrange("p a b -> p (a b)"), start=True, stop=True)
                    if q % 4 == 3:
                        last.then_inc(s_gt_p, 1)
                if more:
                    pe.wait_ge(s_pw_used, b * 2 + 2)
                    tokens(b + 1, EARLY, GROUPS)
                pe.wait_ge(s_gate, b + 1)
                for q in range(NQ):
                    last = nc.tensor.transpose(bank[q // 4][:, q % 4 * 128:(q % 4 + 1) * 128],
                                               chm[:, q * 128:(q + 1) * 128], ident)
                    if q % 4 == 3:
                        last.then_inc(s_gt_p, 1)
                for f in range(2):
                    for q in range(NQ):
                        if q % 4 == 0 and f == 0:
                            pe.wait_ge(s_gt_a, b * 4 + (q // 4 + 3))
                        pe.wait_ge(s_add, b * 2 * NQ + (f * NQ + q + 1))
                        mm(bank[6 + q % 2][:, 0:TOK // 2 * WQ], g_t[:, q * 128:(q + 1) * 128],
                           w2_k[:, f * TOK // 2:(f + 1) * TOK // 2, :].rearrange("p a b -> p (a b)"),
                           start=True, stop=True).then_inc(s_proj, 1)

            pe.wait_ge(s_xn, 1)
            tokens(0, 0, GROUPS, False)
            pe.wait_ge(s_band, N_BAND + G + 1)
            with pe.Fori(0, NB - 1) as b:
                mlp(b, True)
            mlp(NB - 1, False)

        @block.vector
        def _(dve):
            chain = Chain(dve, s_dve)
            link = chain.link
            v = nc.vector
            stat6 = stats[:, :].rearrange("p (b n) -> p b n", b=NB)

            def take_stats(parts, b, c, src):
                dst = stat6[0:parts, ds(b, 1), ds(c * 6, 6)].rearrange("p b n -> p (b n)")
                return v.bn_stats(dst, src)

            def group_norm(r, parts, n_stat, c0=0, c1=NB, which=(0, 1, 2)):
                p, c = slice(0, parts), slice(c0, c1)
                if 0 in which:
                    for b in range(c0, c1):
                        last = v.bn_aggr(mean_var[p, b, :], stat6[p, b, 0:6 * n_stat])
                    last.then_inc(s_gn_v, 1)
                if 1 in which:
                    dve.wait_ge(s_gn_mm, 2 * r + 1)
                    link(v.tensor_copy(gn_mean[p, c], bank_gn[p, c]))
                    link(v.tensor_tensor(gn_off[p, c], mean_var[p, c, 0], gn_mean[p, c], ALU.subtract))
                    link(v.tensor_tensor(gn_sq[p, c], gn_off[p, c], gn_off[p, c], ALU.mult))
                    v.tensor_tensor(gn_sq[p, c], gn_sq[p, c], mean_var[p, c, 1], ALU.add).then_inc(s_gn_v, 1)
                if 2 in which:
                    dve.wait_ge(s_gn_mm, 2 * r + 2)
                    v.tensor_scalar(gn_var[p, c], bank_gn[p, NB + c0:NB + c1], GN_EPS, None, ALU.add).then_inc(s_gn_v, 1)
                    dve.wait_ge(s_gn_std, r + 1)
                    link(v.reciprocal(gn_scale[p, c], gn_std[p, c]))
                    v.scalar_tensor_tensor(out=gn_shift[p, c], in0=gn_mean[p, c], scalar=-1.0, in1=gn_scale[p, c],
                                           op0=ALU.mult, op1=ALU.mult).then_inc(s_gn, 1)
                    dve.wait_ge(s_gn, r + 1)

            v.memset(gn_std[:, :], 1.0)
            v.memset(gn_var[:, :], 1.0).then_inc(s_stat, 1)
            dve.wait_ge(s_const, 16 * N_CONST)
            dve.wait_ge(s_zero, 1)
            for rows, pos, buf, dx in TAPS:
                for dy in range(3):
                    v.tensor_tensor(qk_w[buf][rows, dy, pos, :], qkv_sb[rows, 0:QK], dw_sb[rows, dy * 3 + dx, 0:QK],
                                    ALU.mult)
            for side, dx in ((0, 0), (1, 2)):
                for dy, rows in enumerate((LO, HI)):
                    v.tensor_tensor(qk_w2[rows, side, :], qkv_sb[rows, 0:QK], dw_sb[rows, dy * 3 + dx, 0:QK], ALU.mult)
            for t in range(9):
                for cols in (LO, HI):
                    last = v.tensor_scalar(v_taps[:, t, cols], v_sb, dwv_sb[:, t:t + 1], None, ALU.mult)
            last.then_inc(s_wts, 1)

            def x_stats(c):
                dve.wait_ge(s_split, c + 1 + TWO)
                for s in range(2):
                    at = c // LOADS * IMG + s * SUB + c % LOADS * BN
                    last = take_stats(P, c // LOADS, c % LOADS * 2 + s, image[0:P, at:at + BN])
                last.then_inc(s_stat, 1)

            for c in range(LOADS):
                x_stats(c)
            dve.wait_ge(s_stat, 1 + LOADS)
            group_norm(0, P, NSTAT, 0, 1)

            def take_pair(pairs, i):
                dve.wait_ge(s_qk, pairs + (i + 1 + 4))
                dve.wait_ge(s_gram, pairs + (i + 1))
                v.tensor_copy(qk_sb[i % 2], bank[i % 2][:, 0:4 * QK]).then_inc(s_qk_sb, 1)

            def softmax_step(b, t):
                if t == 0:
                    dve.wait_ge(s_gram, b * PAIRS + (PAIRS + TWO))
                    link(v.tensor_copy(gram, bank_gram[0:QK, 0:QK]))
                    link(v.tensor_tensor(gram_d, gram, ident[0:QK, 0:QK], ALU.mult))
                    link(v.tensor_reduce(col[:, 0:1], gram_d, AX, ALU.add))
                    v.tensor_scalar(col[:, 1:2], col[:, 0:1], NORM_FLOOR_SQ, None, ALU.max).then_inc(s_sm_v, 1)
                elif t == 1:
                    dve.wait_ge(s_sm_a, 2 * b + 1)
                    link(v.reciprocal(col[:, 3:4], col[:, 2:3]))
                    v.tensor_scalar(gram_d, ident[0:QK, 0:QK], col[:, 3:4], None, ALU.mult).then_inc(s_sm_v, 1)
                elif t == 2:
                    dve.wait_ge(s_sm_t, 3 * b + 1)
                    link(v.scalar_tensor_tensor(out=logits, in0=gram[0:C, C:QK], scalar=col[0:C, 3:4],
                                                in1=bank_small[0:C, 0:C], op0=ALU.mult, op1=ALU.mult))
                    link(v.tensor_scalar(logits, logits, temp_sb, None, ALU.mult))
                    link(v.tensor_reduce(col[0:C, 4:5], logits, AX, ALU.max))
                    v.tensor_scalar(col[0:C, 5:6], col[0:C, 4:5], -1.0, None, ALU.mult).then_inc(s_sm_v, 1)
                elif t == 3:
                    dve.wait_ge(s_sm_a, 2 * b + 2)
                    link(v.reciprocal(col[0:C, 7:8], col[0:C, 6:7]))
                    v.tensor_scalar(probs_n, probs, col[0:C, 7:8], None, ALU.mult).then_inc(s_sm_v, 1)
                elif t == 4:
                    dve.wait_ge(s_sm_t, 3 * b + 2)
                    v.tensor_copy(mix_t, bank_small[0:C, 64:64 + C]).then_inc(s_sm_v, 1)
                else:
                    dve.wait_ge(s_sm_t, 3 * b + 3)
                    taps = bank_wt[:, 0:9 * C].rearrange("p (y x c) -> p y x c", y=3, x=3)
                    for rows, pos, buf, dx in TAPS:
                        last = v.tensor_copy(out_w[buf][rows, :, (LO, HI)[pos]], taps[rows, :, dx, :])
                    last.then_inc(s_outw, 1)

            def pack(stages, n, sides=(0, 1)):
                dve.wait_ge(s_stage, stages + (n + 1))
                for side in sides:
                    src = (HI, LO)[side]
                    rows = blk_n[n % 2][src, :].rearrange("p (s n) -> p s n", s=2)
                    v.tensor_copy(blk_2[n % 2][HI, side], rows[:, :, J2:(BLK + 1) * J2])
                    v.tensor_copy(blk_2[n % 2][LO, side, 0], rows[:, 1, 0:BLK * J2])
                    last = v.tensor_copy(blk_2[n % 2][LO, side, 1], rows[:, 0, J2:(BLK + 1) * J2])
                    last.then_inc(s_pack, 1)

            def add_block(b, n, staged, between=None):
                for sub in range(2):
                    dve.wait_ge(s_conv, b * 2 * NBLK + 2 * n + (2 * NBLK + sub + 1))
                    if staged is not None:
                        dve.wait_ge(s_stage, staged)
                    dst = image5[:, ds(b, 1), sub, ds(n * BLK, BLK), :].rearrange("p b k j -> p (b k j)")
                    v.tensor_tensor(dst, dst, bank_out[sub][0:P, :], ALU.add).then_inc(s_x1, 1)
                    dve.wait_ge(s_x1, b * 2 * NBLK + 2 * n + (sub + 1 + TWO))
                    last = take_stats(P, b, 2 * n + sub, dst)
                    if between and sub == 0:
                        between()
                return last

            for i in range(PAIRS):
                take_pair(0, i)
                if 1 <= i <= (NB - 1) * LOADS:
                    x_stats(LOADS + i - 1)
                if i == PAIRS - 3:
                    dve.wait_ge(s_stat, X_STATS)
                    group_norm(1, P, NSTAT, 1, NB)
            pack(NBLK, 0)

            def take_all(b):
                for i in range(PAIRS):
                    take_pair(b * PAIRS + PAIRS, i)
                    if i % 4 in (1, 2) and i // 4 < NBLK - 1:
                        pack(b * 2 * NBLK + NBLK, i // 4 + 1, (i % 4 - 1,))
                    if i in SLOTS:
                        softmax_step(b, SLOTS.index(i))

            with dve.Fori(0, NB - 2) as b:
                chain.enter(b, ATT_LINKS)
                take_all(b)
                with dve.Fori(0, NBLK - 1) as n:
                    add_block(b, n, b * 2 * NBLK + n + (2 * NBLK + 2))
                add_block(b, NBLK - 1, None, lambda: pack(b * 2 * NBLK + 3 * NBLK, 0)).then_inc(s_stat, 1)
                chain.leave(NB - 2)
            take_all(NB - 2)
            dve.wait_ge(s_stat, X_STATS + 2)
            for n in range(NBLK):
                last = add_block(NB - 2, n, (2 * NB - 2) * NBLK + n + 2 if n < NBLK - 1 else None)
                if n == NBLK - 1:
                    last.then_inc(s_stat, 1)
                for t in {0: (0,), 1: (1,), 2: (2,), 4: (3,), 5: (4,), 7: (5,)}.get(n, ()):
                    softmax_step(NB - 1, t)
                if n >= NBLK - 3:
                    group_norm(2, P, NSTAT, 0, 2, (n - NBLK + 3,))
            for n in range(NBLK):
                last = add_block(NB - 1, n, (2 * NB - 1) * NBLK + n + 2 if n < NBLK - 1 else None)
            last.then_inc(s_stat, 1)

            def step(layer, done, scan, n):
                forward, along_w, kind, ahead = SCANS[scan]
                _, at = step_at(forward, n)
                src = (at - 1) % H if ahead else at
                for g in range(2):
                    dve.wait_ge(s_prod[g], done + (layer * PASSES * STEPS + 1))
                    prod = bank[g][0:P, 0:2 * J2].rearrange("p (b j) -> p b j", b=2)
                    v.scalar_tensor_tensor(out=line(g, along_w, at), in0=prod,
                                           scalar=scan_bias[:, 3 * layer + kind:3 * layer + kind + 1],
                                           in1=line(g, along_w, src), op0=ALU.add, op1=ALU.add).then_inc(s_state[g], 1)

            for layer in range(2):
                if layer:
                    for pair in range(2):
                        with dve.Fori(2 * pair, 2 * pair + 2) as b:
                            for m in range(VCH):
                                dve.wait_ge(s_back[m], b * 32 + 32)
                                dst = image[0:P, ds(b * IMG + m * CHUNK, CHUNK)]
                                v.tensor_tensor(dst, dst, back[m], ALU.add).then_inc(s_kept_v, 1)
                            for m in range(PER):
                                if m < VCH:
                                    dve.wait_ge(s_kept_v, VCH * b + (m + 1))
                                else:
                                    dve.wait_ge(s_kept_p, (PER - VCH) * b + (m - VCH + 1))
                                for c in range(4):
                                    last = take_stats(P, b, m * 4 + c, image[0:P, ds(b * IMG + (m * CHUNK + c * BN), BN)])
                            last.then_inc(s_stat, 1)
                        if pair == 0:
                            dve.wait_ge(s_stat, X_STATS + NB + 2)
                            group_norm(4, P, NSTAT, 0, 2)
                dve.wait_ge(s_stat, X_STATS + (1 + layer) * NB)
                group_norm(2 * layer + 3, P, NSTAT, 2, NB)
                for b in (2, 3):
                    dve.wait_ge(s_save[b], (layer + 1) * (64 if b == NB - 1 else 32))
                    cols = image[0:P, b * IMG:b * IMG + V_COLS]
                    last = v.tensor_scalar(cols, cols, gn_scale[0:P, b:b + 1], gn_shift[0:P, b:b + 1],
                                           ALU.mult, ALU.add)
                last.then_inc(s_state[1], 1)
                dve.wait_ge(s_scan_c, 16 * N_SCAN_DMA)
                for scan in range(PASSES):
                    for n in range(STEPS):
                        step(layer, scan * STEPS + n, scan, n)
                dve.wait_ge(s_swap, (layer + 1) * 6 * K2 + 1)
                for g in range(2):
                    dve.wait_ge(s_state[g], (layer + 1) * (PASSES * STEPS + 1))
            with dve.Fori(0, NB // 2) as bp:
                with dve.Fori(0, NBLK // PER) as q:
                    for m in range(PER):
                        dve.wait_ge(s_back[m], bp * (NBLK * 8) + q * 32 + (32 * NB + 32))
                        dve.wait_ge(s_flat[m % 2], bp * (NBLK * 16) + q * 64 + (m // 2 * 32 + 32))
                        for a, half in ((0, 0), (0, 1), (1, 0)):
                            last = natural(v, bp, q, m, a, half)
                        last.then_inc(s_res, 1)

            for b in range(NB):
                dve.wait_ge(s_tok[b], 16)
                for c in range(TCOLS // BN):
                    last = take_stats(128, b, c, toks[:, b, c * BN:(c + 1) * BN])
            last.then_inc(s_stat, 1)
            dve.wait_ge(s_stat, X_STATS + 2 * NB + 1)
            group_norm(6, 128, TCOLS // BN)
            per_w = [128, W, G]
            x1 = hid.rearrange("p (w f) -> p w f", f=HID)[:, :, 0:G]
            x2 = hid.rearrange("p (w f) -> p w f", f=HID)[:, :, G:HID]
            dev_v = dev.rearrange("p (w f) -> p w f", f=G)
            dev2_v = dev2.rearrange("p (w f) -> p w f", f=G)
            chm_v = chm.rearrange("p (q c w) -> p q c w", q=NQ, c=G)
            spm_v = spm.rearrange("p (q c w) -> p q c w", q=NQ, c=G)

            def affine(b):
                v.tensor_scalar(xn, toks[:, ds(b, 1), :].rearrange("p b n -> p (b n)"), gn_scale[:, ds(b, 1)],
                                gn_shift[:, ds(b, 1)], ALU.mult, ALU.add).then_inc(s_xn, 1)

            def take_tokens(b, g):
                dve.wait_ge(s_xt_p, b * GROUPS + (g + 1))
                v.tensor_copy(x_t[1][0:96, :], bank[1][0:96, :]).then_inc(s_xt_v, 1)

            def row_norm(b, i):
                if i == 0:
                    for k in range(2, 4):
                        dve.wait_ge(s_hid_t, b * 4 + (k + 1))
                        v.tensor_copy(*hidden_views(k)).then_inc(s_hid_v, 1)
                    dve.wait_ge(s_hid_a, 2 * b + 2)
                    dve.wait_ge(s_hid_v, 2 * b + 2)
                    link(v.tensor_reduce(s1, x2, AX, ALU.add))
                    link(v.scalar_tensor_tensor(out=dev_v, in0=s1.unsqueeze(2).to_broadcast(per_w), scalar=-1.0 / G,
                                                in1=x2, op0=ALU.mult, op1=ALU.add))
                elif i == 1:
                    link(v.tensor_tensor(dev2, dev, dev, ALU.mult))
                    link(v.tensor_reduce(s2, dev2_v, AX, ALU.add))
                    v.tensor_scalar(s3, s2, 1.0 / G, LN_EPS, ALU.mult, ALU.add).then_inc(s_ln, 1)
                elif i == 2:
                    dve.wait_ge(s_ln_a, 2 * b + 1)
                    link(v.reciprocal(s5, s4))
                    link(v.tensor_tensor(dev2_v, dev_v, s5.unsqueeze(2).to_broadcast(per_w), ALU.mult))
                elif i == 3:
                    link(v.tensor_tensor(dev2_v, dev2_v, gam_sb.unsqueeze(1).to_broadcast(per_w), ALU.mult))
                    v.tensor_tensor(spm_v.rearrange("p q c w -> p q w c"),
                                    dev2.rearrange("p (q w f) -> p q w f", q=NQ, f=G),
                                    bet_sb.unsqueeze(1).unsqueeze(1).to_broadcast([128, NQ, WQ, G]),
                                    ALU.add).then_inc(s_ln, 1)

            def mlp(b, more, even_more):
                for i in range(4):
                    row_norm(b, i)
                    if more:
                        take_tokens(b + 1, 2 * i + 1)
                for g in range(9, EARLY if more else 0, 2):
                    take_tokens(b + 1, g)
                dve.wait_ge(s_gt_p, 8 * b + 6)
                for i in range(2):
                    q4 = [128, 4, G, WQ]
                    v.tensor_tensor(chm_v[:, 4 * i:4 * i + 4],
                                    bank[i][:, :].rearrange("p (q c w) -> p q c w", q=4, c=G),
                                    pwb_sb.unsqueeze(1).unsqueeze(3).to_broadcast(q4), ALU.add).then_inc(s_pw_used, 1)
                for i in range(2):
                    c4 = [128, NQ, 4, WQ]
                    link(v.tensor_tensor(spm_v[:, :, 4 * i:4 * i + 4, :],
                                         bank[6 + i][:, :].rearrange("p (c q w) -> p q c w", c=4, q=NQ),
                                         dwb_sb[:, 4 * i:4 * i + 4].unsqueeze(1).unsqueeze(3).to_broadcast(c4),
                                         ALU.add))
                dve.wait_ge(s_pw_used, 2 * b + 2)
                link(v.tensor_tensor(chm, chm, spm, ALU.mult))
                if more:
                    take_tokens(b + 1, EARLY + 1)
                v.tensor_tensor(chm_v, chm_v, x1.rearrange("p (q w) c -> p q c w", q=NQ), ALU.mult)\
                    .then_inc(s_gate, 1)
                for g in range(EARLY + 3, GROUPS if more else 0, 2):
                    take_tokens(b + 1, g)
                if even_more:
                    affine(b + 2)
                dve.wait_ge(s_b2, b + 1)
                for f in range(2):
                    for q in range(NQ):
                        dve.wait_ge(s_proj, b * 2 * NQ + (f * NQ + q + 1))
                        dst = toks[:, ds(b, 1), :].rearrange("p b (c w) -> p (b c) w", c=C)
                        dst = dst[:, f * TOK // 2:(f + 1) * TOK // 2, q * WQ:(q + 1) * WQ]
                        v.tensor_tensor(dst, dst, bank[6 + q % 2][:, 0:TOK // 2 * WQ].rearrange("p (c w) -> p c w", w=WQ),
                                        ALU.add).then_inc(s_add, 1)

            affine(0)
            dve.wait_ge(s_gate_zero, 2)
            dve.wait_ge(s_gate_w, 16 * N_GATE)
            for g in range(1, GROUPS, 2):
                take_tokens(0, g)
            affine(1)
            with dve.Fori(0, NB - 2) as b:
                chain.enter(b, MLP_LINKS)
                mlp(b, True, True)
                chain.leave(NB - 2)
            mlp(NB - 2, True, False)
            mlp(NB - 1, False, False)


def kernel(**inputs):
    import numpy as np
    import concourse.bacc as bacc
    from concourse.bass_utils import run_bass_kernel_spmd as run

    nc = bacc.Bacc("TRN2", target_bir_lowering=False, num_devices=1)
    a = {k: np.asarray(t) for k, t in inputs.items()}
    half = np.concatenate([np.arange(C) // 3, np.full(HALF - C, -1), np.arange(C) // 3])
    flat_group = np.arange(128) // 8
    scans = [a[f"L{n}_conv_{d}_w"] for n in (1, 2) for d in ("down", "right", "left")]
    biases = [a[f"L{n}_conv_{d}_b"] for n in (1, 2) for d in ("down", "right", "left")]
    dw = a["L0_conv_dw_w"].reshape(3 * C, 9)
    arrays = {
        "x": a["x"],
        "qkv_t": a["L0_conv_qkv_w"].reshape(3 * C, C).T,
        "v_w": a["L0_conv_qkv_w"].reshape(3 * C, C)[2 * C:],
        "dw_t": dw.T.reshape(-1),
        "dw_v": dw[2 * C:],
        "proj_t": a["L0_conv_proj_w"].reshape(C, C).T,
        "temp": a["L0_conv_temperature"].reshape(1),
        "scan_w": np.stack([w.transpose(1, 2, 0) for w in scans]),
        "scan_b": np.stack(biases, axis=1),
        "w1": a["L3_conv_W1"], "b1": a["L3_conv_b1"].reshape(1, HID),
        "gamma": a["L3_conv_gamma"], "beta": a["L3_conv_beta"],
        "gdw": a["L3_conv_dw_w"].reshape(-1), "gdw_b": a["L3_conv_dw_b"],
        "gpw_t": a["L3_conv_pw_w"].reshape(G, G).T, "gpw_b": a["L3_conv_pw_b"],
        "w2": a["L3_conv_W2"], "b2": a["L3_conv_b2"],
        "ident_c": np.eye(128, 130, 1, dtype=np.float32),
        "group_half_c": ((half[:, None] == half[None]) & (half[:, None] >= 0)).astype(np.float32) / np.float32(6),
        "group_flat_c": (flat_group[:, None] == flat_group[None]).astype(np.float32) / np.float32(8),
    }
    arrays = {k: np.ascontiguousarray(t) for k, t in arrays.items()}
    aps = {k: nc.dram_tensor(f"in_{k}", t.shape, F32, kind="ExternalInput").ap() for k, t in arrays.items()}
    saved = [nc.dram_tensor(f"saved{i}", (2, C, COLS), F32).ap() for i in range(2)]
    flat = nc.dram_tensor("flat_rows", (NB, C * H * W), F32).ap()
    out = nc.dram_tensor("out_0", (NB, C, H, W), F32, kind="ExternalOutput").ap()
    build(nc, saved=saved, flat=flat, out=out, **aps)
    r = run(nc, [{f"in_{k}": t for k, t in arrays.items()}], core_ids=[0])
    return r.results[0]["out_0"]
```
